# Optimizing a Trainium2 kernel written in Bass

```python
import numpy as np
import jax
import jax.numpy as jnp

def _softmax(x, axis=-1):
    return jax.nn.softmax(x, axis=axis)

def _gelu(x):
    return jax.nn.gelu(x, approximate=True)

def _silu(x):
    return jax.nn.silu(x)

def _sigmoid(x):
    return jax.nn.sigmoid(x)

def _layernorm(x, axis=-1, eps=1e-05):
    m = jnp.mean(x, axis=axis, keepdims=True)
    v = jnp.var(x, axis=axis, keepdims=True)
    return (x - m) / jnp.sqrt(v + eps)

def _scatter_add(tgt, idx, src, axis=0):
    return tgt.at[idx].add(src)

def _segment_sum(src, seg, n):
    return jax.ops.segment_sum(src, seg, n)
kernel_name = 'mk_prb_d2_jaxref_r8_631ba5'

def setup_inputs(seed: int=0):
    np.random.seed(seed)
    _w = jnp.asarray

    def _L0_attn_setup():
        import jax, jax.numpy as jnp
        import numpy as np
        B, S, IN_DIM, D_MODEL, NUM_HEADS = (4, 256, 128, 128, 16)
        HEAD_DIM = D_MODEL // NUM_HEADS
        CAUSAL = True
        NEG = -9000000000000000.0

        def _xavier(key, shape):
            fan_out, fan_in = shape
            limit = (6.0 / (fan_in + fan_out)) ** 0.5
            return jax.random.uniform(key, shape, jnp.float32, -limit, limit)
        key = jax.random.key(seed)
        ks = jax.random.split(key, 5)
        x = jax.random.normal(ks[0], (B, S, IN_DIM), jnp.float32)
        Wq = _xavier(ks[1], (D_MODEL, IN_DIM))
        Wk = _xavier(ks[2], (D_MODEL, IN_DIM))
        Wv = _xavier(ks[3], (D_MODEL, IN_DIM))
        Wo = _xavier(ks[4], (D_MODEL, D_MODEL))
        bq = jnp.zeros((D_MODEL,), jnp.float32)
        bk = jnp.zeros((D_MODEL,), jnp.float32)
        bv = jnp.zeros((D_MODEL,), jnp.float32)
        bo = jnp.zeros((D_MODEL,), jnp.float32)
        return {'x': x, 'Wq': Wq, 'bq': bq, 'Wk': Wk, 'bk': bk, 'Wv': Wv, 'bv': bv, 'Wo': Wo, 'bo': bo}
    _L0_attn_in = _L0_attn_setup()

    def _L0_ffn_setup():
        import jax, jax.numpy as jnp
        import numpy as np
        E, D, MULT, K = (8, 128, 4, 2)
        B, S = (4, 256)
        H = MULT * D
        key = jax.random.key(seed)
        k0, k1, k2, k3 = jax.random.split(key, 4)
        x = jax.random.normal(k0, (B, S, D), dtype=jnp.float32)
        Wr = jax.random.normal(k1, (E, D), dtype=jnp.float32) * D ** (-0.5)
        W1 = jax.random.normal(k2, (E, D, H), dtype=jnp.float32) * D ** (-0.5)
        b1 = jnp.zeros((E, H), dtype=jnp.float32)
        W2 = jax.random.normal(k3, (E, H, D), dtype=jnp.float32) * H ** (-0.5)
        b2 = jnp.zeros((E, D), dtype=jnp.float32)
        return {'x': x, 'Wr': Wr, 'W1': W1, 'b1': b1, 'W2': W2, 'b2': b2}
    _L0_ffn_in = _L0_ffn_setup()

    def _L1_attn_setup():
        import jax, jax.numpy as jnp
        import numpy as np
        DMODEL = 128
        Q_HEADS = 16
        KV_HEADS = 4
        DHEAD = 64
        SEQ = 256
        TOP_K = 64
        ROPE_BASE = 10000.0
        NEG_INF = -1e+30

        def rope_cos_sin(seq_len, dhead, base):
            inv_freq = 1.0 / base ** (jnp.arange(0, dhead, 2, dtype=jnp.float32) / dhead)
            t = jnp.arange(seq_len, dtype=jnp.float32)
            angles = jnp.outer(t, inv_freq)
            emb = jnp.concatenate([angles, angles], axis=-1)
            return (jnp.cos(emb), jnp.sin(emb))

        def rotate_half(x):
            x1, x2 = jnp.split(x, 2, axis=-1)
            return jnp.concatenate([-x2, x1], axis=-1)

        def apply_rope(x, cos, sin):
            return x * cos[None, None] + rotate_half(x) * sin[None, None]
        key = jax.random.key(seed)
        ks = jax.random.split(key, 5)
        s = 0.02
        return {'x': jax.random.normal(ks[0], (1, SEQ, DMODEL), jnp.float32), 'Wq': jax.random.normal(ks[1], (Q_HEADS * DHEAD, DMODEL), jnp.float32) * s, 'Wk': jax.random.normal(ks[2], (KV_HEADS * DHEAD, DMODEL), jnp.float32) * s, 'Wv': jax.random.normal(ks[3], (KV_HEADS * DHEAD, DMODEL), jnp.float32) * s, 'Wo': jax.random.normal(ks[4], (DMODEL, Q_HEADS * DHEAD), jnp.float32) * s}
    _L1_attn_in = _L1_attn_setup()

    def _L1_ffn_setup():
        import jax, jax.numpy as jnp
        import numpy as np
        DIM = 128
        DEPTH = 7
        PAR = 8
        N_NODES = 2 ** (DEPTH + 1) - 1
        WIDTH = PAR * N_NODES
        key = jax.random.key(seed)
        k1, k2, k3, k4 = jax.random.split(key, 4)
        init_k = float(np.sqrt(1.0 / DIM))
        init_k2 = float(np.sqrt(1.0 / ((DEPTH + 1) * PAR)))
        oldx = jax.random.normal(k1, (4, 256, DIM), dtype=jnp.float32)
        W_in = jax.random.uniform(k2, (WIDTH, DIM), jnp.float32, -init_k, init_k)
        b_in = jax.random.uniform(k3, (WIDTH,), jnp.float32, -init_k, init_k)
        W_out = jax.random.uniform(k4, (DIM, WIDTH), jnp.float32, -init_k2, init_k2)
        return {'oldx': oldx, 'W_in': W_in, 'b_in': b_in, 'W_out': W_out}
    _L1_ffn_in = _L1_ffn_setup()
    _d = {'L0_attn_x': _L0_attn_in['x'], 'L0_attn_Wq': _L0_attn_in['Wq'], 'L0_attn_bq': _L0_attn_in['bq'], 'L0_attn_Wk': _L0_attn_in['Wk'], 'L0_attn_bk': _L0_attn_in['bk'], 'L0_attn_Wv': _L0_attn_in['Wv'], 'L0_attn_bv': _L0_attn_in['bv'], 'L0_attn_Wo': _L0_attn_in['Wo'], 'L0_attn_bo': _L0_attn_in['bo'], 'L0_ffn_Wr': _L0_ffn_in['Wr'], 'L0_ffn_W1': _L0_ffn_in['W1'], 'L0_ffn_b1': _L0_ffn_in['b1'], 'L0_ffn_W2': _L0_ffn_in['W2'], 'L0_ffn_b2': _L0_ffn_in['b2'], 'L1_attn_Wq': _L1_attn_in['Wq'], 'L1_attn_Wk': _L1_attn_in['Wk'], 'L1_attn_Wv': _L1_attn_in['Wv'], 'L1_attn_Wo': _L1_attn_in['Wo'], 'L1_ffn_W_in': _L1_ffn_in['W_in'], 'L1_ffn_b_in': _L1_ffn_in['b_in'], 'L1_ffn_W_out': _L1_ffn_in['W_out']}
    _x0 = _d['L0_attn_x']
    _d['L0_attn_x'] = jax.random.normal(jax.random.fold_in(jax.random.key(seed), 1), (2, 1024, 128), dtype=_x0.dtype)
    del _x0
    return _d

def reference(L0_attn_x, L0_attn_Wq, L0_attn_bq, L0_attn_Wk, L0_attn_bk, L0_attn_Wv, L0_attn_bv, L0_attn_Wo, L0_attn_bo, L0_ffn_Wr, L0_ffn_W1, L0_ffn_b1, L0_ffn_W2, L0_ffn_b2, L1_attn_Wq, L1_attn_Wk, L1_attn_Wv, L1_attn_Wo, L1_ffn_W_in, L1_ffn_b_in, L1_ffn_W_out):

    def _L0_attn_ref(x, Wq, bq, Wk, bk, Wv, bv, Wo, bo):
        import jax, jax.numpy as jnp
        import numpy as np
        B, S, IN_DIM, D_MODEL, NUM_HEADS = (4, 256, 128, 128, 16)
        HEAD_DIM = D_MODEL // NUM_HEADS
        CAUSAL = True
        NEG = -9000000000000000.0

        def _xavier(key, shape):
            fan_out, fan_in = shape
            limit = (6.0 / (fan_in + fan_out)) ** 0.5
            return jax.random.uniform(key, shape, jnp.float32, -limit, limit)
        batch, seq, _ = x.shape
        q = x @ Wq.T + bq
        k = x @ Wk.T + bk
        v = x @ Wv.T + bv

        def split(t):
            return t.reshape(batch, seq, NUM_HEADS, HEAD_DIM).transpose(0, 2, 1, 3)
        q, k, v = (split(q), split(k), split(v))
        scores = jnp.einsum('bhqd,bhkd->bhqk', q, k) / jnp.sqrt(jnp.float32(HEAD_DIM))
        if CAUSAL:
            mask = jnp.tril(jnp.ones((seq, seq), bool))
            scores = jnp.where(mask, scores, jnp.float32(NEG))
        attn = jax.nn.softmax(scores, axis=-1)
        out = jnp.einsum('bhqk,bhkd->bhqd', attn, v)
        out = out.transpose(0, 2, 1, 3).reshape(batch, seq, D_MODEL)
        return out @ Wo.T + bo

    def _L0_ffn_ref(x, Wr, W1, b1, W2, b2):
        import jax, jax.numpy as jnp
        import numpy as np
        E, D, MULT, K = (8, 128, 4, 2)
        B, S = (4, 256)
        H = MULT * D
        probs = jax.nn.softmax(jnp.einsum('bsd,ed->bse', x, Wr), axis=-1)
        topv, topi = jax.lax.top_k(probs, K)
        combine = jnp.sum(topv[..., None] * jax.nn.one_hot(topi, E, dtype=x.dtype), axis=2)

        def body(acc, params):
            w1, bb1, w2, bb2, ce = params
            h = jax.nn.gelu(jnp.einsum('bsd,dh->bsh', x, w1) + bb1, approximate=False)
            y = jnp.einsum('bsh,hd->bsd', h, w2) + bb2
            return (acc + ce[..., None] * y, None)
        cE = jnp.moveaxis(combine, -1, 0)
        out, _ = jax.lax.scan(body, jnp.zeros_like(x), (W1, b1, W2, b2, cE))
        return out

    def _L1_attn_ref(x, Wq, Wk, Wv, Wo):
        import jax, jax.numpy as jnp
        import numpy as np
        DMODEL = 128
        Q_HEADS = 16
        KV_HEADS = 4
        DHEAD = 64
        SEQ = 256
        TOP_K = 64
        ROPE_BASE = 10000.0
        NEG_INF = -1e+30

        def rope_cos_sin(seq_len, dhead, base):
            inv_freq = 1.0 / base ** (jnp.arange(0, dhead, 2, dtype=jnp.float32) / dhead)
            t = jnp.arange(seq_len, dtype=jnp.float32)
            angles = jnp.outer(t, inv_freq)
            emb = jnp.concatenate([angles, angles], axis=-1)
            return (jnp.cos(emb), jnp.sin(emb))

        def rotate_half(x):
            x1, x2 = jnp.split(x, 2, axis=-1)
            return jnp.concatenate([-x2, x1], axis=-1)

        def apply_rope(x, cos, sin):
            return x * cos[None, None] + rotate_half(x) * sin[None, None]
        B, S, _ = x.shape
        cos, sin = rope_cos_sin(S, DHEAD, ROPE_BASE)
        q = (x @ Wq.T).reshape(B, S, Q_HEADS, DHEAD).transpose(0, 2, 1, 3)
        k = (x @ Wk.T).reshape(B, S, KV_HEADS, DHEAD).transpose(0, 2, 1, 3)
        v = (x @ Wv.T).reshape(B, S, KV_HEADS, DHEAD).transpose(0, 2, 1, 3)
        q = apply_rope(q, cos, sin)
        k = apply_rope(k, cos, sin)
        groups = Q_HEADS // KV_HEADS
        k = jnp.repeat(k, groups, axis=1)
        v = jnp.repeat(v, groups, axis=1)
        scores = jnp.einsum('bhqd,bhkd->bhqk', q, k) / np.sqrt(DHEAD)
        causal_mask = jnp.triu(jnp.ones((S, S), bool), k=1)
        scores = jnp.where(causal_mask[None, None], NEG_INF, scores)
        topk_vals, _ = jax.lax.top_k(scores, TOP_K)
        threshold = topk_vals[..., -1:]
        scores = jnp.where(scores < threshold, NEG_INF, scores)
        weights = jax.nn.softmax(scores, axis=-1)
        out = jnp.einsum('bhqk,bhkd->bhqd', weights, v)
        out = out.transpose(0, 2, 1, 3).reshape(B, S, Q_HEADS * DHEAD)
        return out @ Wo.T

    def _L1_ffn_ref(oldx, W_in, b_in, W_out):
        import jax, jax.numpy as jnp
        import numpy as np
        DIM = 128
        DEPTH = 7
        PAR = 8
        N_NODES = 2 ** (DEPTH + 1) - 1
        WIDTH = PAR * N_NODES
        x = oldx.reshape(-1, DIM)
        B = x.shape[0]
        logits = x @ W_in.T + b_in
        decisions = (logits > 0).astype(jnp.int32).reshape(B, PAR, N_NODES)
        acts = jax.nn.silu(logits).reshape(B, PAR, N_NODES)
        current = jnp.zeros((B, PAR), dtype=jnp.int32)
        dmap = jax.nn.one_hot(current, N_NODES, dtype=acts.dtype)
        for d in range(DEPTH):
            cur_platform = 2 ** d - 1
            next_platform = 2 ** (d + 1) - 1
            moves = jnp.take_along_axis(decisions, current[..., None], axis=2)[..., 0]
            current = (current - cur_platform) * 2 + moves + next_platform
            dmap = dmap + jax.nn.one_hot(current, N_NODES, dtype=acts.dtype)
        masked = acts * jax.lax.stop_gradient(dmap)
        out = masked.reshape(B, WIDTH) @ W_out.T
        return out.reshape(oldx.shape)
    x = L0_attn_x
    xn = _layernorm(x, axis=-1)
    x = x + _L0_attn_ref(xn, L0_attn_Wq, L0_attn_bq, L0_attn_Wk, L0_attn_bk, L0_attn_Wv, L0_attn_bv, L0_attn_Wo, L0_attn_bo) + _L0_ffn_ref(xn, L0_ffn_Wr, L0_ffn_W1, L0_ffn_b1, L0_ffn_W2, L0_ffn_b2)
    xn = _layernorm(x, axis=-1)
    x = x + _L1_attn_ref(xn, L1_attn_Wq, L1_attn_Wk, L1_attn_Wv, L1_attn_Wo) + _L1_ffn_ref(xn, L1_ffn_W_in, L1_ffn_b_in, L1_ffn_W_out)
    return x

_drawn_inputs = setup_inputs


def setup_inputs(seed=0):
    import zlib

    import numpy as np

    out = dict(_drawn_inputs(seed))
    spreads = {'L0_attn_bq': (0.0, 0.1),
     'L0_attn_bk': (0.0, 2.0),
     'L0_attn_bv': (0.0, 0.1),
     'L0_attn_bo': (0.0, 0.1),
     'L0_ffn_b1': (0.0, 0.1),
     'L0_ffn_b2': (0.0, 0.1)}
    factors = {'L1_attn_Wq': 8.768, 'L1_attn_Wk': 8.784}
    for name, (base, spread) in spreads.items():
        noise = np.random.default_rng([zlib.crc32(name.encode()), seed]).standard_normal(out[name].shape)
        drawn = base * np.exp(spread * noise) if base else spread * noise
        out[name] = jnp.asarray(drawn.astype(out[name].dtype))
    for name, factor in factors.items():
        out[name] = (out[name] * factor).astype(out[name].dtype)
    return out
```

```python
from contextlib import ExitStack

import concourse.bass as bass
from concourse import mybir

ALU = mybir.AluOpType
ACT = mybir.ActivationFunctionType
AX = mybir.AxisListType
F32 = mybir.dt.float32
BF16 = mybir.dt.bfloat16

P = 128
B, S, D = 2, 1024, 128
NT = B * S // P
TB = S // P
CH = 512
NEG = -1.0e30
EPS = 1e-5

H0, DH0 = 16, 8
ROWS0 = 6 * DH0
SHIFT0 = 64
NSH = 3
VW0 = DH0 + 1

NE, HID = 8, 512
HC = HID // P

H1, KV1, DH1 = 16, 4, 64
TOPK = 64
VW1 = DH1 + 1
NPAIR = (H1 + KV1) // 2

PAR, DEPTH = 8, 7
NODES = 2 ** (DEPTH + 1) - 1
WIDTH = PAR * NODES
NCH = (WIDTH + P - 1) // P
LASTW = WIDTH - (NCH - 1) * P


class Chain:

    def __init__(self, eng, sem, start=0):
        self.eng, self.sem, self.start, self.n = eng, sem, start, 0

    def __call__(self, ins):
        ins.then_inc(self.sem, 1)
        self.n += 1
        self.eng.wait_ge(self.sem, self.start + self.n)


class Room:

    def __init__(self, nc, ctx, stage):
        self.nc, self.ctx, self.stage = nc, ctx, stage

    def sb(self, name, shape, dt=F32):
        return self.ctx.enter_context(self.nc.sbuf_tensor(f"{self.stage}_{name}", shape, dt))

    def ps(self, name, shape, dt=F32):
        return self.ctx.enter_context(self.nc.psum_tensor(f"{self.stage}_{name}", shape, dt))

    def sem(self, name):
        return self.ctx.enter_context(self.nc.semaphore(f"{self.stage}_{name}"))


def norm_rows(dve, chain, src, dst, stats, mv, rs, t1, var_ready, root_ready):
    for t in range(NT):
        last = dve.bn_stats(stats[:, t, :], src[:, t, :])
    chain(last)
    for t in range(NT):
        last = dve.bn_aggr(mv[:, t, :], stats[:, t, :])
    chain(last)
    dve.tensor_scalar(rs[:, 0, :], mv[:, :, 1], EPS, None, ALU.add).then_inc(var_ready, 1)
    dve.wait_ge(root_ready, 1)
    chain(dve.reciprocal(rs[:, 2, :], rs[:, 1, :]))
    chain(dve.tensor_tensor(t1[:, :], rs[:, 2, :], rs[:, 2, :], ALU.mult))
    chain(dve.tensor_tensor(t1[:, :], t1[:, :], rs[:, 0, :], ALU.mult))
    chain(dve.tensor_scalar(t1[:, :], t1[:, :], -0.5, 1.5, ALU.mult, ALU.add))
    chain(dve.tensor_tensor(rs[:, 3, :], rs[:, 2, :], t1[:, :], ALU.mult))
    for t in range(NT):
        dve.tensor_scalar(dst[:, t, :], src[:, t, :], mv[:, t, 0:1], rs[:, 3, t:t + 1],
                          ALU.subtract, ALU.mult).then_inc(chain.sem, 1)
        chain.n += 1


def project_layer0(nc, g):
    with ExitStack() as ctx:
        r = Room(nc, ctx, "p0")
        wq = r.sb("wq", [P, D])
        wk = r.sb("wk", [P, D])
        wv = r.sb("wv", [P, D])
        wr = r.sb("wr", [P, NE])
        bq = r.sb("bq", [P, 1])
        bk = r.sb("bk", [P, 1])
        bv = r.sb("bv", [1, D])
        xn = r.sb("xn", [P, NT, D])
        stats = r.sb("stats", [P, NT, 6])
        mv = r.sb("mv", [P, NT, 2])
        rs = r.sb("rs", [P, 4, NT])
        t1 = r.sb("t1", [P, NT])
        full = r.sb("full", [P, 2, CH])
        rest = r.sb("rest", [P, 2, CH])
        parts = r.sb("parts", [P, 2, 3, NT * P], BF16)
        ps_t = r.ps("ps_t", [P, 2, CH])
        ps_p = r.ps("ps_p", [P, 2, CH])
        ps_v = r.ps("ps_v", [P, 2, CH])
        ps_r = r.ps("ps_r", [P, CH])[:, 0:NT * NE].rearrange("p (t e) -> p t e", e=NE)

        x_in, w_in = r.sem("x_in"), r.sem("w_in")
        step = r.sem("step")
        var_ready, root_ready = r.sem("var_ready"), r.sem("root_ready")
        turned, xnT_ready = r.sem("turned"), r.sem("xnT_ready")
        prod_ready, high_ready, rest_ready = r.sem("prod_ready"), r.sem("high_ready"), r.sem("rest_ready")
        mid_ready, low_ready = r.sem("mid_ready"), r.sem("low_ready")
        v_ready, v_kept, r_ready = r.sem("v_ready"), r.sem("v_kept"), r.sem("r_ready")
        ones_ready, saved = r.sem("ones_ready"), r.sem("saved")
        NCQ = NT * P // CH
        XN0 = 2 + 5

        with nc.Block() as block:
            @block.sync
            def _(sp):
                sp.dma_start(g.x[:, :, :], g.d_x.rearrange("b (j p) d -> p (b j) d", p=P)).then_inc(x_in, 16)
                for dst, src in ((g.ident, g.d_ident), (g.identb, g.d_identb), (wq, g.d_wq0), (wk, g.d_wk0),
                                 (wv, g.d_wv0), (wr, g.d_wr), (bq, g.d_bq0), (bk, g.d_bk0), (bv, g.d_bv0),
                                 (g.maskq, g.d_maskq), (g.maskk, g.d_maskk), (g.desc, g.d_desc)):
                    sp.dma_start(dst[:, :], src).then_inc(w_in, 16)
                sp.wait_ge(low_ready, 2 * NCQ)
                sp.wait_ge(mid_ready, 2 * NCQ)
                for w, order in enumerate(((0, 1, 0, 1, 2, 0), (0, 0, 1, 1, 0, 2))):
                    for b in range(B):
                        for s, part in enumerate(order):
                            sp.dma_start(g.d_stack0[w, b, :, s * DH0:(s + 1) * DH0, :],
                                         parts[:, w, part, b * S:(b + 1) * S]).then_inc(saved, 16)
                sp.wait_ge(saved, 16 * 2 * B * 6)

            @block.vector
            def _(dve):
                dve.memset(g.ones[:, :], 1.0).then_inc(ones_ready, 1)
                dve.memset(g.onesb[:, :], 1.0).then_inc(ones_ready, 1)
                dve.memset(g.v0[:, :, :, :], 1.0).then_inc(ones_ready, 1)
                chain = Chain(dve, step)
                dve.wait_ge(x_in, 16)
                norm_rows(dve, chain, g.x, xn, stats, mv, rs, t1, var_ready, root_ready)
                dve.wait_ge(ones_ready, 3)
                for u in range(2 * NCQ):
                    w, c = u // NCQ, u % NCQ
                    cols = slice(c * CH, (c + 1) * CH)
                    dve.wait_ge(high_ready, 2 * (u + 1))
                    if u >= 2:
                        dve.wait_ge(low_ready, u - 1)
                    dve.tensor_tensor(rest[:, u % 2, :], full[:, u % 2, :], parts[:, w, 0, cols],
                                      ALU.subtract).then_inc(rest_ready, 1)
                    dve.wait_ge(mid_ready, u + 1)
                    dve.tensor_tensor(parts[:, w, 2, cols], rest[:, u % 2, :], parts[:, w, 1, cols],
                                      ALU.subtract).then_inc(low_ready, 1)
                for t in range(NT):
                    dve.wait_ge(v_ready, t + 1)
                    dst = g.v0[:, (t // TB) * H0:(t // TB + 1) * H0, t % TB, 0:DH0]
                    dve.tensor_copy(dst, ps_v[:, t % 2, 0:P].rearrange("p (h d) -> p h d", d=DH0)).then_inc(v_kept, 1)
                dve.wait_ge(r_ready, 1)
                dve.tensor_copy(g.logits[:, :, :], ps_r[:, :, :]).then_inc(v_kept, 1)

            @block.scalar
            def _(act):
                act.wait_ge(var_ready, 1)
                act.activation(rs[:, 1, :], rs[:, 0, :], ACT.Sqrt).then_inc(root_ready, 1)
                for c in range(NCQ):
                    act.wait_ge(turned, c + 1)
                    act.activation(g.xnT[:, c * CH:(c + 1) * CH], ps_t[:, c % 2, :], ACT.Copy).then_inc(xnT_ready, 1)
                act.wait_ge(w_in, 16 * 12)
                for u in range(2 * NCQ):
                    w, c = u // NCQ, u % NCQ
                    cols = slice(c * CH, (c + 1) * CH)
                    bias = (bq, bk)[w]
                    act.wait_ge(prod_ready, u + 1)
                    if u >= 2:
                        act.wait_ge(rest_ready, u - 1)
                    act.activation(full[:, u % 2, :], ps_p[:, u % 2, :], ACT.Identity,
                                   bias=bias[:, 0:1]).then_inc(high_ready, 1)
                    act.activation(parts[:, w, 0, cols], ps_p[:, u % 2, :], ACT.Identity,
                                   bias=bias[:, 0:1]).then_inc(high_ready, 1)
                    act.wait_ge(rest_ready, u + 1)
                    act.activation(parts[:, w, 1, cols], rest[:, u % 2, :], ACT.Copy).then_inc(mid_ready, 1)

            @block.tensor
            def _(pe):
                pe.wait_ge(w_in, 16 * 12)
                for t in range(NT):
                    pe.wait_ge(step, XN0 + t + 1)
                    if t % 4 == 0 and t >= 8:
                        pe.wait_ge(xnT_ready, t // 4 - 1)
                    last = pe.transpose(ps_t[:, (t // 4) % 2, (t % 4) * P:(t % 4 + 1) * P], xn[:, t, :], g.ident[:, :])
                    if t % 4 == 3:
                        last.then_inc(turned, 1)
                for u in range(2 * NCQ):
                    w, c = u // NCQ, u % NCQ
                    pe.wait_ge(xnT_ready, c + 1)
                    if u >= 2:
                        pe.wait_ge(high_ready, 2 * (u - 1))
                    pe.matmul(ps_p[:, u % 2, :], (wq, wk)[w][:, :], g.xnT[:, c * CH:(c + 1) * CH],
                              start=True, stop=True).then_inc(prod_ready, 1)
                pe.wait_ge(ones_ready, 3)
                for t in range(NT):
                    tok = g.xnT[:, t * P:(t + 1) * P]
                    if t >= 2:
                        pe.wait_ge(v_kept, t - 1)
                    pe.matmul(ps_v[:, t % 2, 0:P], tok, wv[:, :], start=True, stop=False)
                    pe.matmul(ps_v[:, t % 2, 0:P], g.ones[0:1, :], bv[0:1, :], start=False, stop=True).then_inc(v_ready, 1)
                for t in range(NT):
                    last = pe.matmul(ps_r[:, t, :], g.xnT[:, t * P:(t + 1) * P], wr[:, :], start=True, stop=True)
                last.then_inc(r_ready, 1)


def attend_layer0(nc, g):
    with ExitStack() as ctx:
        r = Room(nc, ctx, "a0")
        q = r.sb("q", [P, 2, S], BF16)
        k = r.sb("k", [P, 2, S], BF16)
        top = r.sb("top", [P, TB, 2])
        peak = r.sb("peak", [P, TB])
        left = r.sb("left", [P, TB])
        shift = r.sb("shift", [P, 2, TB, NSH], BF16)
        prob = r.sb("prob", [P, 2, S])
        rec = r.sb("rec", [P, TB])
        ps_row = r.ps("ps_row", [P, 2, CH])
        ps_col = r.ps("ps_col", [P, 2, S])
        ps_out = r.ps("ps_out", [P, 2, CH])[:, :, 0:TB * VW0].rearrange("p b (i w) -> p b i w", w=VW0)

        qk_in = [r.sem(f"qk_in{i}") for i in range(2)]
        blank = r.sem("blank")
        row_ready, row_read = r.sem("row_ready"), r.sem("row_read")
        shift_ready, step = r.sem("shift_ready"), r.sem("step")
        col_ready, col_read = r.sem("col_ready"), r.sem("col_read")
        pv_done, rec_ready, kept = r.sem("pv_done"), r.sem("rec_ready"), r.sem("kept")

        NH = B * H0
        SCALE = float(1.0 / (8.0 ** 0.5))
        UNITS = [(i, c) for i in range(TB) for c in range((i * P) // CH + 1)]
        NU = len(UNITS)
        CU = TB + 1
        STEPS = 4
        assert NU % 2 == 0 and CU % 2 == 1

        with nc.Block() as block:
            @block.sync
            def _(sp):
                def load(n, p):
                    sp.dma_start(q[0:ROWS0, p, :], g.d_stack0.rearrange("w b h r n -> w (b h) r n")[0, bass.ds(n, 1)])\
                        .then_inc(qk_in[p], 16)
                    sp.dma_start(k[0:ROWS0, p, :], g.d_stack0.rearrange("w b h r n -> w (b h) r n")[1, bass.ds(n, 1)])\
                        .then_inc(qk_in[p], 16)

                sp.wait_ge(blank, 2)
                load(0, 0)
                load(1, 1)
                with sp.Fori(0, NH // 2 - 1) as i:
                    for p in range(2):
                        sp.wait_ge(pv_done, (i * 2 + p + 1) * TB)
                        load(i * 2 + 2 + p, p)

            @block.tensor
            def _(pe):
                def row_unit(n, i2, p, u):
                    i, c = UNITS[u]
                    width = min(CH, (i + 1) * P - c * CH)
                    diag = (i + 1) * P <= (c + 1) * CH
                    if u == 0:
                        pe.wait_ge(qk_in[p], i2 * 32 + 32)
                    if not (isinstance(n, int) and n == 0 and u < 2):
                        pe.wait_ge(row_read, n * NU + (u - 1))
                    out = ps_row[:, u % 2, 0:width]
                    last = pe.matmul(out, q[0:ROWS0, p, i * P:(i + 1) * P], k[0:ROWS0, p, c * CH:c * CH + width],
                                     start=True, stop=True)
                    if diag:
                        last = pe.matmul(ps_row[:, u % 2, width - P:width], g.identb[:, :], g.maskq[:, :],
                                         start=False, stop=True, skip_group_check=True)
                    last.then_inc(row_ready, 1)

                def free_column(n, first, p, v):
                    if not (first and p == 0 and v < 2):
                        pe.wait_ge(col_read, n * CU + (v - 1))
                    return (CU * p + v) % 2

                def head(n, i2, p, first, last_head):
                    buf = free_column(n, first, p, 0)
                    pe.wait_ge(shift_ready, n + 1)
                    for i in range(TB):
                        m = pe.matmul(ps_col[0:NSH, buf, i * P:(i + 1) * P], shift[:, p, i, :], g.identb[:, :],
                                      start=True, stop=True)
                    m.then_inc(col_ready, 1)
                    nxt = iter(range(NU))

                    def rows_ahead(count):
                        if not last_head:
                            for u in [u for _, u in zip(range(count), nxt)]:
                                row_unit(n + 1, i2 + p, 1 - p, u)

                    def weigh(j):
                        pe.wait_ge(col_read, n * CU + (j + 2))
                        if j == 0 and not first:
                            pe.wait_ge(kept, n - 1)
                        for i in range(j, TB):
                            m = pe.matmul(ps_out[:, p, i, :], prob[:, j % 2, (i - j) * P:(i - j + 1) * P],
                                          g.v0.rearrange("p n j w -> p (n j w)")[
                                              :, bass.ds(n * (TB * VW0) + j * VW0, VW0)],
                                          start=(j == 0 and i == 0), stop=(j == i), skip_group_check=True)
                        m.then_inc(pv_done, 1)

                    rows_ahead(2)
                    for j in range(TB):
                        buf = free_column(n, first, p, j + 1)
                        if j == 0:
                            pe.wait_ge(col_read, n * CU + 1)
                        n_q = S - j * P
                        for c in range(0, n_q, CH):
                            w = min(CH, n_q - c)
                            m = pe.matmul(ps_col[:, buf, c:c + w], k[0:SHIFT0 + NSH, p, j * P:(j + 1) * P],
                                          q[0:SHIFT0 + NSH, p, j * P + c:j * P + c + w], start=True, stop=True)
                            if c == 0:
                                m = pe.matmul(ps_col[:, buf, 0:P], g.identb[:, :], g.maskk[:, :],
                                              start=False, stop=True, skip_group_check=True)
                        m.then_inc(col_ready, 1)
                        rows_ahead(2 if j % 2 == 0 else 1)
                        if j >= 1:
                            weigh(j - 1)
                    rows_ahead(NU)
                    weigh(TB - 1)

                for u in range(NU):
                    row_unit(0, 0, 0, u)
                head(0, 0, 0, True, False)
                head(1, 0, 1, True, False)
                with pe.Fori(1, NH // 2 - 1) as i:
                    head(i * 2, i, 0, False, False)
                    head(i * 2 + 1, i, 1, False, False)
                head(NH - 2, NH // 2 - 1, 0, False, False)
                head(NH - 1, NH // 2 - 1, 1, False, True)

            @block.scalar
            def _(act):
                def head(n, p, first):
                    act.wait_ge(col_ready, n * CU + 1)
                    act.activation(q[SHIFT0:SHIFT0 + NSH, p, :], ps_col[0:NSH, (CU * p) % 2, :],
                                   ACT.Copy).then_inc(col_read, 1)
                    for j in range(TB):
                        act.wait_ge(col_ready, n * CU + (j + 2))
                        if not (first and p == 0 and j < 2):
                            act.wait_ge(pv_done, n * TB + (j - 1))
                        act.activation(prob[:, j % 2, 0:S - j * P], ps_col[:, (CU * p + j + 1) % 2, 0:S - j * P],
                                       ACT.Exp, scale=SCALE).then_inc(col_read, 1)

                head(0, 0, True)
                head(1, 1, True)
                with act.Fori(1, NH // 2) as i:
                    head(i * 2, 0, False)
                    head(i * 2 + 1, 1, False)

            @block.vector
            def _(dve):
                def peaks(n, p, first):
                    chain = Chain(dve, step, n * STEPS)
                    for u, (i, c) in enumerate(UNITS):
                        width = min(CH, (i + 1) * P - c * CH)
                        dve.wait_ge(row_ready, n * NU + (u + 1))
                        m = dve.tensor_reduce(top[:, i, c:c + 1], ps_row[:, u % 2, 0:width], AX.X, ALU.max)
                        m.then_inc(row_read, 1)
                    dve.wait_ge(row_read, n * NU + NU)
                    chain(dve.tensor_tensor(peak[:, :], top[:, :, 0], top[:, :, 1], ALU.max))
                    if not first:
                        dve.wait_ge(col_ready, (n - 2) * CU + 1)
                    chain(dve.tensor_scalar(shift[:, p, :, 0], peak[:, :], -1.0, None, ALU.mult))
                    chain(dve.scalar_tensor_tensor(left[:, :], peak[:, :], -1.0, shift[:, p, :, 0], ALU.mult,
                                                   ALU.subtract))
                    chain(dve.tensor_copy(shift[:, p, :, 1], left[:, :]))
                    dve.tensor_tensor(shift[:, p, :, 2], left[:, :], shift[:, p, :, 1],
                                      ALU.subtract).then_inc(shift_ready, 1)

                def keep(n, p, first=False):
                    if not first:
                        dve.wait_ge(kept, n)
                    chain = Chain(dve, rec_ready, n)
                    dve.wait_ge(pv_done, n * TB + TB)
                    chain(dve.reciprocal(rec[:, :], ps_out[:, p, :, DH0]))
                    b = n // H0
                    o = g.o0[:, bass.ds(b, 1), :, bass.ds((n % H0) * DH0, DH0)]
                    ins = dve.tensor_tensor(o, ps_out[:, p, :, 0:DH0],
                                            rec[:, :].rearrange("p (i o) -> p i o", o=1).broadcast_to([P, TB, DH0]),
                                            ALU.mult)
                    ins.then_inc(kept, 1)

                set_up = Chain(dve, blank)
                dve.memset(q[:, :, :], 0.0)
                dve.memset(top[:, :, :], -3.0e38)
                set_up(dve.memset(k[:, :, :], 0.0))
                set_up(dve.memset(k[SHIFT0:SHIFT0 + NSH, :, :], 1.0))
                peaks(0, 0, True)
                peaks(1, 1, True)
                keep(0, 0, True)
                with dve.Fori(1, NH // 2) as i:
                    peaks(i * 2, 0, False)
                    keep(i * 2 - 1, 1)
                    peaks(i * 2 + 1, 1, False)
                    keep(i * 2, 0)
                keep(NH - 1, 1)


def run_experts(nc, g):
    with ExitStack() as ctx:
        r = Room(nc, ctx, "ex")
        w1 = r.sb("w1", [P, NE, HID])
        w2 = r.sb("w2", [P, NE, HC, D])
        b1 = r.sb("b1", [P, NE, HC])
        hid = r.sb("hid", [P, 2, HC, CH])
        pr = r.sb("pr", [P, NT, NE])
        ta = r.sb("ta", [P, NT, NE])
        tb = r.sb("tb", [P, NT, NE])
        pick = r.sb("pick", [P, NT, NE])
        m1 = r.sb("m1", [P, NT])
        ps_h = r.ps("ps_h", [P, 4, CH])
        ps_y = r.ps("ps_y", [P, 2, 4, P])

        w_in, step, chained = r.sem("w_in"), r.sem("step"), r.sem("chained")
        exp_in, exp_out = r.sem("exp_in"), r.sem("exp_out")
        h_ready, h_read, y_ready, y_read = r.sem("h_ready"), r.sem("h_read"), r.sem("y_ready"), r.sem("y_read")
        NCK = NT * P // CH
        TC = CH // P

        with nc.Block() as block:
            @block.sync
            def _(sp):
                sp.dma_start(w1[:, :, :], g.d_w1.rearrange("e d h -> d e h")).then_inc(w_in, 16)
                sp.dma_start(w2[:, :, :, :], g.d_w2.rearrange("e (c p) d -> p e c d", p=P)).then_inc(w_in, 16)
                sp.dma_start(b1[:, :, :], g.d_b1.rearrange("e (c p) -> p e c", p=P),
                             allow_slow_non_contiguous=True).then_inc(w_in, 16)
                sp.wait_ge(w_in, 48)

            @block.tensor
            def _(pe):
                pe.wait_ge(w_in, 48)

                def second(c, e, first):
                    s = c * NE + e
                    pe.wait_ge(h_read, s * HC + HC)
                    if not (first and e < 2):
                        pe.wait_ge(y_read, (s - 1) * TC)
                    for t in range(TC):
                        for hc in range(HC):
                            m = pe.matmul(ps_y[:, e % 2, t, :], hid[:, e % 2, hc, t * P:(t + 1) * P],
                                          w2[:, e, hc, :], start=(hc == 0), stop=(hc == HC - 1))
                    m.then_inc(y_ready, 1)

                def chunk(c, first):
                    for e in range(NE):
                        for hc in range(HC):
                            if not (first and e == 0):
                                pe.wait_ge(h_read, (c * NE + e) * HC + (hc - 3))
                            pe.matmul(ps_h[:, hc, :], w1[:, e, hc * P:(hc + 1) * P],
                                      g.xnT[:, bass.ds(c * CH, CH)], start=True, stop=True).then_inc(h_ready, 1)
                        if e >= 1:
                            second(c, e - 1, first)
                    second(c, NE - 1, first)

                chunk(0, True)
                with pe.Fori(1, NCK) as c:
                    chunk(c, False)

            @block.scalar
            def _(act):
                act.wait_ge(exp_in, 1)
                act.activation(pr[:, :, :], ta[:, :, :], ACT.Exp).then_inc(exp_out, 1)
                act.wait_ge(w_in, 48)

                def chunk(c, first):
                    for e in range(NE):
                        for hc in range(HC):
                            s = (c * NE + e) * HC + hc
                            act.wait_ge(h_ready, s + 1)
                            if hc == 0 and not (first and e < 2):
                                act.wait_ge(y_ready, c * NE + (e - 1))
                            act.activation(hid[:, e % 2, hc, :], ps_h[:, hc, :], ACT.Gelu,
                                           bias=b1[:, e, hc:hc + 1]).then_inc(h_read, 1)

                chunk(0, True)
                with act.Fori(1, NCK) as c:
                    chunk(c, False)

            @block.vector
            def _(dve):
                chain = Chain(dve, chained)

                def wide(ap):
                    return ap[:, :].rearrange("p (t o) -> p t o", o=1).broadcast_to([P, NT, NE])

                def first_of(dst, src):
                    chain(dve.tensor_reduce(m1[:, :], src[:, :, :], AX.X, ALU.max))
                    chain(dve.tensor_tensor(tb[:, :, :], src[:, :, :], wide(m1), ALU.is_ge))
                    chain(dve.tensor_tensor(tb[:, :, :], tb[:, :, :], g.desc[:, :].rearrange(
                        "p (t e) -> p t e", e=NE), ALU.mult))
                    chain(dve.tensor_reduce(m1[:, :], tb[:, :, :], AX.X, ALU.max))
                    chain(dve.tensor_tensor(dst[:, :, :], tb[:, :, :], wide(m1), ALU.is_ge))

                chain(dve.tensor_reduce(m1[:, :], g.logits[:, :, :], AX.X, ALU.max))
                dve.tensor_tensor(ta[:, :, :], g.logits[:, :, :], wide(m1), ALU.subtract).then_inc(exp_in, 1)
                dve.wait_ge(exp_out, 1)
                chain(dve.tensor_reduce(m1[:, :], pr[:, :, :], AX.X, ALU.add))
                chain(dve.reciprocal(m1[:, :], m1[:, :]))
                chain(dve.tensor_tensor(pr[:, :, :], pr[:, :, :], wide(m1), ALU.mult))
                first_of(pick, pr)
                chain(dve.scalar_tensor_tensor(ta[:, :, :], pick[:, :, :], -4.0, pr[:, :, :], ALU.mult, ALU.add))
                first_of(ta, ta)
                chain(dve.tensor_tensor(pick[:, :, :], pick[:, :, :], ta[:, :, :], ALU.add))
                chain(dve.tensor_tensor(g.comb[:, :, :], pick[:, :, :], pr[:, :, :], ALU.mult))

                comb = g.comb.rearrange("p t e -> p (t e)")
                acc = g.acc.rearrange("p t d -> p (t d)")

                def chunk(c):
                    for e in range(NE):
                        for t in range(TC):
                            dve.wait_ge(y_ready, c * NE + (e + 1))
                            if e >= 1:
                                dve.wait_ge(y_read, (c * NE + (e - 1)) * TC + (t + 1))
                            a = acc[:, bass.ds(c * CH + t * P, P)]
                            w = comb[:, bass.ds(c * (TC * NE) + (t * NE + e), 1)]
                            if e == 0:
                                m = dve.tensor_scalar(a, ps_y[:, e % 2, t, :], w, None, ALU.mult)
                            else:
                                m = dve.scalar_tensor_tensor(a, ps_y[:, e % 2, t, :], w, a, ALU.mult, ALU.add)
                            m.then_inc(y_read, 1)

                with dve.Fori(0, NCK) as c:
                    chunk(c)


def project_layer1(nc, g):
    with ExitStack() as ctx:
        r = Room(nc, ctx, "p1")
        wo = r.sb("wo", [P, D])
        bo = r.sb("bo", [1, D])
        b2 = r.sb("b2", [NE, D])
        wqk = r.sb("wqk", [P, NPAIR, P])
        wqk_rot = r.sb("wqk_rot", [P, NPAIR, P])
        wv = r.sb("wv", [P, KV1 * DH1])
        cos = r.sb("cos", [P, S])
        sin = r.sb("sin", [P, S])
        oT = r.sb("oT", [P, 2, P])
        cT = r.sb("cT", [NE, 2, P])
        xn = r.sb("xn", [P, NT, D])
        stats = r.sb("stats", [P, NT, 6])
        mv = r.sb("mv", [P, NT, 2])
        rs = r.sb("rs", [P, 4, NT])
        t1 = r.sb("t1", [P, NT])
        ra = r.sb("ra", [P, 2, CH])
        rb = r.sb("rb", [P, 2, CH])
        full = r.sb("full", [P, 2, CH])
        rest = r.sb("rest", [P, 2, CH])
        parts = r.sb("parts", [P, 2, 3, CH], BF16)
        ps_a = r.ps("ps_a", [P, 2, CH])
        ps_b = r.ps("ps_b", [P, 2, CH])
        ps_q = r.ps("ps_q", [P, 2, CH])
        ps_qr = r.ps("ps_qr", [P, 2, CH])

        w_in, step = r.sem("w_in"), r.sem("step")
        turned, oT_ready, sum_ready, sum_read = r.sem("turned"), r.sem("oT_ready"), r.sem("sum_ready"), r.sem("sum_read")
        acc_ready, x1_ready = r.sem("acc_ready"), r.sem("x1_ready")
        var_ready, root_ready = r.sem("var_ready"), r.sem("root_ready")
        xturned, xnT_ready = r.sem("xturned"), r.sem("xnT_ready")
        v_ready, v_kept = r.sem("v_ready"), r.sem("v_kept")
        q_ready, rot_a, rot_b, full_ready = r.sem("q_ready"), r.sem("rot_a"), r.sem("rot_b"), r.sem("full_ready")
        high_ready, rest_ready, mid_ready, low_ready = (r.sem("high_ready"), r.sem("rest_ready"), r.sem("mid_ready"),
                                                        r.sem("low_ready"))
        saved = [r.sem(f"saved{i}") for i in range(2)]
        NCQ = NT * P // CH
        XN0 = 2 + 5
        UB = 2 * NPAIR

        with nc.Block() as block:
            @block.sync
            def _(sp):
                for dst, src in ((wo[:, :], g.d_wo0), (bo[:, :], g.d_bo0), (b2[:, :], g.d_b2),
                                 (wv[:, :], g.d_wv1), (cos[:, :], g.d_cos), (sin[:, :], g.d_sin),
                                 (wqk[:, :, :], g.d_wqk1.rearrange("i (m o) -> i m o", o=P)),
                                 (wqk_rot[:, :, :], g.d_wqk1r.rearrange("i (m o) -> i m o", o=P))):
                    sp.dma_start(dst, src).then_inc(w_in, 16)
                sp.wait_ge(w_in, 16 * 8)
                with sp.Fori(0, B) as b:
                    for half in range(2):
                        for m in range(NPAIR):
                            u = half * NPAIR + m
                            sp.wait_ge(low_ready, b * UB + (u + 1))
                            sp.wait_ge(mid_ready, b * UB + (u + 1))
                            for part in range(3):
                                if m < H1 // 2:
                                    dst = g.d_q1[part, bass.ds(b, 1), m * P:(m + 1) * P, half * CH:(half + 1) * CH]
                                else:
                                    mk = m - H1 // 2
                                    dst = g.d_k1[part, bass.ds(b, 1), mk * P:(mk + 1) * P, half * CH:(half + 1) * CH]
                                sp.dma_start(dst, parts[:, u % 2, part, :]).then_inc(saved[u % 2], 16)
                for p in range(2):
                    sp.wait_ge(saved[p], 16 * 3 * UB * B // 2)

            @block.tensor
            def _(pe):
                pe.wait_ge(w_in, 16 * 8)
                for t in range(NT):
                    b, i = t // TB, t % TB
                    if t >= 2:
                        pe.wait_ge(oT_ready, 2 * (t - 1))
                    pe.transpose(ps_a[:, t % 2, 0:P], g.o0[:, b, i, :], g.ident[:, :])
                    pe.transpose(ps_a[0:NE, t % 2, P:2 * P], g.comb[:, t, :], g.ident[:, :]).then_inc(turned, 1)
                    pe.wait_ge(oT_ready, 2 * (t + 1))
                    if t >= 2:
                        pe.wait_ge(acc_ready, t - 1)
                    out = ps_b[:, t % 2, 0:P]
                    pe.matmul(out, oT[:, t % 2, :], wo[:, :], start=True, stop=False)
                    pe.matmul(out, g.ones[0:1, :], bo[0:1, :], start=False, stop=False)
                    pe.matmul(out, cT[:, t % 2, :], b2[:, :], start=False, stop=True).then_inc(sum_ready, 1)
                for t in range(NT):
                    pe.wait_ge(step, XN0 + t + 1)
                    if t % 4 == 0 and t >= 8:
                        pe.wait_ge(xnT_ready, t // 4 - 1)
                    m = pe.transpose(ps_a[:, (t // 4) % 2, (t % 4) * P:(t % 4 + 1) * P], xn[:, t, :], g.ident[:, :])
                    if t % 4 == 3:
                        m.then_inc(xturned, 1)
                for t in range(NT):
                    pe.wait_ge(xnT_ready, t // 4 + 1)
                    if t >= 2:
                        pe.wait_ge(v_kept, t - 1)
                    pe.matmul(ps_b[:, t % 2, 0:KV1 * DH1], g.xnT[:, t * P:(t + 1) * P], wv[:, :],
                              start=True, stop=True).then_inc(v_ready, 1)

                def batch(b, first):
                    for u in range(UB):
                        half, m = u // NPAIR, u % NPAIR
                        if not (first and u < 2):
                            pe.wait_ge(rot_a, b * UB + (u - 1))
                            pe.wait_ge(rot_b, b * UB + (u - 1))
                        xs = g.xnT[:, bass.ds(b * S + half * CH, CH)]
                        pe.matmul(ps_q[:, u % 2, :], wqk[:, m, :], xs, start=True, stop=True)
                        pe.matmul(ps_qr[:, u % 2, :], wqk_rot[:, m, :], xs, start=True, stop=True).then_inc(q_ready, 1)

                batch(0, True)
                with pe.Fori(1, B) as b:
                    batch(b, False)

            @block.vector
            def _(dve):
                dve.memset(g.v1[:, :, :, :], 1.0)
                chain = Chain(dve, step)
                for t in range(NT):
                    dve.tensor_tensor(g.x[:, t, :], g.x[:, t, :], g.acc[:, t, :], ALU.add).then_inc(x1_ready, 1)
                for t in range(NT):
                    dve.wait_ge(sum_ready, t + 1)
                    dve.wait_ge(x1_ready, t + 1)
                    dve.tensor_tensor(g.x[:, t, :], g.x[:, t, :], ps_b[:, t % 2, 0:P], ALU.add).then_inc(acc_ready, 1)
                dve.wait_ge(acc_ready, NT)
                norm_rows(dve, chain, g.x, xn, stats, mv, rs, t1, var_ready, root_ready)
                for t in range(NT):
                    b, j = t // TB, t % TB
                    dve.wait_ge(v_ready, t + 1)
                    dve.tensor_copy(g.v1[:, b * KV1:(b + 1) * KV1, j, 0:DH1],
                                    ps_b[:, t % 2, 0:KV1 * DH1].rearrange("p (h d) -> p h d", d=DH1)).then_inc(v_kept, 1)

                def batch(b, first):
                    for u in range(UB):
                        half = u // NPAIR
                        base = b * UB + u
                        dve.wait_ge(q_ready, base + 1)
                        if not (first and u < 2):
                            dve.wait_ge(full_ready, base - 1)
                        dve.tensor_tensor(ra[:, u % 2, :], ps_q[:, u % 2, :], cos[:, half * CH:(half + 1) * CH],
                                          ALU.mult).then_inc(rot_a, 1)
                        dve.tensor_tensor(rb[:, u % 2, :], ps_qr[:, u % 2, :], sin[:, half * CH:(half + 1) * CH],
                                          ALU.mult).then_inc(rot_b, 1)
                        dve.wait_ge(high_ready, base + 1)
                        if not (first and u < 2):
                            dve.wait_ge(low_ready, base - 1)
                        dve.tensor_tensor(rest[:, u % 2, :], full[:, u % 2, :], parts[:, u % 2, 0, :],
                                          ALU.subtract).then_inc(rest_ready, 1)
                        dve.wait_ge(mid_ready, base + 1)
                        dve.tensor_tensor(parts[:, u % 2, 2, :], rest[:, u % 2, :], parts[:, u % 2, 1, :],
                                          ALU.subtract).then_inc(low_ready, 1)

                batch(0, True)
                with dve.Fori(1, B) as b:
                    batch(b, False)

            @block.gpsimd
            def _(pool):
                def batch(b, first):
                    for u in range(UB):
                        base = b * UB + u
                        pool.wait_ge(rot_a, base + 1)
                        pool.wait_ge(rot_b, base + 1)
                        if not (first and u < 2):
                            pool.wait_ge(rest_ready, base - 1)
                            pool.wait_ge(high_ready, base - 1)
                        pool.tensor_tensor(full[:, u % 2, :], ra[:, u % 2, :], rb[:, u % 2, :],
                                           ALU.add).then_inc(full_ready, 1)

                batch(0, True)
                with pool.Fori(1, B) as b:
                    batch(b, False)

            @block.scalar
            def _(act):
                for t in range(NT):
                    act.wait_ge(turned, t + 1)
                    if t >= 2:
                        act.wait_ge(sum_ready, t - 1)
                    act.activation(oT[:, t % 2, :], ps_a[:, t % 2, 0:P], ACT.Copy).then_inc(oT_ready, 1)
                    act.activation(cT[:, t % 2, :], ps_a[0:NE, t % 2, P:2 * P], ACT.Copy).then_inc(oT_ready, 1)
                act.wait_ge(var_ready, 1)
                act.activation(rs[:, 1, :], rs[:, 0, :], ACT.Sqrt).then_inc(root_ready, 1)
                for c in range(NCQ):
                    act.wait_ge(xturned, c + 1)
                    act.activation(g.xnT[:, c * CH:(c + 1) * CH], ps_a[:, c % 2, :], ACT.Copy).then_inc(xnT_ready, 1)

                def batch(b, first):
                    for u in range(UB):
                        base = b * UB + u
                        act.wait_ge(full_ready, base + 1)
                        if not (first and u < 2):
                            act.wait_ge(saved[u % 2], b * (24 * UB) + 48 * (u // 2))
                        act.activation(parts[:, u % 2, 0, :], full[:, u % 2, :], ACT.Copy).then_inc(high_ready, 1)
                        act.wait_ge(rest_ready, base + 1)
                        act.activation(parts[:, u % 2, 1, :], rest[:, u % 2, :], ACT.Copy).then_inc(mid_ready, 1)

                batch(0, True)
                with act.Fori(1, B) as b:
                    batch(b, False)


def attend_layer1(nc, g):
    with ExitStack() as ctx:
        r = Room(nc, ctx, "a1")
        q = r.sb("q", [P, 2, 2, S], BF16)
        k = r.sb("k", [P, 2, 3, S], BF16)
        sc = r.sb("sc", [P, 2, S])
        work = r.sb("work", [P, S])
        best = r.sb("best", [P, 2, 8, 8])
        npeak = r.sb("npeak", [P, 2])
        prob = r.sb("prob", [P, 2, S])
        kept = r.sb("kept", [P, 2, S])
        kT = r.sb("kT", [P, 2, CH])
        rec = r.sb("rec", [P, 2])
        ps_s = r.ps("ps_s", [P, 2, S])
        ps_t = r.ps("ps_t", [P, 2, CH])
        ps_o = r.ps("ps_o", [P, 2, CH])[:, :, 0:VW1]

        qk_in = [r.sem(f"qk_in{i}") for i in range(2)]
        s_ready, s_kept, step = r.sem("s_ready"), r.sem("s_kept"), r.sem("step")
        best_ready, peak_ready, p_ready = r.sem("best_ready"), r.sem("peak_ready"), r.sem("p_ready")
        cut_ready, t_ready, t_read = r.sem("cut_ready"), r.sem("t_ready"), r.sem("t_read")
        o_ready, o_kept = r.sem("o_ready"), r.sem("o_kept")

        NH = B * H1
        GRP = H1 // KV1
        ROUNDS = TOPK // 8
        TU = sum((i * P) // CH + 1 for i in range(TB))
        STEPS = TB * (2 * ROUNDS - 1)
        SCALE = 1.0 / 8.0
        assert TU % 2 == 0
        T0 = [sum((a * P) // CH + 1 for a in range(i)) for i in range(TB)]

        with nc.Block() as block:
            @block.sync
            def _(sp):
                def load(n, p):
                    for st, (top, low) in enumerate(((0, 1), (0, 2))):
                        for half, part in enumerate((top, low)):
                            src = g.d_q1.rearrange("t b (h r) n -> t (b h) r n", r=DH1)[part, bass.ds(n, 1)]
                            sp.dma_start(q[half * DH1:(half + 1) * DH1, p, st, :], src).then_inc(qk_in[p], 16)
                    for st, (top, low) in enumerate(((0, 0), (1, 1), (2, 0))):
                        for half, part in enumerate((top, low)):
                            src = g.d_k1.rearrange("t b (h r) n -> t (b h) r n", r=DH1)[part, bass.ds(n // GRP, 1)]
                            sp.dma_start(k[half * DH1:(half + 1) * DH1, p, st, :], src).then_inc(qk_in[p], 16)

                load(0, 0)
                load(1, 1)
                with sp.Fori(0, NH // 2 - 1) as i:
                    for p in range(2):
                        sp.wait_ge(s_ready, (i * 2 + p + 1) * TB)
                        load(i * 2 + 2 + p, p)

            @block.tensor
            def _(pe):
                def scores(n, i2, p, i, first):
                    if i == 0:
                        pe.wait_ge(qk_in[p], i2 * 160 + 160)
                    if not (first and p == 0 and i < 2):
                        pe.wait_ge(s_kept, n * TB + (i - 1))
                    width = (i + 1) * P
                    qa, qc = q[:, p, 0, i * P:width], q[:, p, 1, i * P:width]
                    for c in range(0, width, CH):
                        w = min(CH, width - c)
                        diag = c + w == width
                        out = ps_s[:, i % 2, c:c + w]
                        pe.matmul(out, qa, k[:, p, 0, c:c + w], start=True, stop=False)
                        pe.matmul(out, qa, k[:, p, 1, c:c + w], start=False, stop=False)
                        m = pe.matmul(out, qc, k[:, p, 2, c:c + w], start=False, stop=True)
                        if diag:
                            m = pe.matmul(ps_s[:, i % 2, width - P:width], g.identb[:, :], g.maskq[:, :],
                                          start=False, stop=True, skip_group_check=True)
                    m.then_inc(s_ready, 1)

                def values(n, p, i, first):
                    pe.wait_ge(cut_ready, n * TB + (i + 1))
                    v = g.v1.rearrange("p n j w -> p (n j w)")
                    nj = i + 1
                    chunks = [(c, min(4, nj - c)) for c in range(0, nj, 4)]

                    def turn(x):
                        c, cnt = chunks[x]
                        tu = T0[i] + x
                        if not (first and p == 0 and tu < 2):
                            pe.wait_ge(t_read, n * TU + (tu - 1))
                        for j in range(c, c + cnt):
                            m = pe.transpose(ps_t[:, tu % 2, (j - c) * P:(j - c + 1) * P],
                                             kept[:, i % 2, j * P:(j + 1) * P], g.ident[:, :])
                        m.then_inc(t_ready, 1)

                    for x in range(len(chunks)):
                        turn(x)
                    if not (first and p == 0 and i < 2):
                        pe.wait_ge(o_kept, n * TB + (i - 1))
                    for x, (c, cnt) in enumerate(chunks):
                        tu = T0[i] + x
                        pe.wait_ge(t_read, n * TU + (tu + 1))
                        for j in range(c, c + cnt):
                            m = pe.matmul(ps_o[:, i % 2, :], kT[:, tu % 2, (j - c) * P:(j - c + 1) * P],
                                          v[:, bass.ds((n // GRP) * (TB * VW1) + j * VW1, VW1)],
                                          start=(j == 0), stop=(j == i))
                    m.then_inc(o_ready, 1)

                def head(n, i2, p, first, last_head):
                    for i in range(TB):
                        if i < TB - 2:
                            scores(n, i2, p, i + 2, first)
                        elif not last_head:
                            scores(n + 1, i2 + p, 1 - p, i + 2 - TB, False)
                        values(n, p, i, first)

                scores(0, 0, 0, 0, True)
                scores(0, 0, 0, 1, True)
                head(0, 0, 0, True, False)
                head(1, 0, 1, True, False)
                with pe.Fori(1, NH // 2 - 1) as i:
                    head(i * 2, i, 0, False, False)
                    head(i * 2 + 1, i, 1, False, False)
                head(NH - 2, NH // 2 - 1, 0, False, False)
                head(NH - 1, NH // 2 - 1, 1, False, True)

            @block.scalar
            def _(act):
                def keep_scores(n, p, i, first):
                    act.wait_ge(s_ready, n * TB + (i + 1))
                    if not (first and p == 0 and i < 2):
                        act.wait_ge(cut_ready, n * TB + (i - 1))
                    act.activation(sc[:, i % 2, 0:(i + 1) * P], ps_s[:, i % 2, 0:(i + 1) * P], ACT.Copy,
                                   scale=SCALE).then_inc(s_kept, 1)

                def weights(n, p, i, first):
                    act.wait_ge(peak_ready, n * TB + (i + 1))
                    act.activation(prob[:, i % 2, 0:(i + 1) * P], sc[:, i % 2, 0:(i + 1) * P], ACT.Exp,
                                   bias=npeak[:, i % 2:i % 2 + 1]).then_inc(p_ready, 1)

                def turned(n, p, i, first):
                    for x, c in enumerate(range(0, i + 1, 4)):
                        cnt = min(4, i + 1 - c)
                        tu = T0[i] + x
                        act.wait_ge(t_ready, n * TU + (tu + 1))
                        if x == 0 and not (first and p == 0 and i == 0):
                            act.wait_ge(o_ready, n * TB + i)
                        act.activation(kT[:, tu % 2, 0:cnt * P], ps_t[:, tu % 2, 0:cnt * P],
                                       ACT.Copy).then_inc(t_read, 1)

                def head(n, p, first, start_tile=0):
                    for i in range(TB):
                        weights(n, p, i, first)
                        if not (first and p == 0 and i == 0):
                            if i == 0:
                                turned(n - 1, 1 - p, TB - 1, first and p == 1)
                            else:
                                turned(n, p, i - 1, first)
                        if i + 1 < TB:
                            keep_scores(n, p, i + 1, first)
                        elif start_tile is not None:
                            keep_scores(n + 1, 1 - p, 0, False)

                keep_scores(0, 0, 0, True)
                head(0, 0, True)
                head(1, 1, True)
                with act.Fori(1, NH // 2 - 1) as i:
                    head(i * 2, 0, False)
                    head(i * 2 + 1, 1, False)
                head(NH - 2, 0, False)
                head(NH - 1, 1, False, None)
                turned(NH - 1, 1, TB - 1, False)

            @block.vector
            def _(dve):
                def cut(n, p, i, first):
                    dve.wait_ge(p_ready, n * TB + (i + 1))
                    if not (first and p == 0 and i < 2):
                        dve.wait_ge(o_ready, n * TB + (i - 1))
                    w = (i + 1) * P
                    dve.scalar_tensor_tensor(kept[:, i % 2, 0:w], sc[:, i % 2, 0:w], best[:, i % 2, 7, 7:8],
                                             prob[:, i % 2, 0:w], ALU.is_ge, ALU.mult).then_inc(cut_ready, 1)

                def out(n, p, i):
                    dve.wait_ge(o_ready, n * TB + (i + 1))
                    chain = Chain(dve, rec_done, n * TB + i)
                    chain(dve.reciprocal(rec[:, i % 2:i % 2 + 1], ps_o[:, i % 2, DH1:VW1]))
                    b = n // H1
                    o = g.o1[:, bass.ds(b, 1), i, bass.ds((n % H1) * DH1, DH1)]
                    dve.tensor_scalar(o, ps_o[:, i % 2, 0:DH1], rec[:, i % 2:i % 2 + 1], None,
                                      ALU.mult).then_inc(o_kept, 1)

                def head(n, p, first):
                    for i in range(TB):
                        w = (i + 1) * P
                        if not (first and p == 0 and i == 0):
                            dve.sem_clear(step)
                        bst = best[:, i % 2]
                        dve.wait_ge(s_kept, n * TB + (i + 1))
                        dve.sem_inc(step, 1)
                        chain = Chain(dve, step, 1)
                        dve.wait_ge(step, 1)
                        chain(dve.max(bst[:, 0, :], sc[:, i % 2, 0:w]))
                        if not (first and p == 0 and i < 2):
                            dve.wait_ge(p_ready, n * TB + (i - 1))
                        dve.tensor_scalar(npeak[:, i % 2:i % 2 + 1], bst[:, 0, 0:1], -1.0, None,
                                          ALU.mult).then_inc(peak_ready, 1)
                        src = sc[:, i % 2, 0:w]
                        for rd in range(1, ROUNDS):
                            chain(dve.match_replace(work[:, 0:w], bst[:, rd - 1, :], src, -3.0e38))
                            src = work[:, 0:w]
                            chain(dve.max(bst[:, rd, :], src))
                        cut(n, p, i, first)
                        if not (first and p == 0 and i == 0):
                            if i == 0:
                                out(n - 1, 1 - p, TB - 1)
                            else:
                                out(n, p, i - 1)

                rec_done = r.sem("rec_done")
                head(0, 0, True)
                head(1, 1, True)
                with dve.Fori(1, NH // 2) as i:
                    head(i * 2, 0, False)
                    head(i * 2 + 1, 1, False)
                out(NH - 1, 1, TB - 1)


def walk_trees(nc, g):
    with ExitStack() as ctx:
        r = Room(nc, ctx, "ff")
        win = r.sb("win", [P, WIDTH])
        wout = r.sb("wout", [P, NCH, D])
        bin32 = r.sb("bin32", [1, WIDTH])
        rest = r.sb("rest", [1, WIDTH])
        binp = r.sb("binp", [1, 3, WIDTH], BF16)
        xt = r.sb("xt", [P, 2, P])
        dec = r.sb("dec", [P, PAR, NODES], BF16)
        path = r.sb("path", [P, PAR, NODES], BF16)
        act_v = r.sb("act_v", [P, 2, WIDTH])
        mT = r.sb("mT", [P, 2, CH])
        ps_l = r.ps("ps_l", [P, 4 * CH])
        ps_t = r.ps("ps_t", [P, 2, CH])
        ps_f = r.ps("ps_f", [P, CH])

        w_in, bias_ready, step = r.sem("w_in"), r.sem("bias_ready"), r.sem("step")
        x_ready, l_ready, dec_ready, silu_ready = r.sem("x_ready"), r.sem("l_ready"), r.sem("dec_ready"), r.sem("silu_ready")
        masked, t_ready, t_read, f_ready, f_read = (r.sem("masked"), r.sem("t_ready"), r.sem("t_read"), r.sem("f_ready"),
                                                    r.sem("f_read"))
        NCK = (NCH + 3) // 4
        STEPS = 2 * DEPTH - 1
        HALVES = [(0, 2 * CH), (2 * CH, WIDTH)]
        BOUNDS = [(c * CH, min(CH, WIDTH - c * CH)) for c in range(4)]

        with nc.Block() as block:
            @block.sync
            def _(sp):
                sp.dma_start(win[:, :], g.d_win).then_inc(w_in, 16)
                sp.dma_start(bin32[:, :], g.d_bin).then_inc(w_in, 16)
                sp.dma_start(wout[:, 0:NCH - 1, :], g.d_wout[0:(NCH - 1) * P, :].rearrange(
                    "(c p) d -> p c d", p=P)).then_inc(w_in, 16)
                sp.dma_start(wout[0:LASTW, NCH - 1, :], g.d_wout[(NCH - 1) * P:WIDTH, :]).then_inc(w_in, 16)
                sp.wait_ge(w_in, 64)

            @block.gpsimd
            def _(pool):
                def tile(t, p, first):
                    if not first:
                        pool.wait_ge(l_ready, t - 1)
                    pool.tensor_copy(xt[:, p, :], g.xnT[:, bass.ds(t * P, P)]).then_inc(x_ready, 1)

                tile(0, 0, True)
                tile(1, 1, True)
                with pool.Fori(1, NT // 2) as i:
                    tile(i * 2, 0, False)
                    tile(i * 2 + 1, 1, False)

            @block.tensor
            def _(pe):
                pe.wait_ge(w_in, 64)
                pe.wait_ge(bias_ready, 5)

                def logits(t, p, first):
                    pe.wait_ge(x_ready, t + 1)
                    if not (first and p == 0):
                        pe.wait_ge(silu_ready, t * 2)
                    for c, w in BOUNDS:
                        for part in range(3):
                            pe.matmul(ps_l[:, c:c + w], g.onesb[0:1, :], binp[0:1, part, c:c + w],
                                      start=(part == 0), stop=False)
                        m = pe.matmul(ps_l[:, c:c + w], xt[:, p, :], win[:, c:c + w], start=False, stop=True)
                    m.then_inc(l_ready, 1)

                def outputs(t, p, first):
                    pe.wait_ge(masked, t + 1)
                    if not (first and p == 0):
                        pe.wait_ge(f_read, t)

                    def turn(x):
                        if not (first and p == 0 and x < 2):
                            pe.wait_ge(t_read, t * NCK + (x - 1))
                        for c in range(4 * x, min(4 * x + 4, NCH)):
                            w = P if c < NCH - 1 else LASTW
                            m = pe.transpose(ps_t[0:w, x % 2, (c % 4) * P:(c % 4 + 1) * P],
                                             act_v[:, p, c * P:c * P + w], g.ident[:, :])
                        m.then_inc(t_ready, 1)

                    turn(0)
                    for x in range(NCK):
                        if x + 1 < NCK:
                            turn(x + 1)
                        pe.wait_ge(t_read, t * NCK + (x + 1))
                        for c in range(4 * x, min(4 * x + 4, NCH)):
                            w = P if c < NCH - 1 else LASTW
                            m = pe.matmul(ps_f[:, 0:P], mT[0:w, x % 2, (c % 4) * P:(c % 4 + 1) * P],
                                          wout[0:w, c, :], start=(c == 0), stop=(c == NCH - 1))
                        if x == NCK - 1:
                            m.then_inc(f_ready, 1)

                logits(0, 0, True)
                logits(1, 1, True)
                outputs(0, 0, True)
                with pe.Fori(1, NT // 2) as i:
                    logits(i * 2, 0, False)
                    outputs(i * 2 - 1, 1, False)
                    logits(i * 2 + 1, 1, False)
                    outputs(i * 2, 0, False)
                outputs(NT - 1, 1, False)

            @block.scalar
            def _(act):
                def silu(t, p, first):
                    act.wait_ge(l_ready, t + 1)
                    if not first:
                        act.wait_ge(t_ready, (t - 1) * NCK)
                    for x, (lo, hi) in enumerate(HALVES):
                        act.wait_ge(dec_ready, t * 2 + (x + 1))
                        act.activation(act_v[:, p, lo:hi], ps_l[:, lo:hi], ACT.Silu).then_inc(silu_ready, 1)

                def turned(t, p, first):
                    for x in range(NCK):
                        act.wait_ge(t_ready, t * NCK + (x + 1))
                        full = 4 * P if x < NCK - 1 else (NCH - 1 - 4 * x) * P
                        if x < NCK - 1:
                            act.activation(mT[:, x % 2, 0:full], ps_t[:, x % 2, 0:full], ACT.Copy).then_inc(t_read, 1)
                        else:
                            act.activation(mT[:, x % 2, 0:full], ps_t[:, x % 2, 0:full], ACT.Copy)
                            act.activation(mT[0:LASTW, x % 2, full:full + P], ps_t[0:LASTW, x % 2, full:full + P],
                                           ACT.Copy).then_inc(t_read, 1)

                silu(0, 0, True)
                silu(1, 1, True)
                turned(0, 0, True)
                with act.Fori(1, NT // 2) as i:
                    silu(i * 2, 0, False)
                    turned(i * 2 - 1, 1, False)
                    silu(i * 2 + 1, 1, False)
                    turned(i * 2, 0, False)
                turned(NT - 1, 1, False)

            @block.vector
            def _(dve):
                dve.wait_ge(w_in, 64)
                b = Chain(dve, bias_ready)
                b(dve.tensor_copy(binp[0:1, 0, :], bin32[0:1, :]))
                b(dve.tensor_tensor(rest[0:1, :], bin32[0:1, :], binp[0:1, 0, :], ALU.subtract))
                b(dve.tensor_copy(binp[0:1, 1, :], rest[0:1, :]))
                b(dve.tensor_tensor(binp[0:1, 2, :], rest[0:1, :], binp[0:1, 1, :], ALU.subtract))
                b(dve.memset(path[:, :, 0:1], 1.0))

                def walk(t, p):
                    dve.wait_ge(l_ready, t + 1)
                    for lo, hi in HALVES:
                        dve.tensor_scalar(dec.rearrange("p a n -> p (a n)")[:, lo:hi], ps_l[:, lo:hi], 0.0, None,
                                          ALU.is_gt).then_inc(dec_ready, 1)
                    dve.wait_ge(dec_ready, t * 2 + 2)
                    chain = Chain(dve, step, t * STEPS)
                    for d in range(DEPTH):
                        lo, nx = 2 ** d - 1, 2 ** (d + 1) - 1
                        here = path[:, :, lo:lo + 2 ** d]
                        kids = path[:, :, nx:nx + 2 ** (d + 1)].rearrange("p a (n k) -> p a n k", k=2)
                        chain(dve.tensor_tensor(kids[:, :, :, 1], here, dec[:, :, lo:lo + 2 ** d], ALU.mult))
                        m = dve.tensor_tensor(kids[:, :, :, 0], here, kids[:, :, :, 1], ALU.subtract)
                        if d < DEPTH - 1:
                            chain(m)
                    m.then_inc(leaf_ready, 1)
                    dve.wait_ge(leaf_ready, t + 1)
                    dve.wait_ge(silu_ready, t * 2 + 2)
                    a = act_v[:, p, :]
                    dve.tensor_tensor(a, a, path.rearrange("p a n -> p (a n)"), ALU.mult).then_inc(masked, 1)

                def add(t):
                    dve.wait_ge(f_ready, t + 1)
                    xs = g.x.rearrange("p t d -> p (t d)")[:, bass.ds(t * P, P)]
                    dve.tensor_tensor(xs, xs, ps_f[:, 0:P], ALU.add).then_inc(f_read, 1)

                leaf_ready = r.sem("leaf_ready")
                walk(0, 0)
                walk(1, 1)
                add(0)
                with dve.Fori(1, NT // 2) as i:
                    walk(i * 2, 0)
                    add(i * 2 - 1)
                    walk(i * 2 + 1, 1)
                    add(i * 2)
                add(NT - 1)


def finish(nc, g):
    with ExitStack() as ctx:
        r = Room(nc, ctx, "fin")
        wo = r.sb("wo", [P, H1 // 2, D])
        oT = r.sb("oT", [P, 4, CH])
        ps_t = r.ps("ps_t", [P, 4, CH])
        ps_f = r.ps("ps_f", [P, 2, CH])
        w_in, turned, oT_ready = r.sem("w_in"), r.sem("turned"), r.sem("oT_ready")
        f_ready, f_read, out_done = r.sem("f_ready"), r.sem("f_read"), r.sem("out_done")

        with nc.Block() as block:
            @block.sync
            def _(sp):
                sp.dma_start(wo[:, :, :], g.d_wo1.rearrange("(c p) d -> p c d", p=P)).then_inc(w_in, 16)
                for t in range(NT):
                    sp.wait_ge(f_read, t + 1)
                    b, j = t // TB, t % TB
                    sp.dma_start(g.d_out[b, j * P:(j + 1) * P, :], g.x[:, t, :]).then_inc(out_done, 16)
                sp.wait_ge(out_done, 16 * NT)

            @block.tensor
            def _(pe):
                pe.wait_ge(w_in, 16)

                def turn(t):
                    b, i = t // TB, t % TB
                    for x in range(2):
                        u = 2 * t + x
                        if u >= 4:
                            pe.wait_ge(oT_ready, u - 3)
                        for c in range(4):
                            f = (4 * x + c) * P
                            m = pe.transpose(ps_t[:, u % 4, c * P:(c + 1) * P], g.o1[:, b, i, f:f + P], g.ident[:, :])
                        m.then_inc(turned, 1)

                turn(0)
                for t in range(NT):
                    if t + 1 < NT:
                        turn(t + 1)
                    pe.wait_ge(oT_ready, 2 * t + 2)
                    if t >= 2:
                        pe.wait_ge(f_read, t - 1)
                    for c in range(8):
                        u = 2 * t + c // 4
                        m = pe.matmul(ps_f[:, t % 2, 0:P], oT[:, u % 4, (c % 4) * P:(c % 4 + 1) * P], wo[:, c, :],
                                      start=(c == 0), stop=(c == 7))
                    m.then_inc(f_ready, 1)

            @block.scalar
            def _(act):
                for u in range(2 * NT):
                    act.wait_ge(turned, u + 1)
                    if u >= 4:
                        act.wait_ge(f_ready, (u - 4) // 2 + 1)
                    act.activation(oT[:, u % 4, :], ps_t[:, u % 4, :], ACT.Copy).then_inc(oT_ready, 1)

            @block.vector
            def _(dve):
                for t in range(NT):
                    dve.wait_ge(f_ready, t + 1)
                    dve.tensor_tensor(g.x[:, t, :], g.x[:, t, :], ps_f[:, t % 2, 0:P], ALU.add).then_inc(f_read, 1)


class Shared:
    pass


STAGES = 6


def build_program(nc, g):
    with ExitStack() as ctx:
        r = Room(nc, ctx, "g")
        g.d_stack0 = nc.dram_tensor("stack0", (2, B, H0, ROWS0, S), BF16, kind="Internal").ap()
        g.d_q1 = nc.dram_tensor("q1parts", (3, B, H1 * DH1, S), BF16, kind="Internal").ap()
        g.d_k1 = nc.dram_tensor("k1parts", (3, B, KV1 * DH1, S), BF16, kind="Internal").ap()
        g.ident = r.sb("ident", [P, P])
        g.identb = r.sb("identb", [P, P], BF16)
        g.maskq = r.sb("maskq", [P, P], BF16)
        g.maskk = r.sb("maskk", [P, P], BF16)
        g.ones = r.sb("ones", [P, P])
        g.onesb = r.sb("onesb", [P, P], BF16)
        g.x = r.sb("x", [P, NT, D])
        g.xnT = r.sb("xnT", [P, NT * P])
        with ExitStack() as layer:
            r0 = Room(nc, layer, "l0")
            g.desc = r0.sb("desc", [P, NT * NE])
            g.logits = r0.sb("logits", [P, NT, NE])
            g.comb = r0.sb("comb", [P, NT, NE])
            g.v0 = r0.sb("v0", [P, B * H0, TB, VW0])
            g.o0 = r0.sb("o0", [P, B, TB, H0 * DH0])
            g.acc = r0.sb("acc", [P, NT, D])
            g.v1 = r0.sb("v1", [P, B * KV1, TB, VW1])
            project_layer0(nc, g)
            attend_layer0(nc, g)
            run_experts(nc, g)
            project_layer1(nc, g)
            g.o1 = r0.sb("o1", [P, B, TB, H1 * DH1])
            if STAGES > 4:
                attend_layer1(nc, g)
            if STAGES > 5:
                walk_trees(nc, g)
            finish(nc, g)


_OUTS = [((B, S, D), "float32")]


def kernel(L0_attn_x, L0_attn_Wq, L0_attn_bq, L0_attn_Wk, L0_attn_bk, L0_attn_Wv, L0_attn_bv, L0_attn_Wo,
           L0_attn_bo, L0_ffn_Wr, L0_ffn_W1, L0_ffn_b1, L0_ffn_W2, L0_ffn_b2, L1_attn_Wq, L1_attn_Wk, L1_attn_Wv,
           L1_attn_Wo, L1_ffn_W_in, L1_ffn_b_in, L1_ffn_W_out):
    import ml_dtypes
    import numpy as np
    import concourse.bacc as bacc
    from concourse.bass_utils import run_bass_kernel_spmd

    def lay(a):
        return np.ascontiguousarray(a)

    future = np.triu(np.ones((P, P), bool), 1)
    maskq = np.where(future, np.float32(NEG), np.float32(0)).astype(ml_dtypes.bfloat16)
    inv_freq = (1.0 / np.float32(10000.0) ** (np.arange(0, DH1, 2, dtype=np.float32) / np.float32(DH1)))
    angles = np.outer(np.arange(S, dtype=np.float32), inv_freq.astype(np.float32))
    emb = np.concatenate([angles, angles], axis=-1)
    cos, sin = np.cos(emb).T, np.sin(emb).T
    sign = np.where(np.arange(DH1) < DH1 // 2, -1.0, 1.0).astype(np.float32)[:, None]
    desc = np.tile(np.arange(NE, 0, -1, dtype=np.float32), (P, NT))

    wqk = np.concatenate([np.asarray(L1_attn_Wq), np.asarray(L1_attn_Wk)], axis=0)
    half = DH1 // 2
    turned = wqk.reshape(H1 + KV1, 2, half, D)[:, ::-1].reshape(wqk.shape)
    feeds = {
        "d_x": lay(L0_attn_x), "d_wq0": lay(np.asarray(L0_attn_Wq).T), "d_wk0": lay(np.asarray(L0_attn_Wk).T),
        "d_wv0": lay(np.asarray(L0_attn_Wv).T), "d_wo0": lay(np.asarray(L0_attn_Wo).T),
        "d_bq0": lay(np.asarray(L0_attn_bq).reshape(P, 1)), "d_bk0": lay(np.asarray(L0_attn_bk).reshape(P, 1)),
        "d_bv0": lay(np.asarray(L0_attn_bv).reshape(1, P)), "d_bo0": lay(np.asarray(L0_attn_bo).reshape(1, P)),
        "d_wr": lay(np.asarray(L0_ffn_Wr).T), "d_w1": lay(L0_ffn_W1), "d_b1": lay(L0_ffn_b1),
        "d_w2": lay(L0_ffn_W2), "d_b2": lay(L0_ffn_b2),
        "d_wqk1": lay(wqk.T), "d_wqk1r": lay(turned.T), "d_wv1": lay(np.asarray(L1_attn_Wv).T),
        "d_wo1": lay(np.asarray(L1_attn_Wo).T), "d_win": lay(np.asarray(L1_ffn_W_in).T),
        "d_bin": lay(np.asarray(L1_ffn_b_in).reshape(1, WIDTH)), "d_wout": lay(np.asarray(L1_ffn_W_out).T),
        "d_ident": np.eye(P, dtype=np.float32), "d_identb": np.eye(P, dtype=np.float32).astype(ml_dtypes.bfloat16),
        "d_maskq": lay(maskq), "d_maskk": lay(maskq.T), "d_desc": desc,
        "d_cos": lay(np.concatenate([cos, cos]).astype(np.float32)),
        "d_sin": lay(np.concatenate([sin * sign, sin * sign]).astype(np.float32)),
    }
    nc = bacc.Bacc("TRN2", target_bir_lowering=False, num_devices=1)
    g = Shared()
    arrays = {}
    for name, a in feeds.items():
        arrays[name] = a
        g.__dict__[name] = nc.dram_tensor(name, a.shape, mybir.dt.from_np(a.dtype), kind="ExternalInput").ap()
    shape, dtype = _OUTS[0]
    g.d_out = nc.dram_tensor("out", shape, mybir.dt.from_np(np.dtype(dtype)), kind="ExternalOutput").ap()
    build_program(nc, g)
    r = run_bass_kernel_spmd(nc, [arrays], core_ids=[0])
    return r.results[0]["out"]
```

```python
from contextlib import ExitStack

import concourse.bass as bass
from concourse import mybir

ALU = mybir.AluOpType
ACT = mybir.ActivationFunctionType
AX = mybir.AxisListType
F32 = mybir.dt.float32
BF16 = mybir.dt.bfloat16

P = 128
B, S, D = 2, 1024, 128
NT = B * S // P
TB = S // P
CH = 512
NEG = -1.0e30
EPS = 1e-5

H0, DH0 = 16, 8
ROWS0 = 6 * DH0
SHIFT0 = 64
NSH = 3
VW0 = DH0 + 1

NE, HID = 8, 512
HC = HID // P

H1, KV1, DH1 = 16, 4, 64
TOPK = 64
VW1 = DH1 + 1
NPAIR = (H1 + KV1) // 2

PAR, DEPTH = 8, 7
NODES = 2 ** (DEPTH + 1) - 1
WIDTH = PAR * NODES
NCH = (WIDTH + P - 1) // P
LASTW = WIDTH - (NCH - 1) * P


class Chain:

    def __init__(self, eng, sem, start=0):
        self.eng, self.sem, self.start, self.n = eng, sem, start, 0

    def __call__(self, ins):
        ins.then_inc(self.sem, 1)
        self.n += 1
        self.eng.wait_ge(self.sem, self.start + self.n)


def is_at(n, value):
    return isinstance(n, int) and n == value


def wait(eng, sem, value):
    if not (isinstance(value, int) and value <= 0):
        eng.wait_ge(sem, value)


class Room:

    def __init__(self, nc, ctx, stage):
        self.nc, self.ctx, self.stage = nc, ctx, stage

    def sb(self, name, shape, dt=F32):
        return self.ctx.enter_context(self.nc.sbuf_tensor(f"{self.stage}_{name}", shape, dt))

    def ps(self, name, shape, dt=F32):
        return self.ctx.enter_context(self.nc.psum_tensor(f"{self.stage}_{name}", shape, dt))

    def sem(self, name):
        return self.ctx.enter_context(self.nc.semaphore(f"{self.stage}_{name}"))


def norm_rows(dve, chain, src, dst, stats, mv, rs, t1, var_ready, root_ready):
    for t in range(NT):
        last = dve.bn_stats(stats[:, t, :], src[:, t, :])
    chain(last)
    for t in range(NT):
        last = dve.bn_aggr(mv[:, t, :], stats[:, t, :])
    chain(last)
    dve.tensor_scalar(rs[:, 0, :], mv[:, :, 1], EPS, None, ALU.add).then_inc(var_ready, 1)
    dve.wait_ge(root_ready, 1)
    chain(dve.reciprocal(rs[:, 2, :], rs[:, 1, :]))
    chain(dve.tensor_tensor(t1[:, :], rs[:, 2, :], rs[:, 2, :], ALU.mult))
    chain(dve.tensor_tensor(t1[:, :], t1[:, :], rs[:, 0, :], ALU.mult))
    chain(dve.tensor_scalar(t1[:, :], t1[:, :], -0.5, 1.5, ALU.mult, ALU.add))
    chain(dve.tensor_tensor(rs[:, 3, :], rs[:, 2, :], t1[:, :], ALU.mult))
    for t in range(NT):
        dve.tensor_scalar(dst[:, t, :], src[:, t, :], mv[:, t, 0:1], rs[:, 3, t:t + 1],
                          ALU.subtract, ALU.mult).then_inc(chain.sem, 1)
        chain.n += 1


def project_layer0(nc, g):
    with ExitStack() as ctx:
        r = Room(nc, ctx, "p0")
        wq = r.sb("wq", [P, D])
        wk = r.sb("wk", [P, D])
        wv = r.sb("wv", [P, D])
        wr = r.sb("wr", [P, NE])
        bq = r.sb("bq", [P, 1])
        bk = r.sb("bk", [P, 1])
        bv = r.sb("bv", [1, D])
        xn = r.sb("xn", [P, NT, D])
        stats = r.sb("stats", [P, NT, 6])
        mv = r.sb("mv", [P, NT, 2])
        rs = r.sb("rs", [P, 4, NT])
        t1 = r.sb("t1", [P, NT])
        full = r.sb("full", [P, 2, CH])
        rest = r.sb("rest", [P, 2, CH])
        parts = r.sb("parts", [P, 2, 3, NT * P], BF16)
        ps_t = r.ps("ps_t", [P, 2, CH])
        ps_p = r.ps("ps_p", [P, 2, CH])
        ps_v = r.ps("ps_v", [P, 2, CH])
        ps_r = r.ps("ps_r", [P, CH])[:, 0:NT * NE].rearrange("p (t e) -> p t e", e=NE)

        x_in, w_in = r.sem("x_in"), r.sem("w_in")
        step = r.sem("step")
        var_ready, root_ready = r.sem("var_ready"), r.sem("root_ready")
        turned, xnT_ready = r.sem("turned"), r.sem("xnT_ready")
        prod_ready, high_ready, rest_ready = r.sem("prod_ready"), r.sem("high_ready"), r.sem("rest_ready")
        mid_ready, low_ready = r.sem("mid_ready"), r.sem("low_ready")
        v_ready, v_kept, r_ready = r.sem("v_ready"), r.sem("v_kept"), r.sem("r_ready")
        ones_ready, saved = r.sem("ones_ready"), r.sem("saved")
        NCQ = NT * P // CH
        XN0 = 2 + 5

        with nc.Block() as block:
            @block.sync
            def _(sp):
                sp.dma_start(g.x[:, :, :], g.d_x.rearrange("b (j p) d -> p (b j) d", p=P)).then_inc(x_in, 16)
                for dst, src in ((g.ident, g.d_ident), (g.identb, g.d_identb), (wq, g.d_wq0), (wk, g.d_wk0),
                                 (wv, g.d_wv0), (wr, g.d_wr), (bq, g.d_bq0), (bk, g.d_bk0), (bv, g.d_bv0),
                                 (g.maskq, g.d_maskq), (g.maskk, g.d_maskk), (g.desc, g.d_desc)):
                    sp.dma_start(dst[:, :], src).then_inc(w_in, 16)
                sp.wait_ge(low_ready, 2 * NCQ)
                sp.wait_ge(mid_ready, 2 * NCQ)
                for w, order in enumerate(((0, 1, 0, 1, 2, 0), (0, 0, 1, 1, 0, 2))):
                    for b in range(B):
                        for s, part in enumerate(order):
                            sp.dma_start(g.d_stack0[w, b, :, s * DH0:(s + 1) * DH0, :],
                                         parts[:, w, part, b * S:(b + 1) * S]).then_inc(saved, 16)
                sp.wait_ge(saved, 16 * 2 * B * 6)

            @block.vector
            def _(dve):
                dve.memset(g.ones[:, :], 1.0).then_inc(ones_ready, 1)
                dve.memset(g.onesb[:, :], 1.0).then_inc(ones_ready, 1)
                dve.memset(g.v0[:, :, :, :], 1.0).then_inc(ones_ready, 1)
                chain = Chain(dve, step)
                dve.wait_ge(x_in, 16)
                norm_rows(dve, chain, g.x, xn, stats, mv, rs, t1, var_ready, root_ready)
                dve.wait_ge(ones_ready, 3)
                for u in range(2 * NCQ):
                    w, c = u // NCQ, u % NCQ
                    cols = slice(c * CH, (c + 1) * CH)
                    dve.wait_ge(high_ready, 2 * (u + 1))
                    if u >= 2:
                        dve.wait_ge(low_ready, u - 1)
                    dve.tensor_tensor(rest[:, u % 2, :], full[:, u % 2, :], parts[:, w, 0, cols],
                                      ALU.subtract).then_inc(rest_ready, 1)
                    dve.wait_ge(mid_ready, u + 1)
                    dve.tensor_tensor(parts[:, w, 2, cols], rest[:, u % 2, :], parts[:, w, 1, cols],
                                      ALU.subtract).then_inc(low_ready, 1)
                for t in range(NT):
                    dve.wait_ge(v_ready, t + 1)
                    dst = g.v0[:, (t // TB) * H0:(t // TB + 1) * H0, t % TB, 0:DH0]
                    dve.tensor_copy(dst, ps_v[:, t % 2, 0:P].rearrange("p (h d) -> p h d", d=DH0)).then_inc(v_kept, 1)
                dve.wait_ge(r_ready, 1)
                dve.tensor_copy(g.logits[:, :, :], ps_r[:, :, :]).then_inc(v_kept, 1)

            @block.scalar
            def _(act):
                act.wait_ge(var_ready, 1)
                act.activation(rs[:, 1, :], rs[:, 0, :], ACT.Sqrt).then_inc(root_ready, 1)
                for c in range(NCQ):
                    act.wait_ge(turned, c + 1)
                    act.activation(g.xnT[:, c * CH:(c + 1) * CH], ps_t[:, c % 2, :], ACT.Copy).then_inc(xnT_ready, 1)
                act.wait_ge(w_in, 16 * 12)
                for u in range(2 * NCQ):
                    w, c = u // NCQ, u % NCQ
                    cols = slice(c * CH, (c + 1) * CH)
                    bias = (bq, bk)[w]
                    act.wait_ge(prod_ready, u + 1)
                    if u >= 2:
                        act.wait_ge(rest_ready, u - 1)
                    act.activation(full[:, u % 2, :], ps_p[:, u % 2, :], ACT.Identity,
                                   bias=bias[:, 0:1]).then_inc(high_ready, 1)
                    act.activation(parts[:, w, 0, cols], ps_p[:, u % 2, :], ACT.Identity,
                                   bias=bias[:, 0:1]).then_inc(high_ready, 1)
                    act.wait_ge(rest_ready, u + 1)
                    act.activation(parts[:, w, 1, cols], rest[:, u % 2, :], ACT.Copy).then_inc(mid_ready, 1)

            @block.tensor
            def _(pe):
                pe.wait_ge(w_in, 16 * 12)
                for t in range(NT):
                    pe.wait_ge(step, XN0 + t + 1)
                    if t % 4 == 0 and t >= 8:
                        pe.wait_ge(xnT_ready, t // 4 - 1)
                    last = pe.transpose(ps_t[:, (t // 4) % 2, (t % 4) * P:(t % 4 + 1) * P], xn[:, t, :], g.ident[:, :])
                    if t % 4 == 3:
                        last.then_inc(turned, 1)
                for u in range(2 * NCQ):
                    w, c = u // NCQ, u % NCQ
                    pe.wait_ge(xnT_ready, c + 1)
                    if u >= 2:
                        pe.wait_ge(high_ready, 2 * (u - 1))
                    pe.matmul(ps_p[:, u % 2, :], (wq, wk)[w][:, :], g.xnT[:, c * CH:(c + 1) * CH],
                              start=True, stop=True).then_inc(prod_ready, 1)
                pe.wait_ge(ones_ready, 3)
                for t in range(NT):
                    tok = g.xnT[:, t * P:(t + 1) * P]
                    if t >= 2:
                        pe.wait_ge(v_kept, t - 1)
                    pe.matmul(ps_v[:, t % 2, 0:P], tok, wv[:, :], start=True, stop=False)
                    pe.matmul(ps_v[:, t % 2, 0:P], g.ones[0:1, :], bv[0:1, :], start=False, stop=True).then_inc(v_ready, 1)
                for t in range(NT):
                    last = pe.matmul(ps_r[:, t, :], g.xnT[:, t * P:(t + 1) * P], wr[:, :], start=True, stop=True)
                last.then_inc(r_ready, 1)


def attend_layer0(nc, g):
    with ExitStack() as ctx:
        r = Room(nc, ctx, "a0")
        NQ = 4
        GR = 4
        GW = P // GR
        q = r.sb("q", [P, NQ, S], BF16)
        k = r.sb("k", [P, NQ, S], BF16)
        v = r.sb("v", [P, 2, TB, GW])
        nil = r.sb("nil", [P, CH], BF16)
        top = r.sb("top", [P, TB, 2])
        peak = r.sb("peak", [P, TB])
        left = r.sb("left", [P, TB])
        shift = r.sb("shift", [P, 2, TB, NSH], BF16)
        PW = sum(S - j * P for j in range(TB))
        PO = [sum(S - a * P for a in range(j)) for j in range(TB)]
        prob = r.sb("prob", [P, 2, PW])
        oT = r.sb("oT", [P, S])
        osum = r.sb("osum", [P, TB, VW0])
        rec = r.sb("rec", [P, TB])
        ps_row = r.ps("ps_row", [P, 2, CH])
        ps_col = r.ps("ps_col", [P, 2, S])
        ps_out = r.ps("ps_out", [P, S])

        qk_in = [r.sem(f"qk_in{i}") for i in range(NQ)]
        blank, v_ready = r.sem("blank"), r.sem("v_ready")
        row_ready, row_read = r.sem("row_ready"), r.sem("row_read")
        shift_ready, step = r.sem("shift_ready"), r.sem("step")
        col_ready, col_read = r.sem("col_ready"), r.sem("col_read")
        pv_done, out_read = r.sem("pv_done"), r.sem("out_read")
        rec_ready, kept = r.sem("rec_ready"), r.sem("kept")

        NH = B * H0
        SCALE = float(1.0 / (8.0 ** 0.5))
        UNITS = [(i, c) for i in range(TB) for c in range((i * P) // CH + 1)]
        NU = len(UNITS)
        CU = TB + 1
        STEPS = 4
        assert NU % 2 == 0 and CU % 2 == 1 and NH % NQ == 0

        def row_base(n):
            if is_at(n, 0):
                return NU
            if is_at(n, NH):
                return row_base(NH - 1) + 2
            return n * (NU + 2) + (NU - 2)

        def heads(eng, section):
            for n in range(NQ):
                section(n, 0, n)
            with eng.Fori(1, NH // NQ - 1) as i:
                for h in range(NQ):
                    section(i * NQ + h, i, h)
            for n in range(NH - NQ, NH + 1):
                section(n, n // NQ, n % NQ)

        with nc.Block() as block:
            @block.sync
            def _(sp):
                def load(n, h):
                    stacks = g.d_stack0.rearrange("w b h r n -> w (b h) r n")
                    sp.dma_start(q[0:ROWS0, h, :], stacks[0, bass.ds(n, 1)]).then_inc(qk_in[h], 16)
                    sp.dma_start(k[0:ROWS0, h, :], stacks[1, bass.ds(n, 1)]).then_inc(qk_in[h], 16)

                sp.wait_ge(blank, 2)
                for h in range(NQ):
                    load(h, h)
                with sp.Fori(1, NH // NQ) as i:
                    for h in range(NQ):
                        sp.wait_ge(col_ready, i * (NQ * CU) + (h - NQ + 1) * CU)
                        load(i * NQ + h, h)

            @block.gpsimd
            def _(pool):
                def values(n, p, first=False):
                    if not first:
                        pool.wait_ge(pv_done, n - 1)
                    src = g.v0.rearrange("p n j w -> p n (j w)")[:, bass.ds(n, 1), :]
                    pool.tensor_copy(v[:, p, :, 0:VW0], src.rearrange("p o (j w) -> p (o j) w", w=VW0)).then_inc(v_ready, 1)

                pool.wait_ge(blank, 3)
                values(0, 0, True)
                values(1, 1, True)
                with pool.Fori(1, NH // 2) as i:
                    values(i * 2, 0)
                    values(i * 2 + 1, 1)

            @block.tensor
            def _(pe):
                def row_unit(n, i4, h, unit, u):
                    i, c = UNITS[u]
                    width = min(CH, (i + 1) * P - c * CH)
                    diag = (i + 1) * P <= (c + 1) * CH
                    if u == 0:
                        pe.wait_ge(qk_in[h], i4 * 32 + 32)
                    wait(pe, row_read, unit - 1)
                    last = pe.matmul(ps_row[:, u % 2, 0:width], q[0:SHIFT0, h, i * P:(i + 1) * P],
                                     k[0:SHIFT0, h, c * CH:c * CH + width], start=True, stop=True)
                    if diag:
                        last = pe.matmul(ps_row[:, u % 2, width - P:width], g.identb[:, :], g.maskq[:, :],
                                         start=False, stop=True, skip_group_check=True)
                    last.then_inc(row_ready, 1)

                def pv(n, p, x):
                    bank = 0 if x == 1 else 1
                    if x == 0:
                        pe.wait_ge(v_ready, n + 1)
                        wait(pe, out_read, n)
                        pe.wait_ge(col_read, n * CU + (GR + 1))
                    if x == 2:
                        pe.wait_ge(col_read, n * CU + CU)
                    if x == 1:
                        for a in range(1, GR):
                            pe.matmul(ps_out[a * GW:(a + 1) * GW, 0:CH], nil[:, 0:GW], nil[:, :],
                                      start=True, stop=True)
                    for a in range(GR):
                        j = a if x < 2 else a + GR
                        lo, hi = max(j * P, bank * CH), (bank + 1) * CH
                        m = pe.matmul(ps_out[a * GW:(a + 1) * GW, lo:hi], v[:, p, j, :],
                                      prob[:, p, PO[j] + lo - j * P:PO[j] + hi - j * P],
                                      start=(x == 0 or (x == 1 and a == 0)), stop=True, skip_group_check=True)
                    if x == 2:
                        m.then_inc(pv_done, 1)

                def section(n, i4, h):
                    p = h % 2
                    rows = not (is_at(n, NH - 1) or is_at(n, NH))
                    ahead = iter(range(NU if rows else 0))

                    def rows_ahead(count):
                        for u in [u for _, u in zip(range(count), ahead)]:
                            nh = (h + 1) % NQ
                            row_unit(n + 1, i4 + (h + 1) // NQ, nh, row_base(n) + u, u)

                    if not is_at(n, NH):
                        wait(pe, col_read, n * CU - 1)
                        pe.wait_ge(shift_ready, n + 1)
                        for i in range(TB):
                            m = pe.matmul(ps_col[0:NSH, p % 2, i * P:(i + 1) * P], shift[:, p, i, :], g.identb[:, :],
                                          start=True, stop=True)
                        m.then_inc(col_ready, 1)
                    rows_ahead(2)
                    for j in range(TB):
                        if not is_at(n, NH):
                            wait(pe, col_read, n * CU + j)
                            if j == 0:
                                pe.wait_ge(col_read, n * CU + 1)
                            buf = (p + j + 1) % 2
                            n_q = S - j * P
                            for c in range(0, n_q, CH):
                                w = min(CH, n_q - c)
                                m = pe.matmul(ps_col[:, buf, c:c + w], k[:, h, j * P:(j + 1) * P],
                                              q[:, h, j * P + c:j * P + c + w], start=True, stop=True)
                                if c == 0:
                                    m = pe.matmul(ps_col[:, buf, 0:P], g.identb[:, :], g.maskk[:, :],
                                                  start=False, stop=True, skip_group_check=True)
                            m.then_inc(col_ready, 1)
                        rows_ahead(2 if j in (0, 2) else 1)
                        if j in (0, 2, 4) and not is_at(n, 0):
                            pv(n - 1, 1 - p, j // 2)
                    rows_ahead(NU)
                    if not is_at(n, 0):
                        pe.wait_ge(out_read, n)
                        base = row_base(n) + (NU if rows else 0)
                        for x in range(2):
                            pe.wait_ge(row_read, base + (x - 1))
                            for i in range(4):
                                m = pe.transpose(ps_row[:, x, i * P:(i + 1) * P],
                                                 oT[:, (4 * x + i) * P:(4 * x + i + 1) * P], g.ident[:, :])
                            m.then_inc(row_ready, 1)

                pe.wait_ge(blank, 4)
                for u in range(NU):
                    row_unit(0, 0, 0, u, u)
                heads(pe, section)

            @block.scalar
            def _(act):
                def section(n, i4, h):
                    p = h % 2
                    if not is_at(n, NH):
                        act.wait_ge(col_ready, n * CU + 1)
                        act.activation(q[SHIFT0:SHIFT0 + NSH, h, :], ps_col[0:NSH, p, :], ACT.Copy).then_inc(col_read, 1)
                    for j in range(TB):
                        if not is_at(n, NH):
                            act.wait_ge(col_ready, n * CU + (j + 2))
                            if j == 0:
                                wait(act, pv_done, n - 1)
                            act.activation(prob[:, p, PO[j]:PO[j] + S - j * P], ps_col[:, (p + j + 1) % 2, 0:S - j * P],
                                           ACT.Exp, scale=SCALE).then_inc(col_read, 1)
                        if j == 5 and not is_at(n, 0):
                            act.wait_ge(pv_done, n)
                            if not is_at(n, 1):
                                act.wait_ge(row_ready, row_base(n - 1) + (2 if is_at(n, NH) else NU + 2))
                            act.activation(oT[:, :], ps_out[:, :], ACT.Copy).then_inc(out_read, 1)

                heads(act, section)

            @block.vector
            def _(dve):
                def peaks(n, p, base):
                    chain = Chain(dve, step, n * STEPS)
                    for u, (i, c) in enumerate(UNITS):
                        width = min(CH, (i + 1) * P - c * CH)
                        dve.wait_ge(row_ready, base + (u + 1))
                        m = dve.tensor_reduce(top[:, i, c:c + 1], ps_row[:, u % 2, 0:width], AX.X, ALU.max)
                        m.then_inc(row_read, 1)
                    dve.wait_ge(row_read, base + NU)
                    chain(dve.tensor_tensor(peak[:, :], top[:, :, 0], top[:, :, 1], ALU.max))
                    wait(dve, col_ready, n * CU - (2 * CU - 1))
                    chain(dve.tensor_scalar(shift[:, p, :, 0], peak[:, :], -1.0, None, ALU.mult))
                    chain(dve.scalar_tensor_tensor(left[:, :], peak[:, :], -1.0, shift[:, p, :, 0], ALU.mult,
                                                   ALU.subtract))
                    chain(dve.tensor_copy(shift[:, p, :, 1], left[:, :]))
                    dve.tensor_tensor(shift[:, p, :, 2], left[:, :], shift[:, p, :, 1],
                                      ALU.subtract).then_inc(shift_ready, 1)

                def keep(n, base):
                    wait(dve, kept, n)
                    for x in range(2):
                        dve.wait_ge(row_ready, base + (x + 1))
                        grouped = ps_row[:, x, :].rearrange("p (i a w) -> p i w a", a=GR, w=GW)[:, :, 0:VW0, :]
                        dve.tensor_reduce(osum[:, 4 * x:4 * x + 4, :], grouped, AX.X, ALU.add).then_inc(row_read, 1)
                    dve.wait_ge(row_read, base + 2)
                    chain = Chain(dve, rec_ready, n)
                    chain(dve.reciprocal(rec[:, :], osum[:, :, DH0]))
                    b = n // H0
                    o = g.o0[:, bass.ds(b, 1), :, bass.ds((n % H0) * DH0, DH0)]
                    dve.tensor_tensor(o, osum[:, :, 0:DH0],
                                      rec[:, :].rearrange("p (i o) -> p i o", o=1).broadcast_to([P, TB, DH0]),
                                      ALU.mult).then_inc(kept, 1)

                def section(n, i4, h):
                    rows = not (is_at(n, NH - 1) or is_at(n, NH))
                    if rows:
                        peaks(n + 1, 1 - h % 2, row_base(n))
                    if not is_at(n, 0):
                        keep(n - 1, row_base(n) + (NU if rows else 0))

                set_up = Chain(dve, blank)
                dve.memset(q[:, :, :], 0.0)
                dve.memset(top[:, :, :], -3.0e38)
                set_up(dve.memset(k[:, :, :], 0.0))
                set_up(dve.memset(k[SHIFT0:SHIFT0 + NSH, :, :], 1.0))
                set_up(dve.memset(v[:, :, :, :], 0.0))
                set_up(dve.memset(nil[:, :], 0.0))
                peaks(0, 0, 0)
                heads(dve, section)


def run_experts(nc, g):
    with ExitStack() as ctx:
        r = Room(nc, ctx, "ex")
        w1 = r.sb("w1", [P, NE, HID])
        w2 = r.sb("w2", [P, NE, HC, D])
        b1 = r.sb("b1", [P, NE, HC])
        hid = r.sb("hid", [P, 2, HC, CH])
        pr = r.sb("pr", [P, NT, NE])
        ta = r.sb("ta", [P, NT, NE])
        tb = r.sb("tb", [P, NT, NE])
        pick = r.sb("pick", [P, NT, NE])
        m1 = r.sb("m1", [P, NT])
        ps_h = r.ps("ps_h", [P, 4, CH])
        ps_y = r.ps("ps_y", [P, 2, 4, P])

        w_in, step, chained = r.sem("w_in"), r.sem("step"), r.sem("chained")
        exp_in, exp_out = r.sem("exp_in"), r.sem("exp_out")
        h_ready, h_read, y_ready, y_read = r.sem("h_ready"), r.sem("h_read"), r.sem("y_ready"), r.sem("y_read")
        NCK = NT * P // CH
        TC = CH // P

        with nc.Block() as block:
            @block.sync
            def _(sp):
                sp.dma_start(w1[:, :, :], g.d_w1.rearrange("e d h -> d e h")).then_inc(w_in, 16)
                sp.dma_start(w2[:, :, :, :], g.d_w2.rearrange("e (c p) d -> p e c d", p=P)).then_inc(w_in, 16)
                sp.dma_start(b1[:, :, :], g.d_b1.rearrange("e (c p) -> p e c", p=P),
                             allow_slow_non_contiguous=True).then_inc(w_in, 16)
                sp.wait_ge(w_in, 48)

            @block.tensor
            def _(pe):
                pe.wait_ge(w_in, 48)

                def second(c, e, first):
                    s = c * NE + e
                    pe.wait_ge(h_read, s * HC + HC)
                    if not (first and e < 2):
                        pe.wait_ge(y_read, (s - 1) * TC)
                    for t in range(TC):
                        for hc in range(HC):
                            m = pe.matmul(ps_y[:, e % 2, t, :], hid[:, e % 2, hc, t * P:(t + 1) * P],
                                          w2[:, e, hc, :], start=(hc == 0), stop=(hc == HC - 1))
                    m.then_inc(y_ready, 1)

                def chunk(c, first):
                    for e in range(NE):
                        for hc in range(HC):
                            if not (first and e == 0):
                                pe.wait_ge(h_read, (c * NE + e) * HC + (hc - 3))
                            pe.matmul(ps_h[:, hc, :], w1[:, e, hc * P:(hc + 1) * P],
                                      g.xnT[:, bass.ds(c * CH, CH)], start=True, stop=True).then_inc(h_ready, 1)
                        if e >= 1:
                            second(c, e - 1, first)
                    second(c, NE - 1, first)

                chunk(0, True)
                with pe.Fori(1, NCK) as c:
                    chunk(c, False)

            @block.scalar
            def _(act):
                act.wait_ge(exp_in, 1)
                act.activation(pr[:, :, :], ta[:, :, :], ACT.Exp).then_inc(exp_out, 1)
                act.wait_ge(w_in, 48)

                def chunk(c, first):
                    for e in range(NE):
                        for hc in range(HC):
                            s = (c * NE + e) * HC + hc
                            act.wait_ge(h_ready, s + 1)
                            if hc == 0 and not (first and e < 2):
                                act.wait_ge(y_ready, c * NE + (e - 1))
                            act.activation(hid[:, e % 2, hc, :], ps_h[:, hc, :], ACT.Gelu,
                                           bias=b1[:, e, hc:hc + 1]).then_inc(h_read, 1)

                chunk(0, True)
                with act.Fori(1, NCK) as c:
                    chunk(c, False)

            @block.vector
            def _(dve):
                chain = Chain(dve, chained)

                def wide(ap):
                    return ap[:, :].rearrange("p (t o) -> p t o", o=1).broadcast_to([P, NT, NE])

                def first_of(dst, src):
                    chain(dve.tensor_reduce(m1[:, :], src[:, :, :], AX.X, ALU.max))
                    chain(dve.tensor_tensor(tb[:, :, :], src[:, :, :], wide(m1), ALU.is_ge))
                    chain(dve.tensor_tensor(tb[:, :, :], tb[:, :, :], g.desc[:, :].rearrange(
                        "p (t e) -> p t e", e=NE), ALU.mult))
                    chain(dve.tensor_reduce(m1[:, :], tb[:, :, :], AX.X, ALU.max))
                    chain(dve.tensor_tensor(dst[:, :, :], tb[:, :, :], wide(m1), ALU.is_ge))

                chain(dve.tensor_reduce(m1[:, :], g.logits[:, :, :], AX.X, ALU.max))
                dve.tensor_tensor(ta[:, :, :], g.logits[:, :, :], wide(m1), ALU.subtract).then_inc(exp_in, 1)
                dve.wait_ge(exp_out, 1)
                chain(dve.tensor_reduce(m1[:, :], pr[:, :, :], AX.X, ALU.add))
                chain(dve.reciprocal(m1[:, :], m1[:, :]))
                chain(dve.tensor_tensor(pr[:, :, :], pr[:, :, :], wide(m1), ALU.mult))
                first_of(pick, pr)
                chain(dve.scalar_tensor_tensor(ta[:, :, :], pick[:, :, :], -4.0, pr[:, :, :], ALU.mult, ALU.add))
                first_of(ta, ta)
                chain(dve.tensor_tensor(pick[:, :, :], pick[:, :, :], ta[:, :, :], ALU.add))
                chain(dve.tensor_tensor(g.comb[:, :, :], pick[:, :, :], pr[:, :, :], ALU.mult))

                comb = g.comb.rearrange("p t e -> p (t e)")
                acc = g.acc.rearrange("p t d -> p (t d)")

                def chunk(c):
                    for e in range(NE):
                        for t in range(TC):
                            dve.wait_ge(y_ready, c * NE + (e + 1))
                            if e >= 1:
                                dve.wait_ge(y_read, (c * NE + (e - 1)) * TC + (t + 1))
                            a = acc[:, bass.ds(c * CH + t * P, P)]
                            w = comb[:, bass.ds(c * (TC * NE) + (t * NE + e), 1)]
                            if e == 0:
                                m = dve.tensor_scalar(a, ps_y[:, e % 2, t, :], w, None, ALU.mult)
                            else:
                                m = dve.scalar_tensor_tensor(a, ps_y[:, e % 2, t, :], w, a, ALU.mult, ALU.add)
                            m.then_inc(y_read, 1)

                with dve.Fori(0, NCK) as c:
                    chunk(c)


def project_layer1(nc, g):
    with ExitStack() as ctx:
        r = Room(nc, ctx, "p1")
        wo = r.sb("wo", [P, D])
        bo = r.sb("bo", [1, D])
        b2 = r.sb("b2", [NE, D])
        wqk = r.sb("wqk", [P, NPAIR, P])
        wqk_rot = r.sb("wqk_rot", [P, NPAIR, P])
        wv = r.sb("wv", [P, KV1 * DH1])
        cos = r.sb("cos", [P, S])
        sin = r.sb("sin", [P, S])
        oT = r.sb("oT", [P, 2, P])
        cT = r.sb("cT", [NE, 2, P])
        xn = r.sb("xn", [P, NT, D])
        stats = r.sb("stats", [P, NT, 6])
        mv = r.sb("mv", [P, NT, 2])
        rs = r.sb("rs", [P, 4, NT])
        t1 = r.sb("t1", [P, NT])
        ra = r.sb("ra", [P, 2, CH])
        rb = r.sb("rb", [P, 2, CH])
        full = r.sb("full", [P, 2, CH])
        rest = r.sb("rest", [P, 2, CH])
        parts = r.sb("parts", [P, 2, 3, CH], BF16)
        ps_a = r.ps("ps_a", [P, 2, CH])
        ps_b = r.ps("ps_b", [P, 2, CH])
        ps_q = r.ps("ps_q", [P, 2, CH])
        ps_qr = r.ps("ps_qr", [P, 2, CH])

        w_in, step = r.sem("w_in"), r.sem("step")
        turned, oT_ready, sum_ready, sum_read = r.sem("turned"), r.sem("oT_ready"), r.sem("sum_ready"), r.sem("sum_read")
        acc_ready, x1_ready = r.sem("acc_ready"), r.sem("x1_ready")
        var_ready, root_ready = r.sem("var_ready"), r.sem("root_ready")
        xturned, xnT_ready = r.sem("xturned"), r.sem("xnT_ready")
        v_ready, v_kept = r.sem("v_ready"), r.sem("v_kept")
        q_ready, rot_a, rot_b, full_ready = r.sem("q_ready"), r.sem("rot_a"), r.sem("rot_b"), r.sem("full_ready")
        high_ready, rest_ready, mid_ready, low_ready = (r.sem("high_ready"), r.sem("rest_ready"), r.sem("mid_ready"),
                                                        r.sem("low_ready"))
        saved = [r.sem(f"saved{i}") for i in range(2)]
        NCQ = NT * P // CH
        XN0 = 2 + 5
        UB = 2 * NPAIR

        with nc.Block() as block:
            @block.sync
            def _(sp):
                for dst, src in ((wo[:, :], g.d_wo0), (bo[:, :], g.d_bo0), (b2[:, :], g.d_b2),
                                 (wv[:, :], g.d_wv1), (cos[:, :], g.d_cos), (sin[:, :], g.d_sin),
                                 (wqk[:, :, :], g.d_wqk1.rearrange("i (m o) -> i m o", o=P)),
                                 (wqk_rot[:, :, :], g.d_wqk1r.rearrange("i (m o) -> i m o", o=P))):
                    sp.dma_start(dst, src).then_inc(w_in, 16)
                sp.wait_ge(w_in, 16 * 8)
                with sp.Fori(0, B) as b:
                    for half in range(2):
                        for m in range(NPAIR):
                            u = half * NPAIR + m
                            sp.wait_ge(low_ready, b * UB + (u + 1))
                            sp.wait_ge(mid_ready, b * UB + (u + 1))
                            for part in range(3):
                                if m < H1 // 2:
                                    dst = g.d_q1[part, bass.ds(b, 1), m * P:(m + 1) * P, half * CH:(half + 1) * CH]
                                else:
                                    mk = m - H1 // 2
                                    dst = g.d_k1[part, bass.ds(b, 1), mk * P:(mk + 1) * P, half * CH:(half + 1) * CH]
                                sp.dma_start(dst, parts[:, u % 2, part, :]).then_inc(saved[u % 2], 16)
                for p in range(2):
                    sp.wait_ge(saved[p], 16 * 3 * UB * B // 2)

            @block.tensor
            def _(pe):
                pe.wait_ge(w_in, 16 * 8)
                for t in range(NT):
                    b, i = t // TB, t % TB
                    if t >= 2:
                        pe.wait_ge(oT_ready, 2 * (t - 1))
                    pe.transpose(ps_a[:, t % 2, 0:P], g.o0[:, b, i, :], g.ident[:, :])
                    pe.transpose(ps_a[0:NE, t % 2, P:2 * P], g.comb[:, t, :], g.ident[:, :]).then_inc(turned, 1)
                    pe.wait_ge(oT_ready, 2 * (t + 1))
                    if t >= 2:
                        pe.wait_ge(acc_ready, t - 1)
                    out = ps_b[:, t % 2, 0:P]
                    pe.matmul(out, oT[:, t % 2, :], wo[:, :], start=True, stop=False)
                    pe.matmul(out, g.ones[0:1, :], bo[0:1, :], start=False, stop=False)
                    pe.matmul(out, cT[:, t % 2, :], b2[:, :], start=False, stop=True).then_inc(sum_ready, 1)
                for t in range(NT):
                    pe.wait_ge(step, XN0 + t + 1)
                    if t % 4 == 0 and t >= 8:
                        pe.wait_ge(xnT_ready, t // 4 - 1)
                    m = pe.transpose(ps_a[:, (t // 4) % 2, (t % 4) * P:(t % 4 + 1) * P], xn[:, t, :], g.ident[:, :])
                    if t % 4 == 3:
                        m.then_inc(xturned, 1)
                for t in range(NT):
                    pe.wait_ge(xnT_ready, t // 4 + 1)
                    if t >= 2:
                        pe.wait_ge(v_kept, t - 1)
                    pe.matmul(ps_b[:, t % 2, 0:KV1 * DH1], g.xnT[:, t * P:(t + 1) * P], wv[:, :],
                              start=True, stop=True).then_inc(v_ready, 1)

                def batch(b, first):
                    for u in range(UB):
                        half, m = u // NPAIR, u % NPAIR
                        if not (first and u < 2):
                            pe.wait_ge(rot_a, b * UB + (u - 1))
                            pe.wait_ge(rot_b, b * UB + (u - 1))
                        xs = g.xnT[:, bass.ds(b * S + half * CH, CH)]
                        pe.matmul(ps_q[:, u % 2, :], wqk[:, m, :], xs, start=True, stop=True)
                        pe.matmul(ps_qr[:, u % 2, :], wqk_rot[:, m, :], xs, start=True, stop=True).then_inc(q_ready, 1)

                batch(0, True)
                with pe.Fori(1, B) as b:
                    batch(b, False)

            @block.vector
            def _(dve):
                dve.memset(g.v1[:, :, :, :], 1.0)
                chain = Chain(dve, step)
                for t in range(NT):
                    dve.tensor_tensor(g.x[:, t, :], g.x[:, t, :], g.acc[:, t, :], ALU.add).then_inc(x1_ready, 1)
                for t in range(NT):
                    dve.wait_ge(sum_ready, t + 1)
                    dve.wait_ge(x1_ready, t + 1)
                    dve.tensor_tensor(g.x[:, t, :], g.x[:, t, :], ps_b[:, t % 2, 0:P], ALU.add).then_inc(acc_ready, 1)
                dve.wait_ge(acc_ready, NT)
                norm_rows(dve, chain, g.x, xn, stats, mv, rs, t1, var_ready, root_ready)
                for t in range(NT):
                    b, j = t // TB, t % TB
                    dve.wait_ge(v_ready, t + 1)
                    dve.tensor_copy(g.v1[:, b * KV1:(b + 1) * KV1, j, 0:DH1],
                                    ps_b[:, t % 2, 0:KV1 * DH1].rearrange("p (h d) -> p h d", d=DH1)).then_inc(v_kept, 1)

                def batch(b, first):
                    for u in range(UB):
                        half = u // NPAIR
                        base = b * UB + u
                        dve.wait_ge(q_ready, base + 1)
                        if not (first and u < 2):
                            dve.wait_ge(full_ready, base - 1)
                        dve.tensor_tensor(ra[:, u % 2, :], ps_q[:, u % 2, :], cos[:, half * CH:(half + 1) * CH],
                                          ALU.mult).then_inc(rot_a, 1)
                        dve.tensor_tensor(rb[:, u % 2, :], ps_qr[:, u % 2, :], sin[:, half * CH:(half + 1) * CH],
                                          ALU.mult).then_inc(rot_b, 1)
                        dve.wait_ge(high_ready, base + 1)
                        if not (first and u < 2):
                            dve.wait_ge(low_ready, base - 1)
                        dve.tensor_tensor(rest[:, u % 2, :], full[:, u % 2, :], parts[:, u % 2, 0, :],
                                          ALU.subtract).then_inc(rest_ready, 1)
                        dve.wait_ge(mid_ready, base + 1)
                        dve.tensor_tensor(parts[:, u % 2, 2, :], rest[:, u % 2, :], parts[:, u % 2, 1, :],
                                          ALU.subtract).then_inc(low_ready, 1)

                batch(0, True)
                with dve.Fori(1, B) as b:
                    batch(b, False)

            @block.gpsimd
            def _(pool):
                def batch(b, first):
                    for u in range(UB):
                        base = b * UB + u
                        pool.wait_ge(rot_a, base + 1)
                        pool.wait_ge(rot_b, base + 1)
                        if not (first and u < 2):
                            pool.wait_ge(rest_ready, base - 1)
                            pool.wait_ge(high_ready, base - 1)
                        pool.tensor_tensor(full[:, u % 2, :], ra[:, u % 2, :], rb[:, u % 2, :],
                                           ALU.add).then_inc(full_ready, 1)

                batch(0, True)
                with pool.Fori(1, B) as b:
                    batch(b, False)

            @block.scalar
            def _(act):
                for t in range(NT):
                    act.wait_ge(turned, t + 1)
                    if t >= 2:
                        act.wait_ge(sum_ready, t - 1)
                    act.activation(oT[:, t % 2, :], ps_a[:, t % 2, 0:P], ACT.Copy).then_inc(oT_ready, 1)
                    act.activation(cT[:, t % 2, :], ps_a[0:NE, t % 2, P:2 * P], ACT.Copy).then_inc(oT_ready, 1)
                act.wait_ge(var_ready, 1)
                act.activation(rs[:, 1, :], rs[:, 0, :], ACT.Sqrt).then_inc(root_ready, 1)
                for c in range(NCQ):
                    act.wait_ge(xturned, c + 1)
                    act.activation(g.xnT[:, c * CH:(c + 1) * CH], ps_a[:, c % 2, :], ACT.Copy).then_inc(xnT_ready, 1)

                def batch(b, first):
                    for u in range(UB):
                        base = b * UB + u
                        act.wait_ge(full_ready, base + 1)
                        if not (first and u < 2):
                            act.wait_ge(saved[u % 2], b * (24 * UB) + 48 * (u // 2))
                        act.activation(parts[:, u % 2, 0, :], full[:, u % 2, :], ACT.Copy).then_inc(high_ready, 1)
                        act.wait_ge(rest_ready, base + 1)
                        act.activation(parts[:, u % 2, 1, :], rest[:, u % 2, :], ACT.Copy).then_inc(mid_ready, 1)

                batch(0, True)
                with act.Fori(1, B) as b:
                    batch(b, False)


def attend_layer1(nc, g):
    with ExitStack() as ctx:
        r = Room(nc, ctx, "a1")
        q = r.sb("q", [P, 2, 2, S], BF16)
        k = r.sb("k", [P, 2, 3, S], BF16)
        sc = r.sb("sc", [P, 2, S])
        work = r.sb("work", [P, S])
        best = r.sb("best", [P, 2, 8, 8])
        npeak = r.sb("npeak", [P, 2])
        prob = r.sb("prob", [P, 2, S])
        kept = r.sb("kept", [P, 2, S])
        kT = r.sb("kT", [P, 2, CH])
        rec = r.sb("rec", [P, 2])
        ps_s = r.ps("ps_s", [P, 2, S])
        ps_t = r.ps("ps_t", [P, 2, CH])
        ps_o = r.ps("ps_o", [P, 2, CH])[:, :, 0:VW1]

        qk_in = [r.sem(f"qk_in{i}") for i in range(2)]
        s_ready, s_kept, step = r.sem("s_ready"), r.sem("s_kept"), r.sem("step")
        best_ready, peak_ready, p_ready = r.sem("best_ready"), r.sem("peak_ready"), r.sem("p_ready")
        cut_ready, t_ready, t_read = r.sem("cut_ready"), r.sem("t_ready"), r.sem("t_read")
        o_ready, o_kept = r.sem("o_ready"), r.sem("o_kept")

        NH = B * H1
        GRP = H1 // KV1
        ROUNDS = TOPK // 8
        TU = sum((i * P) // CH + 1 for i in range(TB))
        STEPS = TB * (2 * ROUNDS - 1)
        SCALE = 1.0 / 8.0
        assert TU % 2 == 0
        T0 = [sum((a * P) // CH + 1 for a in range(i)) for i in range(TB)]

        with nc.Block() as block:
            @block.sync
            def _(sp):
                def load(n, p):
                    for st, (top, low) in enumerate(((0, 1), (0, 2))):
                        for half, part in enumerate((top, low)):
                            src = g.d_q1.rearrange("t b (h r) n -> t (b h) r n", r=DH1)[part, bass.ds(n, 1)]
                            sp.dma_start(q[half * DH1:(half + 1) * DH1, p, st, :], src).then_inc(qk_in[p], 16)
                    for st, (top, low) in enumerate(((0, 0), (1, 1), (2, 0))):
                        for half, part in enumerate((top, low)):
                            src = g.d_k1.rearrange("t b (h r) n -> t (b h) r n", r=DH1)[part, bass.ds(n // GRP, 1)]
                            sp.dma_start(k[half * DH1:(half + 1) * DH1, p, st, :], src).then_inc(qk_in[p], 16)

                load(0, 0)
                load(1, 1)
                with sp.Fori(0, NH // 2 - 1) as i:
                    for p in range(2):
                        sp.wait_ge(s_ready, (i * 2 + p + 1) * TB)
                        load(i * 2 + 2 + p, p)

            @block.tensor
            def _(pe):
                def scores(n, i2, p, i, first):
                    if i == 0:
                        pe.wait_ge(qk_in[p], i2 * 160 + 160)
                    if not (first and p == 0 and i < 2):
                        pe.wait_ge(s_kept, n * TB + (i - 1))
                    width = (i + 1) * P
                    qa, qc = q[:, p, 0, i * P:width], q[:, p, 1, i * P:width]
                    for c in range(0, width, CH):
                        w = min(CH, width - c)
                        diag = c + w == width
                        out = ps_s[:, i % 2, c:c + w]
                        pe.matmul(out, qa, k[:, p, 0, c:c + w], start=True, stop=False)
                        pe.matmul(out, qa, k[:, p, 1, c:c + w], start=False, stop=False)
                        m = pe.matmul(out, qc, k[:, p, 2, c:c + w], start=False, stop=True)
                        if diag:
                            m = pe.matmul(ps_s[:, i % 2, width - P:width], g.identb[:, :], g.maskq[:, :],
                                          start=False, stop=True, skip_group_check=True)
                    m.then_inc(s_ready, 1)

                def values(n, p, i, first):
                    pe.wait_ge(cut_ready, n * TB + (i + 1))
                    v = g.v1.rearrange("p n j w -> p (n j w)")
                    nj = i + 1
                    chunks = [(c, min(4, nj - c)) for c in range(0, nj, 4)]

                    def turn(x):
                        c, cnt = chunks[x]
                        tu = T0[i] + x
                        if not (first and p == 0 and tu < 2):
                            pe.wait_ge(t_read, n * TU + (tu - 1))
                        for j in range(c, c + cnt):
                            m = pe.transpose(ps_t[:, tu % 2, (j - c) * P:(j - c + 1) * P],
                                             kept[:, i % 2, j * P:(j + 1) * P], g.ident[:, :])
                        m.then_inc(t_ready, 1)

                    for x in range(len(chunks)):
                        turn(x)
                    if not (first and p == 0 and i < 2):
                        pe.wait_ge(o_kept, n * TB + (i - 1))
                    for x, (c, cnt) in enumerate(chunks):
                        tu = T0[i] + x
                        pe.wait_ge(t_read, n * TU + (tu + 1))
                        for j in range(c, c + cnt):
                            m = pe.matmul(ps_o[:, i % 2, :], kT[:, tu % 2, (j - c) * P:(j - c + 1) * P],
                                          v[:, bass.ds((n // GRP) * (TB * VW1) + j * VW1, VW1)],
                                          start=(j == 0), stop=(j == i))
                    m.then_inc(o_ready, 1)

                def head(n, i2, p, first, last_head):
                    for i in range(TB):
                        if i < TB - 2:
                            scores(n, i2, p, i + 2, first)
                        elif not last_head:
                            scores(n + 1, i2 + p, 1 - p, i + 2 - TB, False)
                        values(n, p, i, first)

                scores(0, 0, 0, 0, True)
                scores(0, 0, 0, 1, True)
                head(0, 0, 0, True, False)
                head(1, 0, 1, True, False)
                with pe.Fori(1, NH // 2 - 1) as i:
                    head(i * 2, i, 0, False, False)
                    head(i * 2 + 1, i, 1, False, False)
                head(NH - 2, NH // 2 - 1, 0, False, False)
                head(NH - 1, NH // 2 - 1, 1, False, True)

            @block.scalar
            def _(act):
                def keep_scores(n, p, i, first):
                    act.wait_ge(s_ready, n * TB + (i + 1))
                    if not (first and p == 0 and i < 2):
                        act.wait_ge(cut_ready, n * TB + (i - 1))
                    act.activation(sc[:, i % 2, 0:(i + 1) * P], ps_s[:, i % 2, 0:(i + 1) * P], ACT.Copy,
                                   scale=SCALE).then_inc(s_kept, 1)

                def weights(n, p, i, first):
                    act.wait_ge(peak_ready, n * TB + (i + 1))
                    act.activation(prob[:, i % 2, 0:(i + 1) * P], sc[:, i % 2, 0:(i + 1) * P], ACT.Exp,
                                   bias=npeak[:, i % 2:i % 2 + 1]).then_inc(p_ready, 1)

                def turned(n, p, i, first):
                    for x, c in enumerate(range(0, i + 1, 4)):
                        cnt = min(4, i + 1 - c)
                        tu = T0[i] + x
                        act.wait_ge(t_ready, n * TU + (tu + 1))
                        if x == 0 and not (first and p == 0 and i == 0):
                            act.wait_ge(o_ready, n * TB + i)
                        act.activation(kT[:, tu % 2, 0:cnt * P], ps_t[:, tu % 2, 0:cnt * P],
                                       ACT.Copy).then_inc(t_read, 1)

                def head(n, p, first, start_tile=0):
                    for i in range(TB):
                        weights(n, p, i, first)
                        if not (first and p == 0 and i == 0):
                            if i == 0:
                                turned(n - 1, 1 - p, TB - 1, first and p == 1)
                            else:
                                turned(n, p, i - 1, first)
                        if i + 1 < TB:
                            keep_scores(n, p, i + 1, first)
                        elif start_tile is not None:
                            keep_scores(n + 1, 1 - p, 0, False)

                keep_scores(0, 0, 0, True)
                head(0, 0, True)
                head(1, 1, True)
                with act.Fori(1, NH // 2 - 1) as i:
                    head(i * 2, 0, False)
                    head(i * 2 + 1, 1, False)
                head(NH - 2, 0, False)
                head(NH - 1, 1, False, None)
                turned(NH - 1, 1, TB - 1, False)

            @block.vector
            def _(dve):
                def cut(n, p, i, first):
                    dve.wait_ge(p_ready, n * TB + (i + 1))
                    if not (first and p == 0 and i < 2):
                        dve.wait_ge(o_ready, n * TB + (i - 1))
                    w = (i + 1) * P
                    dve.scalar_tensor_tensor(kept[:, i % 2, 0:w], sc[:, i % 2, 0:w], best[:, i % 2, 7, 7:8],
                                             prob[:, i % 2, 0:w], ALU.is_ge, ALU.mult).then_inc(cut_ready, 1)

                def out(n, p, i):
                    dve.wait_ge(o_ready, n * TB + (i + 1))
                    chain = Chain(dve, rec_done, n * TB + i)
                    chain(dve.reciprocal(rec[:, i % 2:i % 2 + 1], ps_o[:, i % 2, DH1:VW1]))
                    b = n // H1
                    o = g.o1[:, bass.ds(b, 1), i, bass.ds((n % H1) * DH1, DH1)]
                    dve.tensor_scalar(o, ps_o[:, i % 2, 0:DH1], rec[:, i % 2:i % 2 + 1], None,
                                      ALU.mult).then_inc(o_kept, 1)

                def head(n, p, first):
                    for i in range(TB):
                        w = (i + 1) * P
                        if not (first and p == 0 and i == 0):
                            dve.sem_clear(step)
                        bst = best[:, i % 2]
                        dve.wait_ge(s_kept, n * TB + (i + 1))
                        dve.sem_inc(step, 1)
                        chain = Chain(dve, step, 1)
                        dve.wait_ge(step, 1)
                        chain(dve.max(bst[:, 0, :], sc[:, i % 2, 0:w]))
                        if not (first and p == 0 and i < 2):
                            dve.wait_ge(p_ready, n * TB + (i - 1))
                        dve.tensor_scalar(npeak[:, i % 2:i % 2 + 1], bst[:, 0, 0:1], -1.0, None,
                                          ALU.mult).then_inc(peak_ready, 1)
                        src = sc[:, i % 2, 0:w]
                        for rd in range(1, ROUNDS):
                            chain(dve.match_replace(work[:, 0:w], bst[:, rd - 1, :], src, -3.0e38))
                            src = work[:, 0:w]
                            chain(dve.max(bst[:, rd, :], src))
                        cut(n, p, i, first)
                        if not (first and p == 0 and i == 0):
                            if i == 0:
                                out(n - 1, 1 - p, TB - 1)
                            else:
                                out(n, p, i - 1)

                rec_done = r.sem("rec_done")
                head(0, 0, True)
                head(1, 1, True)
                with dve.Fori(1, NH // 2) as i:
                    head(i * 2, 0, False)
                    head(i * 2 + 1, 1, False)
                out(NH - 1, 1, TB - 1)


def walk_trees(nc, g):
    with ExitStack() as ctx:
        r = Room(nc, ctx, "ff")
        win = r.sb("win", [P, WIDTH])
        wout = r.sb("wout", [P, NCH, D])
        bin32 = r.sb("bin32", [1, WIDTH])
        rest = r.sb("rest", [1, WIDTH])
        binp = r.sb("binp", [1, 3, WIDTH], BF16)
        xt = r.sb("xt", [P, 2, P])
        dec = r.sb("dec", [P, PAR, NODES], BF16)
        path = r.sb("path", [P, PAR, NODES], BF16)
        act_v = r.sb("act_v", [P, 2, WIDTH])
        mT = r.sb("mT", [P, 2, CH])
        ps_l = r.ps("ps_l", [P, 4 * CH])
        ps_t = r.ps("ps_t", [P, 2, CH])
        ps_f = r.ps("ps_f", [P, CH])

        w_in, bias_ready, step = r.sem("w_in"), r.sem("bias_ready"), r.sem("step")
        x_ready, l_ready, dec_ready, silu_ready = r.sem("x_ready"), r.sem("l_ready"), r.sem("dec_ready"), r.sem("silu_ready")
        masked, t_ready, t_read, f_ready, f_read = (r.sem("masked"), r.sem("t_ready"), r.sem("t_read"), r.sem("f_ready"),
                                                    r.sem("f_read"))
        NCK = (NCH + 3) // 4
        STEPS = 2 * DEPTH - 1
        HALVES = [(0, 2 * CH), (2 * CH, WIDTH)]
        BOUNDS = [(c * CH, min(CH, WIDTH - c * CH)) for c in range(4)]

        with nc.Block() as block:
            @block.sync
            def _(sp):
                sp.dma_start(win[:, :], g.d_win).then_inc(w_in, 16)
                sp.dma_start(bin32[:, :], g.d_bin).then_inc(w_in, 16)
                sp.dma_start(wout[:, 0:NCH - 1, :], g.d_wout[0:(NCH - 1) * P, :].rearrange(
                    "(c p) d -> p c d", p=P)).then_inc(w_in, 16)
                sp.dma_start(wout[0:LASTW, NCH - 1, :], g.d_wout[(NCH - 1) * P:WIDTH, :]).then_inc(w_in, 16)
                sp.wait_ge(w_in, 64)

            @block.gpsimd
            def _(pool):
                def tile(t, p, first):
                    if not first:
                        pool.wait_ge(l_ready, t - 1)
                    pool.tensor_copy(xt[:, p, :], g.xnT[:, bass.ds(t * P, P)]).then_inc(x_ready, 1)

                tile(0, 0, True)
                tile(1, 1, True)
                with pool.Fori(1, NT // 2) as i:
                    tile(i * 2, 0, False)
                    tile(i * 2 + 1, 1, False)

            @block.tensor
            def _(pe):
                pe.wait_ge(w_in, 64)
                pe.wait_ge(bias_ready, 5)

                def logits(t, p, first):
                    pe.wait_ge(x_ready, t + 1)
                    if not (first and p == 0):
                        pe.wait_ge(silu_ready, t * 2)
                    for c, w in BOUNDS:
                        for part in range(3):
                            pe.matmul(ps_l[:, c:c + w], g.onesb[0:1, :], binp[0:1, part, c:c + w],
                                      start=(part == 0), stop=False)
                        m = pe.matmul(ps_l[:, c:c + w], xt[:, p, :], win[:, c:c + w], start=False, stop=True)
                    m.then_inc(l_ready, 1)

                def outputs(t, p, first):
                    pe.wait_ge(masked, t + 1)
                    if not (first and p == 0):
                        pe.wait_ge(f_read, t)

                    def turn(x):
                        if not (first and p == 0 and x < 2):
                            pe.wait_ge(t_read, t * NCK + (x - 1))
                        for c in range(4 * x, min(4 * x + 4, NCH)):
                            w = P if c < NCH - 1 else LASTW
                            m = pe.transpose(ps_t[0:w, x % 2, (c % 4) * P:(c % 4 + 1) * P],
                                             act_v[:, p, c * P:c * P + w], g.ident[:, :])
                        m.then_inc(t_ready, 1)

                    turn(0)
                    for x in range(NCK):
                        if x + 1 < NCK:
                            turn(x + 1)
                        pe.wait_ge(t_read, t * NCK + (x + 1))
                        for c in range(4 * x, min(4 * x + 4, NCH)):
                            w = P if c < NCH - 1 else LASTW
                            m = pe.matmul(ps_f[:, 0:P], mT[0:w, x % 2, (c % 4) * P:(c % 4 + 1) * P],
                                          wout[0:w, c, :], start=(c == 0), stop=(c == NCH - 1))
                        if x == NCK - 1:
                            m.then_inc(f_ready, 1)

                logits(0, 0, True)
                logits(1, 1, True)
                outputs(0, 0, True)
                with pe.Fori(1, NT // 2) as i:
                    logits(i * 2, 0, False)
                    outputs(i * 2 - 1, 1, False)
                    logits(i * 2 + 1, 1, False)
                    outputs(i * 2, 0, False)
                outputs(NT - 1, 1, False)

            @block.scalar
            def _(act):
                def silu(t, p, first):
                    act.wait_ge(l_ready, t + 1)
                    if not first:
                        act.wait_ge(t_ready, (t - 1) * NCK)
                    for x, (lo, hi) in enumerate(HALVES):
                        act.wait_ge(dec_ready, t * 2 + (x + 1))
                        act.activation(act_v[:, p, lo:hi], ps_l[:, lo:hi], ACT.Silu).then_inc(silu_ready, 1)

                def turned(t, p, first):
                    for x in range(NCK):
                        act.wait_ge(t_ready, t * NCK + (x + 1))
                        full = 4 * P if x < NCK - 1 else (NCH - 1 - 4 * x) * P
                        if x < NCK - 1:
                            act.activation(mT[:, x % 2, 0:full], ps_t[:, x % 2, 0:full], ACT.Copy).then_inc(t_read, 1)
                        else:
                            act.activation(mT[:, x % 2, 0:full], ps_t[:, x % 2, 0:full], ACT.Copy)
                            act.activation(mT[0:LASTW, x % 2, full:full + P], ps_t[0:LASTW, x % 2, full:full + P],
                                           ACT.Copy).then_inc(t_read, 1)

                silu(0, 0, True)
                silu(1, 1, True)
                turned(0, 0, True)
                with act.Fori(1, NT // 2) as i:
                    silu(i * 2, 0, False)
                    turned(i * 2 - 1, 1, False)
                    silu(i * 2 + 1, 1, False)
                    turned(i * 2, 0, False)
                turned(NT - 1, 1, False)

            @block.vector
            def _(dve):
                dve.wait_ge(w_in, 64)
                b = Chain(dve, bias_ready)
                b(dve.tensor_copy(binp[0:1, 0, :], bin32[0:1, :]))
                b(dve.tensor_tensor(rest[0:1, :], bin32[0:1, :], binp[0:1, 0, :], ALU.subtract))
                b(dve.tensor_copy(binp[0:1, 1, :], rest[0:1, :]))
                b(dve.tensor_tensor(binp[0:1, 2, :], rest[0:1, :], binp[0:1, 1, :], ALU.subtract))
                b(dve.memset(path[:, :, 0:1], 1.0))

                def walk(t, p):
                    dve.wait_ge(l_ready, t + 1)
                    for lo, hi in HALVES:
                        dve.tensor_scalar(dec.rearrange("p a n -> p (a n)")[:, lo:hi], ps_l[:, lo:hi], 0.0, None,
                                          ALU.is_gt).then_inc(dec_ready, 1)
                    dve.wait_ge(dec_ready, t * 2 + 2)
                    chain = Chain(dve, step, t * STEPS)
                    for d in range(DEPTH):
                        lo, nx = 2 ** d - 1, 2 ** (d + 1) - 1
                        here = path[:, :, lo:lo + 2 ** d]
                        kids = path[:, :, nx:nx + 2 ** (d + 1)].rearrange("p a (n k) -> p a n k", k=2)
                        chain(dve.tensor_tensor(kids[:, :, :, 1], here, dec[:, :, lo:lo + 2 ** d], ALU.mult))
                        m = dve.tensor_tensor(kids[:, :, :, 0], here, kids[:, :, :, 1], ALU.subtract)
                        if d < DEPTH - 1:
                            chain(m)
                    m.then_inc(leaf_ready, 1)
                    dve.wait_ge(leaf_ready, t + 1)
                    dve.wait_ge(silu_ready, t * 2 + 2)
                    a = act_v[:, p, :]
                    dve.tensor_tensor(a, a, path.rearrange("p a n -> p (a n)"), ALU.mult).then_inc(masked, 1)

                def add(t):
                    dve.wait_ge(f_ready, t + 1)
                    xs = g.x.rearrange("p t d -> p (t d)")[:, bass.ds(t * P, P)]
                    dve.tensor_tensor(xs, xs, ps_f[:, 0:P], ALU.add).then_inc(f_read, 1)

                leaf_ready = r.sem("leaf_ready")
                walk(0, 0)
                walk(1, 1)
                add(0)
                with dve.Fori(1, NT // 2) as i:
                    walk(i * 2, 0)
                    add(i * 2 - 1)
                    walk(i * 2 + 1, 1)
                    add(i * 2)
                add(NT - 1)


def finish(nc, g):
    with ExitStack() as ctx:
        r = Room(nc, ctx, "fin")
        wo = r.sb("wo", [P, H1 // 2, D])
        oT = r.sb("oT", [P, 4, CH])
        ps_t = r.ps("ps_t", [P, 4, CH])
        ps_f = r.ps("ps_f", [P, 2, CH])
        w_in, turned, oT_ready = r.sem("w_in"), r.sem("turned"), r.sem("oT_ready")
        f_ready, f_read, out_done = r.sem("f_ready"), r.sem("f_read"), r.sem("out_done")

        with nc.Block() as block:
            @block.sync
            def _(sp):
                sp.dma_start(wo[:, :, :], g.d_wo1.rearrange("(c p) d -> p c d", p=P)).then_inc(w_in, 16)
                for t in range(NT):
                    sp.wait_ge(f_read, t + 1)
                    b, j = t // TB, t % TB
                    sp.dma_start(g.d_out[b, j * P:(j + 1) * P, :], g.x[:, t, :]).then_inc(out_done, 16)
                sp.wait_ge(out_done, 16 * NT)

            @block.tensor
            def _(pe):
                pe.wait_ge(w_in, 16)

                def turn(t):
                    b, i = t // TB, t % TB
                    for x in range(2):
                        u = 2 * t + x
                        if u >= 4:
                            pe.wait_ge(oT_ready, u - 3)
                        for c in range(4):
                            f = (4 * x + c) * P
                            m = pe.transpose(ps_t[:, u % 4, c * P:(c + 1) * P], g.o1[:, b, i, f:f + P], g.ident[:, :])
                        m.then_inc(turned, 1)

                turn(0)
                for t in range(NT):
                    if t + 1 < NT:
                        turn(t + 1)
                    pe.wait_ge(oT_ready, 2 * t + 2)
                    if t >= 2:
                        pe.wait_ge(f_read, t - 1)
                    for c in range(8):
                        u = 2 * t + c // 4
                        m = pe.matmul(ps_f[:, t % 2, 0:P], oT[:, u % 4, (c % 4) * P:(c % 4 + 1) * P], wo[:, c, :],
                                      start=(c == 0), stop=(c == 7))
                    m.then_inc(f_ready, 1)

            @block.scalar
            def _(act):
                for u in range(2 * NT):
                    act.wait_ge(turned, u + 1)
                    if u >= 4:
                        act.wait_ge(f_ready, (u - 4) // 2 + 1)
                    act.activation(oT[:, u % 4, :], ps_t[:, u % 4, :], ACT.Copy).then_inc(oT_ready, 1)

            @block.vector
            def _(dve):
                for t in range(NT):
                    dve.wait_ge(f_ready, t + 1)
                    dve.tensor_tensor(g.x[:, t, :], g.x[:, t, :], ps_f[:, t % 2, 0:P], ALU.add).then_inc(f_read, 1)


class Shared:
    pass


STAGES = 6


def build_program(nc, g):
    with ExitStack() as ctx:
        r = Room(nc, ctx, "g")
        g.d_stack0 = nc.dram_tensor("stack0", (2, B, H0, ROWS0, S), BF16, kind="Internal").ap()
        g.d_q1 = nc.dram_tensor("q1parts", (3, B, H1 * DH1, S), BF16, kind="Internal").ap()
        g.d_k1 = nc.dram_tensor("k1parts", (3, B, KV1 * DH1, S), BF16, kind="Internal").ap()
        g.ident = r.sb("ident", [P, P])
        g.identb = r.sb("identb", [P, P], BF16)
        g.maskq = r.sb("maskq", [P, P], BF16)
        g.maskk = r.sb("maskk", [P, P], BF16)
        g.ones = r.sb("ones", [P, P])
        g.onesb = r.sb("onesb", [P, P], BF16)
        g.x = r.sb("x", [P, NT, D])
        g.xnT = r.sb("xnT", [P, NT * P])
        with ExitStack() as layer:
            r0 = Room(nc, layer, "l0")
            g.desc = r0.sb("desc", [P, NT * NE])
            g.logits = r0.sb("logits", [P, NT, NE])
            g.comb = r0.sb("comb", [P, NT, NE])
            g.v0 = r0.sb("v0", [P, B * H0, TB, VW0])
            g.o0 = r0.sb("o0", [P, B, TB, H0 * DH0])
            g.acc = r0.sb("acc", [P, NT, D])
            g.v1 = r0.sb("v1", [P, B * KV1, TB, VW1])
            project_layer0(nc, g)
            attend_layer0(nc, g)
            run_experts(nc, g)
            project_layer1(nc, g)
            g.o1 = r0.sb("o1", [P, B, TB, H1 * DH1])
            if STAGES > 4:
                attend_layer1(nc, g)
            if STAGES > 5:
                walk_trees(nc, g)
            finish(nc, g)


_OUTS = [((B, S, D), "float32")]


def kernel(L0_attn_x, L0_attn_Wq, L0_attn_bq, L0_attn_Wk, L0_attn_bk, L0_attn_Wv, L0_attn_bv, L0_attn_Wo,
           L0_attn_bo, L0_ffn_Wr, L0_ffn_W1, L0_ffn_b1, L0_ffn_W2, L0_ffn_b2, L1_attn_Wq, L1_attn_Wk, L1_attn_Wv,
           L1_attn_Wo, L1_ffn_W_in, L1_ffn_b_in, L1_ffn_W_out):
    import ml_dtypes
    import numpy as np
    import concourse.bacc as bacc
    from concourse.bass_utils import run_bass_kernel_spmd

    def lay(a):
        return np.ascontiguousarray(a)

    future = np.triu(np.ones((P, P), bool), 1)
    maskq = np.where(future, np.float32(NEG), np.float32(0)).astype(ml_dtypes.bfloat16)
    inv_freq = (1.0 / np.float32(10000.0) ** (np.arange(0, DH1, 2, dtype=np.float32) / np.float32(DH1)))
    angles = np.outer(np.arange(S, dtype=np.float32), inv_freq.astype(np.float32))
    emb = np.concatenate([angles, angles], axis=-1)
    cos, sin = np.cos(emb).T, np.sin(emb).T
    sign = np.where(np.arange(DH1) < DH1 // 2, -1.0, 1.0).astype(np.float32)[:, None]
    desc = np.tile(np.arange(NE, 0, -1, dtype=np.float32), (P, NT))

    wqk = np.concatenate([np.asarray(L1_attn_Wq), np.asarray(L1_attn_Wk)], axis=0)
    half = DH1 // 2
    turned = wqk.reshape(H1 + KV1, 2, half, D)[:, ::-1].reshape(wqk.shape)
    feeds = {
        "d_x": lay(L0_attn_x), "d_wq0": lay(np.asarray(L0_attn_Wq).T), "d_wk0": lay(np.asarray(L0_attn_Wk).T),
        "d_wv0": lay(np.asarray(L0_attn_Wv).T), "d_wo0": lay(np.asarray(L0_attn_Wo).T),
        "d_bq0": lay(np.asarray(L0_attn_bq).reshape(P, 1)), "d_bk0": lay(np.asarray(L0_attn_bk).reshape(P, 1)),
        "d_bv0": lay(np.asarray(L0_attn_bv).reshape(1, P)), "d_bo0": lay(np.asarray(L0_attn_bo).reshape(1, P)),
        "d_wr": lay(np.asarray(L0_ffn_Wr).T), "d_w1": lay(L0_ffn_W1), "d_b1": lay(L0_ffn_b1),
        "d_w2": lay(L0_ffn_W2), "d_b2": lay(L0_ffn_b2),
        "d_wqk1": lay(wqk.T), "d_wqk1r": lay(turned.T), "d_wv1": lay(np.asarray(L1_attn_Wv).T),
        "d_wo1": lay(np.asarray(L1_attn_Wo).T), "d_win": lay(np.asarray(L1_ffn_W_in).T),
        "d_bin": lay(np.asarray(L1_ffn_b_in).reshape(1, WIDTH)), "d_wout": lay(np.asarray(L1_ffn_W_out).T),
        "d_ident": np.eye(P, dtype=np.float32), "d_identb": np.eye(P, dtype=np.float32).astype(ml_dtypes.bfloat16),
        "d_maskq": lay(maskq), "d_maskk": lay(maskq.T), "d_desc": desc,
        "d_cos": lay(np.concatenate([cos, cos]).astype(np.float32)),
        "d_sin": lay(np.concatenate([sin * sign, sin * sign]).astype(np.float32)),
    }
    nc = bacc.Bacc("TRN2", target_bir_lowering=False, num_devices=1)
    g = Shared()
    arrays = {}
    for name, a in feeds.items():
        arrays[name] = a
        g.__dict__[name] = nc.dram_tensor(name, a.shape, mybir.dt.from_np(a.dtype), kind="ExternalInput").ap()
    shape, dtype = _OUTS[0]
    g.d_out = nc.dram_tensor("out", shape, mybir.dt.from_np(np.dtype(dtype)), kind="ExternalOutput").ap()
    build_program(nc, g)
    r = run_bass_kernel_spmd(nc, [arrays], core_ids=[0])
    return r.results[0]["out"]
```

```python
from contextlib import ExitStack

import numpy as np

import concourse.bass as bass
from concourse import mybir

ALU = mybir.AluOpType
ACT = mybir.ActivationFunctionType
AX = mybir.AxisListType
F32 = mybir.dt.float32
BF16 = mybir.dt.bfloat16

P = 128
B, S, D = 2, 1024, 128
NT = B * S // P
TB = S // P
CH = 512
NEG = -1.0e30
EPS = 1e-5

H0, DH0 = 16, 8
ROWS0 = 6 * DH0
SHIFT0 = 64
NSH = 3
VW0 = DH0 + 1

NE, HID = 8, 512
HC = HID // P

H1, KV1, DH1 = 16, 4, 64
TOPK = 64
VW1 = DH1 + 1
NPAIR = (H1 + KV1) // 2

PAR, DEPTH = 8, 7
NODES = 2 ** (DEPTH + 1) - 1
WIDTH = PAR * NODES
NCH = (WIDTH + P - 1) // P
LASTW = WIDTH - (NCH - 1) * P


class Chain:

    def __init__(self, eng, sem, start=0):
        self.eng, self.sem, self.start, self.n = eng, sem, start, 0

    def __call__(self, ins):
        ins.then_inc(self.sem, 1)
        self.n += 1
        self.eng.wait_ge(self.sem, self.start + self.n)


def is_at(n, value):
    return isinstance(n, int) and n == value


def wait(eng, sem, value):
    if not (isinstance(value, int) and value <= 0):
        eng.wait_ge(sem, value)


class Room:

    def __init__(self, nc, ctx, stage):
        self.nc, self.ctx, self.stage = nc, ctx, stage

    def sb(self, name, shape, dt=F32):
        return self.ctx.enter_context(self.nc.sbuf_tensor(f"{self.stage}_{name}", shape, dt))

    def ps(self, name, shape, dt=F32):
        return self.ctx.enter_context(self.nc.psum_tensor(f"{self.stage}_{name}", shape, dt))

    def sem(self, name):
        return self.ctx.enter_context(self.nc.semaphore(f"{self.stage}_{name}"))


def norm_rows(dve, chain, src, dst, stats, mv, rs, t1, var_ready, root_ready):
    for t in range(NT):
        last = dve.bn_stats(stats[:, t, :], src[:, t, :])
    chain(last)
    for t in range(NT):
        last = dve.bn_aggr(mv[:, t, :], stats[:, t, :])
    chain(last)
    dve.tensor_scalar(rs[:, 0, :], mv[:, :, 1], EPS, None, ALU.add).then_inc(var_ready, 1)
    dve.wait_ge(root_ready, 1)
    chain(dve.reciprocal(rs[:, 2, :], rs[:, 1, :]))
    chain(dve.tensor_tensor(t1[:, :], rs[:, 2, :], rs[:, 2, :], ALU.mult))
    chain(dve.tensor_tensor(t1[:, :], t1[:, :], rs[:, 0, :], ALU.mult))
    chain(dve.tensor_scalar(t1[:, :], t1[:, :], -0.5, 1.5, ALU.mult, ALU.add))
    chain(dve.tensor_tensor(rs[:, 3, :], rs[:, 2, :], t1[:, :], ALU.mult))
    for t in range(NT):
        dve.tensor_scalar(dst[:, t, :], src[:, t, :], mv[:, t, 0:1], rs[:, 3, t:t + 1],
                          ALU.subtract, ALU.mult).then_inc(chain.sem, 1)
        chain.n += 1


def project_layer0(nc, g):
    with ExitStack() as ctx:
        r = Room(nc, ctx, "p0")
        wq = r.sb("wq", [P, D])
        wk = r.sb("wk", [P, D])
        wv = r.sb("wv", [P, D])
        wr = r.sb("wr", [P, NE])
        bq = r.sb("bq", [P, 1])
        bk = r.sb("bk", [P, 1])
        bv = r.sb("bv", [1, D])
        xn = r.sb("xn", [P, NT, D])
        stats = r.sb("stats", [P, NT, 6])
        mv = r.sb("mv", [P, NT, 2])
        rs = r.sb("rs", [P, 4, NT])
        t1 = r.sb("t1", [P, NT])
        full = r.sb("full", [P, 2, CH])
        rest = r.sb("rest", [P, 2, CH])
        parts = r.sb("parts", [P, 2, 3, NT * P], BF16)
        ps_t = r.ps("ps_t", [P, 2, CH])
        ps_p = r.ps("ps_p", [P, 2, CH])
        ps_v = r.ps("ps_v", [P, 2, CH])
        ps_r = r.ps("ps_r", [P, CH])[:, 0:NT * NE].rearrange("p (t e) -> p t e", e=NE)

        x_in, w_in = r.sem("x_in"), r.sem("w_in")
        step = r.sem("step")
        var_ready, root_ready = r.sem("var_ready"), r.sem("root_ready")
        turned, xnT_ready = r.sem("turned"), r.sem("xnT_ready")
        prod_ready, high_ready, rest_ready = r.sem("prod_ready"), r.sem("high_ready"), r.sem("rest_ready")
        mid_ready, low_ready = r.sem("mid_ready"), r.sem("low_ready")
        v_ready, v_kept, r_ready = r.sem("v_ready"), r.sem("v_kept"), r.sem("r_ready")
        ones_ready, saved = r.sem("ones_ready"), r.sem("saved")
        NCQ = NT * P // CH
        XN0 = 2 + 5

        with nc.Block() as block:
            @block.sync
            def _(sp):
                sp.dma_start(g.x[:, :, :], g.d_x.rearrange("b (j p) d -> p (b j) d", p=P)).then_inc(x_in, 16)
                for dst, src in ((g.ident, g.d_ident), (g.identb, g.d_identb), (wq, g.d_wq0), (wk, g.d_wk0),
                                 (wv, g.d_wv0), (wr, g.d_wr), (bq, g.d_bq0), (bk, g.d_bk0), (bv, g.d_bv0),
                                 (g.maskq, g.d_maskq), (g.maskk, g.d_maskk), (g.desc, g.d_desc)):
                    sp.dma_start(dst[:, :], src).then_inc(w_in, 16)
                sp.dma_start(g.w1[:, :, :], g.d_w1.rearrange("e d h -> d e h")).then_inc(g.experts_in, 16)
                sp.dma_start(g.w2[:, :, :, :], g.d_w2.rearrange("e (c p) d -> p e c d", p=P)).then_inc(g.experts_in, 16)
                sp.dma_start(g.b1[:, :, :], g.d_b1.rearrange("e (c p) -> p e c", p=P),
                             allow_slow_non_contiguous=True).then_inc(g.experts_in, 16)
                sp.wait_ge(low_ready, 2 * NCQ)
                sp.wait_ge(mid_ready, 2 * NCQ)
                for w, order in enumerate(((0, 1, 0, 1, 2, 0), (0, 0, 1, 1, 0, 2))):
                    for b in range(B):
                        for s, part in enumerate(order):
                            sp.dma_start(g.d_stack0[w, b, :, s * DH0:(s + 1) * DH0, :],
                                         parts[:, w, part, b * S:(b + 1) * S]).then_inc(saved, 16)
                sp.wait_ge(saved, 16 * 2 * B * 6)

            @block.vector
            def _(dve):
                dve.memset(g.ones[:, :], 1.0).then_inc(ones_ready, 1)
                dve.memset(g.onesb[:, :], 1.0).then_inc(ones_ready, 1)
                dve.memset(g.v0[:, :, :, :], 1.0).then_inc(ones_ready, 1)
                chain = Chain(dve, step)
                dve.wait_ge(x_in, 16)
                norm_rows(dve, chain, g.x, xn, stats, mv, rs, t1, var_ready, root_ready)
                dve.wait_ge(ones_ready, 3)
                for u in range(2 * NCQ):
                    w, c = u // NCQ, u % NCQ
                    cols = slice(c * CH, (c + 1) * CH)
                    dve.wait_ge(high_ready, 2 * (u + 1))
                    if u >= 2:
                        dve.wait_ge(low_ready, u - 1)
                    dve.tensor_tensor(rest[:, u % 2, :], full[:, u % 2, :], parts[:, w, 0, cols],
                                      ALU.subtract).then_inc(rest_ready, 1)
                    dve.wait_ge(mid_ready, u + 1)
                    dve.tensor_tensor(parts[:, w, 2, cols], rest[:, u % 2, :], parts[:, w, 1, cols],
                                      ALU.subtract).then_inc(low_ready, 1)
                for t in range(NT):
                    dve.wait_ge(v_ready, t + 1)
                    dst = g.v0[:, (t // TB) * H0:(t // TB + 1) * H0, t % TB, 0:DH0]
                    dve.tensor_copy(dst, ps_v[:, t % 2, 0:P].rearrange("p (h d) -> p h d", d=DH0)).then_inc(v_kept, 1)
                dve.wait_ge(r_ready, 1)
                dve.tensor_copy(g.logits[:, :, :], ps_r[:, :, :]).then_inc(v_kept, 1)

            @block.scalar
            def _(act):
                act.wait_ge(var_ready, 1)
                act.activation(rs[:, 1, :], rs[:, 0, :], ACT.Sqrt).then_inc(root_ready, 1)
                for c in range(NCQ):
                    act.wait_ge(turned, c + 1)
                    act.activation(g.xnT[:, c * CH:(c + 1) * CH], ps_t[:, c % 2, :], ACT.Copy).then_inc(xnT_ready, 1)
                act.wait_ge(w_in, 16 * 12)
                for u in range(2 * NCQ):
                    w, c = u // NCQ, u % NCQ
                    cols = slice(c * CH, (c + 1) * CH)
                    bias = (bq, bk)[w]
                    act.wait_ge(prod_ready, u + 1)
                    if u >= 2:
                        act.wait_ge(rest_ready, u - 1)
                    act.activation(full[:, u % 2, :], ps_p[:, u % 2, :], ACT.Identity,
                                   bias=bias[:, 0:1]).then_inc(high_ready, 1)
                    act.activation(parts[:, w, 0, cols], ps_p[:, u % 2, :], ACT.Identity,
                                   bias=bias[:, 0:1]).then_inc(high_ready, 1)
                    act.wait_ge(rest_ready, u + 1)
                    act.activation(parts[:, w, 1, cols], rest[:, u % 2, :], ACT.Copy).then_inc(mid_ready, 1)

            @block.tensor
            def _(pe):
                pe.wait_ge(w_in, 16 * 12)
                for t in range(NT):
                    pe.wait_ge(step, XN0 + t + 1)
                    if t % 4 == 0 and t >= 8:
                        pe.wait_ge(xnT_ready, t // 4 - 1)
                    last = pe.transpose(ps_t[:, (t // 4) % 2, (t % 4) * P:(t % 4 + 1) * P], xn[:, t, :], g.ident[:, :])
                    if t % 4 == 3:
                        last.then_inc(turned, 1)
                for u in range(2 * NCQ):
                    w, c = u // NCQ, u % NCQ
                    pe.wait_ge(xnT_ready, c + 1)
                    if u >= 2:
                        pe.wait_ge(high_ready, 2 * (u - 1))
                    pe.matmul(ps_p[:, u % 2, :], (wq, wk)[w][:, :], g.xnT[:, c * CH:(c + 1) * CH],
                              start=True, stop=True).then_inc(prod_ready, 1)
                pe.wait_ge(ones_ready, 3)
                for t in range(NT):
                    tok = g.xnT[:, t * P:(t + 1) * P]
                    if t >= 2:
                        pe.wait_ge(v_kept, t - 1)
                    pe.matmul(ps_v[:, t % 2, 0:P], tok, wv[:, :], start=True, stop=False)
                    pe.matmul(ps_v[:, t % 2, 0:P], g.ones[0:1, :], bv[0:1, :], start=False, stop=True).then_inc(v_ready, 1)
                for t in range(NT):
                    last = pe.matmul(ps_r[:, t, :], g.xnT[:, t * P:(t + 1) * P], wr[:, :], start=True, stop=True)
                last.then_inc(r_ready, 1)


def attend_layer0(nc, g):
    with ExitStack() as ctx:
        r = Room(nc, ctx, "a0")
        NQ = 4
        GR = 4
        GW = P // GR
        q = r.sb("q", [P, NQ, S], BF16)
        k = r.sb("k", [P, NQ, S], BF16)
        v = r.sb("v", [P, 2, TB, GW])
        nil = r.sb("nil", [P, CH], BF16)
        top = r.sb("top", [P, TB, 2])
        peak = r.sb("peak", [P, TB])
        left = r.sb("left", [P, TB])
        shift = r.sb("shift", [P, 2, TB, NSH], BF16)
        PW = sum(S - j * P for j in range(TB))
        PO = [sum(S - a * P for a in range(j)) for j in range(TB)]
        prob = r.sb("prob", [P, 2, PW])
        oT = r.sb("oT", [P, S])
        osum = r.sb("osum", [P, TB, VW0])
        rec = r.sb("rec", [P, TB])
        ps_row = r.ps("ps_row", [P, 2, CH])
        ps_col = r.ps("ps_col", [P, 2, S])
        ps_out = r.ps("ps_out", [P, S])

        qk_in = [r.sem(f"qk_in{i}") for i in range(NQ)]
        blank, v_ready = r.sem("blank"), r.sem("v_ready")
        row_ready, row_read = r.sem("row_ready"), r.sem("row_read")
        shift_ready, step = r.sem("shift_ready"), r.sem("step")
        col_ready, col_read = r.sem("col_ready"), r.sem("col_read")
        pv_done, out_read = r.sem("pv_done"), r.sem("out_read")
        rec_ready, kept = r.sem("rec_ready"), r.sem("kept")

        NH = B * H0
        SCALE = float(1.0 / (8.0 ** 0.5))
        UNITS = [(i, c) for i in range(TB) for c in range((i * P) // CH + 1)]
        NU = len(UNITS)
        CU = TB + 1
        STEPS = 4
        assert NU % 2 == 0 and CU % 2 == 1 and NH % NQ == 0

        def row_base(n):
            if is_at(n, 0):
                return NU
            if is_at(n, NH):
                return row_base(NH - 1) + 2
            return n * (NU + 2) + (NU - 2)

        def heads(eng, section):
            for n in range(NQ):
                section(n, 0, n)
            with eng.Fori(1, NH // NQ - 1) as i:
                for h in range(NQ):
                    section(i * NQ + h, i, h)
            for n in range(NH - NQ, NH + 1):
                section(n, n // NQ, n % NQ)

        with nc.Block() as block:
            @block.sync
            def _(sp):
                def load(n, h):
                    stacks = g.d_stack0.rearrange("w b h r n -> w (b h) r n")
                    sp.dma_start(q[0:ROWS0, h, :], stacks[0, bass.ds(n, 1)]).then_inc(qk_in[h], 16)
                    sp.dma_start(k[0:ROWS0, h, :], stacks[1, bass.ds(n, 1)]).then_inc(qk_in[h], 16)

                sp.wait_ge(blank, 2)
                for h in range(NQ):
                    load(h, h)
                with sp.Fori(1, NH // NQ) as i:
                    for h in range(NQ):
                        sp.wait_ge(col_ready, i * (NQ * CU) + (h - NQ + 1) * CU)
                        load(i * NQ + h, h)

            @block.gpsimd
            def _(pool):
                def values(n, p, first=False):
                    if not first:
                        pool.wait_ge(pv_done, n - 1)
                    src = g.v0.rearrange("p n j w -> p n (j w)")[:, bass.ds(n, 1), :]
                    pool.tensor_copy(v[:, p, :, 0:VW0], src.rearrange("p o (j w) -> p (o j) w", w=VW0)).then_inc(v_ready, 1)

                pool.wait_ge(blank, 3)
                values(0, 0, True)
                values(1, 1, True)
                with pool.Fori(1, NH // 2) as i:
                    values(i * 2, 0)
                    values(i * 2 + 1, 1)

            @block.tensor
            def _(pe):
                def row_unit(n, i4, h, unit, u):
                    i, c = UNITS[u]
                    width = min(CH, (i + 1) * P - c * CH)
                    diag = (i + 1) * P <= (c + 1) * CH
                    if u == 0:
                        pe.wait_ge(qk_in[h], i4 * 32 + 32)
                    wait(pe, row_read, unit - 1)
                    last = pe.matmul(ps_row[:, u % 2, 0:width], q[0:SHIFT0, h, i * P:(i + 1) * P],
                                     k[0:SHIFT0, h, c * CH:c * CH + width], start=True, stop=True)
                    if diag:
                        last = pe.matmul(ps_row[:, u % 2, width - P:width], g.identb[:, :], g.maskq[:, :],
                                         start=False, stop=True, skip_group_check=True)
                    last.then_inc(row_ready, 1)

                def pv(n, p, x):
                    bank = 0 if x == 1 else 1
                    if x == 0:
                        pe.wait_ge(v_ready, n + 1)
                        wait(pe, out_read, n)
                        pe.wait_ge(col_read, n * CU + (GR + 1))
                    if x == 2:
                        pe.wait_ge(col_read, n * CU + CU)
                    if x == 1:
                        for a in range(1, GR):
                            pe.matmul(ps_out[a * GW:(a + 1) * GW, 0:CH], nil[:, 0:GW], nil[:, :],
                                      start=True, stop=True)
                    for a in range(GR):
                        j = a if x < 2 else a + GR
                        lo, hi = max(j * P, bank * CH), (bank + 1) * CH
                        m = pe.matmul(ps_out[a * GW:(a + 1) * GW, lo:hi], v[:, p, j, :],
                                      prob[:, p, PO[j] + lo - j * P:PO[j] + hi - j * P],
                                      start=(x == 0 or (x == 1 and a == 0)), stop=True, skip_group_check=True)
                    if x == 2:
                        m.then_inc(pv_done, 1)

                def section(n, i4, h):
                    p = h % 2
                    rows = not (is_at(n, NH - 1) or is_at(n, NH))
                    ahead = iter(range(NU if rows else 0))

                    def rows_ahead(count):
                        for u in [u for _, u in zip(range(count), ahead)]:
                            nh = (h + 1) % NQ
                            row_unit(n + 1, i4 + (h + 1) // NQ, nh, row_base(n) + u, u)

                    if not is_at(n, NH):
                        wait(pe, col_read, n * CU - 1)
                        pe.wait_ge(shift_ready, n + 1)
                        for i in range(TB):
                            m = pe.matmul(ps_col[0:NSH, p % 2, i * P:(i + 1) * P], shift[:, p, i, :], g.identb[:, :],
                                          start=True, stop=True)
                        m.then_inc(col_ready, 1)
                    rows_ahead(2)
                    for j in range(TB):
                        if not is_at(n, NH):
                            wait(pe, col_read, n * CU + j)
                            if j == 0:
                                pe.wait_ge(col_read, n * CU + 1)
                            buf = (p + j + 1) % 2
                            n_q = S - j * P
                            for c in range(0, n_q, CH):
                                w = min(CH, n_q - c)
                                m = pe.matmul(ps_col[:, buf, c:c + w], k[:, h, j * P:(j + 1) * P],
                                              q[:, h, j * P + c:j * P + c + w], start=True, stop=True)
                                if c == 0:
                                    m = pe.matmul(ps_col[:, buf, 0:P], g.identb[:, :], g.maskk[:, :],
                                                  start=False, stop=True, skip_group_check=True)
                            m.then_inc(col_ready, 1)
                        rows_ahead(2 if j in (0, 2) else 1)
                        if j in (0, 2, 4) and not is_at(n, 0):
                            pv(n - 1, 1 - p, j // 2)
                    rows_ahead(NU)
                    if not is_at(n, 0):
                        pe.wait_ge(out_read, n)
                        base = row_base(n) + (NU if rows else 0)
                        for x in range(2):
                            pe.wait_ge(row_read, base + (x - 1))
                            for i in range(4):
                                m = pe.transpose(ps_row[:, x, i * P:(i + 1) * P],
                                                 oT[:, (4 * x + i) * P:(4 * x + i + 1) * P], g.ident[:, :])
                            m.then_inc(row_ready, 1)

                pe.wait_ge(blank, 4)
                for u in range(NU):
                    row_unit(0, 0, 0, u, u)
                heads(pe, section)

            @block.scalar
            def _(act):
                def section(n, i4, h):
                    p = h % 2
                    if not is_at(n, NH):
                        act.wait_ge(col_ready, n * CU + 1)
                        act.activation(q[SHIFT0:SHIFT0 + NSH, h, :], ps_col[0:NSH, p, :], ACT.Copy).then_inc(col_read, 1)
                    for j in range(TB):
                        if not is_at(n, NH):
                            act.wait_ge(col_ready, n * CU + (j + 2))
                            if j == 0:
                                wait(act, pv_done, n - 1)
                            act.activation(prob[:, p, PO[j]:PO[j] + S - j * P], ps_col[:, (p + j + 1) % 2, 0:S - j * P],
                                           ACT.Exp, scale=SCALE).then_inc(col_read, 1)
                        if j == 5 and not is_at(n, 0):
                            act.wait_ge(pv_done, n)
                            if not is_at(n, 1):
                                act.wait_ge(row_ready, row_base(n - 1) + (2 if is_at(n, NH) else NU + 2))
                            act.activation(oT[:, :], ps_out[:, :], ACT.Copy).then_inc(out_read, 1)

                heads(act, section)

            @block.vector
            def _(dve):
                def peaks(n, p, base):
                    chain = Chain(dve, step, n * STEPS)
                    for u, (i, c) in enumerate(UNITS):
                        width = min(CH, (i + 1) * P - c * CH)
                        dve.wait_ge(row_ready, base + (u + 1))
                        m = dve.tensor_reduce(top[:, i, c:c + 1], ps_row[:, u % 2, 0:width], AX.X, ALU.max)
                        m.then_inc(row_read, 1)
                    dve.wait_ge(row_read, base + NU)
                    chain(dve.tensor_tensor(peak[:, :], top[:, :, 0], top[:, :, 1], ALU.max))
                    wait(dve, col_ready, n * CU - (2 * CU - 1))
                    chain(dve.tensor_scalar(shift[:, p, :, 0], peak[:, :], -1.0, None, ALU.mult))
                    chain(dve.scalar_tensor_tensor(left[:, :], peak[:, :], -1.0, shift[:, p, :, 0], ALU.mult,
                                                   ALU.subtract))
                    chain(dve.tensor_copy(shift[:, p, :, 1], left[:, :]))
                    dve.tensor_tensor(shift[:, p, :, 2], left[:, :], shift[:, p, :, 1],
                                      ALU.subtract).then_inc(shift_ready, 1)

                def keep(n, base):
                    wait(dve, kept, n)
                    for x in range(2):
                        dve.wait_ge(row_ready, base + (x + 1))
                        grouped = ps_row[:, x, :].rearrange("p (i a w) -> p i w a", a=GR, w=GW)[:, :, 0:VW0, :]
                        dve.tensor_reduce(osum[:, 4 * x:4 * x + 4, :], grouped, AX.X, ALU.add).then_inc(row_read, 1)
                    dve.wait_ge(row_read, base + 2)
                    chain = Chain(dve, rec_ready, n)
                    chain(dve.reciprocal(rec[:, :], osum[:, :, DH0]))
                    b = n // H0
                    o = g.o0[:, bass.ds(b, 1), :, bass.ds((n % H0) * DH0, DH0)]
                    dve.tensor_tensor(o, osum[:, :, 0:DH0],
                                      rec[:, :].rearrange("p (i o) -> p i o", o=1).broadcast_to([P, TB, DH0]),
                                      ALU.mult).then_inc(kept, 1)

                def section(n, i4, h):
                    rows = not (is_at(n, NH - 1) or is_at(n, NH))
                    if rows:
                        peaks(n + 1, 1 - h % 2, row_base(n))
                    if not is_at(n, 0):
                        keep(n - 1, row_base(n) + (NU if rows else 0))

                set_up = Chain(dve, blank)
                dve.memset(q[:, :, :], 0.0)
                dve.memset(top[:, :, :], -3.0e38)
                set_up(dve.memset(k[:, :, :], 0.0))
                set_up(dve.memset(k[SHIFT0:SHIFT0 + NSH, :, :], 1.0))
                set_up(dve.memset(v[:, :, :, :], 0.0))
                set_up(dve.memset(nil[:, :], 0.0))
                peaks(0, 0, 0)
                heads(dve, section)


def run_experts(nc, g):
    with ExitStack() as ctx:
        r = Room(nc, ctx, "ex")
        w1, w2, b1, w_in = g.w1, g.w2, g.b1, g.experts_in
        hid = r.sb("hid", [P, 2, HC, CH])
        pr = r.sb("pr", [P, NT, NE])
        ta = r.sb("ta", [P, NT, NE])
        tb = r.sb("tb", [P, NT, NE])
        pick = r.sb("pick", [P, NT, NE])
        m1 = r.sb("m1", [P, NT])
        ps_h = r.ps("ps_h", [P, 4, CH])
        ps_y = r.ps("ps_y", [P, 2, 4, P])

        chained = r.sem("chained")
        exp_in, exp_out = r.sem("exp_in"), r.sem("exp_out")
        h_ready, h_read, y_ready, y_read = r.sem("h_ready"), r.sem("h_read"), r.sem("y_ready"), r.sem("y_read")
        NCK = NT * P // CH
        TC = CH // P

        with nc.Block() as block:
            @block.sync
            def _(sp):
                sp.dma_start(g.win[:, :], g.d_win).then_inc(g.trees_in, 16)
                sp.dma_start(g.bin32[:, :], g.d_bin).then_inc(g.trees_in, 16)
                sp.dma_start(g.wout[:, 0:NCH - 1, :], g.d_wout[0:(NCH - 1) * P, :].rearrange(
                    "(c p) d -> p c d", p=P)).then_inc(g.trees_in, 16)
                sp.dma_start(g.wout[0:LASTW, NCH - 1, :], g.d_wout[(NCH - 1) * P:WIDTH, :]).then_inc(g.trees_in, 16)

            @block.tensor
            def _(pe):
                pe.wait_ge(w_in, 48)

                def second(c, e, first):
                    s = c * NE + e
                    pe.wait_ge(h_read, s * HC + HC)
                    if not (first and e < 2):
                        pe.wait_ge(y_read, (s - 1) * TC)
                    for t in range(TC):
                        for hc in range(HC):
                            m = pe.matmul(ps_y[:, e % 2, t, :], hid[:, e % 2, hc, t * P:(t + 1) * P],
                                          w2[:, e, hc, :], start=(hc == 0), stop=(hc == HC - 1))
                    m.then_inc(y_ready, 1)

                def chunk(c, first):
                    for e in range(NE):
                        for hc in range(HC):
                            if not (first and e == 0):
                                pe.wait_ge(h_read, (c * NE + e) * HC + (hc - 3))
                            pe.matmul(ps_h[:, hc, :], w1[:, e, hc * P:(hc + 1) * P],
                                      g.xnT[:, bass.ds(c * CH, CH)], start=True, stop=True).then_inc(h_ready, 1)
                        if e >= 1:
                            second(c, e - 1, first)
                    second(c, NE - 1, first)

                chunk(0, True)
                with pe.Fori(1, NCK) as c:
                    chunk(c, False)

            @block.scalar
            def _(act):
                act.wait_ge(exp_in, 1)
                act.activation(pr[:, :, :], ta[:, :, :], ACT.Exp).then_inc(exp_out, 1)
                act.wait_ge(w_in, 48)

                def chunk(c, first):
                    for e in range(NE):
                        for hc in range(HC):
                            s = (c * NE + e) * HC + hc
                            act.wait_ge(h_ready, s + 1)
                            if hc == 0 and not (first and e < 2):
                                act.wait_ge(y_ready, c * NE + (e - 1))
                            act.activation(hid[:, e % 2, hc, :], ps_h[:, hc, :], ACT.Gelu,
                                           bias=b1[:, e, hc:hc + 1]).then_inc(h_read, 1)

                chunk(0, True)
                with act.Fori(1, NCK) as c:
                    chunk(c, False)

            @block.vector
            def _(dve):
                chain = Chain(dve, chained)

                def wide(ap):
                    return ap[:, :].rearrange("p (t o) -> p t o", o=1).broadcast_to([P, NT, NE])

                def first_of(dst, src):
                    chain(dve.tensor_reduce(m1[:, :], src[:, :, :], AX.X, ALU.max))
                    chain(dve.tensor_tensor(tb[:, :, :], src[:, :, :], wide(m1), ALU.is_ge))
                    chain(dve.tensor_tensor(tb[:, :, :], tb[:, :, :], g.desc[:, :].rearrange(
                        "p (t e) -> p t e", e=NE), ALU.mult))
                    chain(dve.tensor_reduce(m1[:, :], tb[:, :, :], AX.X, ALU.max))
                    chain(dve.tensor_tensor(dst[:, :, :], tb[:, :, :], wide(m1), ALU.is_ge))

                chain(dve.tensor_reduce(m1[:, :], g.logits[:, :, :], AX.X, ALU.max))
                dve.tensor_tensor(ta[:, :, :], g.logits[:, :, :], wide(m1), ALU.subtract).then_inc(exp_in, 1)
                dve.wait_ge(exp_out, 1)
                chain(dve.tensor_reduce(m1[:, :], pr[:, :, :], AX.X, ALU.add))
                chain(dve.reciprocal(m1[:, :], m1[:, :]))
                chain(dve.tensor_tensor(pr[:, :, :], pr[:, :, :], wide(m1), ALU.mult))
                first_of(pick, pr)
                chain(dve.scalar_tensor_tensor(ta[:, :, :], pick[:, :, :], -4.0, pr[:, :, :], ALU.mult, ALU.add))
                first_of(ta, ta)
                chain(dve.tensor_tensor(pick[:, :, :], pick[:, :, :], ta[:, :, :], ALU.add))
                chain(dve.tensor_tensor(g.comb[:, :, :], pick[:, :, :], pr[:, :, :], ALU.mult))

                comb = g.comb.rearrange("p t e -> p (t e)")
                acc = g.acc.rearrange("p t d -> p (t d)")

                def chunk(c):
                    for e in range(NE):
                        for t in range(TC):
                            dve.wait_ge(y_ready, c * NE + (e + 1))
                            if e >= 1:
                                dve.wait_ge(y_read, (c * NE + (e - 1)) * TC + (t + 1))
                            a = acc[:, bass.ds(c * CH + t * P, P)]
                            w = comb[:, bass.ds(c * (TC * NE) + (t * NE + e), 1)]
                            if e == 0:
                                m = dve.tensor_scalar(a, ps_y[:, e % 2, t, :], w, None, ALU.mult)
                            else:
                                m = dve.scalar_tensor_tensor(a, ps_y[:, e % 2, t, :], w, a, ALU.mult, ALU.add)
                            m.then_inc(y_read, 1)

                with dve.Fori(0, NCK) as c:
                    chunk(c)


def project_layer1(nc, g):
    with ExitStack() as ctx:
        r = Room(nc, ctx, "p1")
        wo = r.sb("wo", [P, D])
        bo = r.sb("bo", [1, D])
        b2 = r.sb("b2", [NE, D])
        wqk = r.sb("wqk", [P, NPAIR, P])
        wqk_rot = r.sb("wqk_rot", [P, NPAIR, P])
        wv = r.sb("wv", [P, KV1 * DH1])
        cos = r.sb("cos", [P, S])
        sin = r.sb("sin", [P, S])
        oT = r.sb("oT", [P, 2, P])
        cT = r.sb("cT", [NE, 2, P])
        xn = r.sb("xn", [P, NT, D])
        stats = r.sb("stats", [P, NT, 6])
        mv = r.sb("mv", [P, NT, 2])
        rs = r.sb("rs", [P, 4, NT])
        t1 = r.sb("t1", [P, NT])
        ra = r.sb("ra", [P, 2, CH])
        rb = r.sb("rb", [P, 2, CH])
        full = r.sb("full", [P, 2, CH])
        rest = r.sb("rest", [P, 2, CH])
        NBUF = 4
        parts = r.sb("parts", [P, NBUF, 3, CH], BF16)
        ps_a = r.ps("ps_a", [P, 2, CH])
        ps_b = r.ps("ps_b", [P, 2, CH])
        ps_q = r.ps("ps_q", [P, 2, CH])
        ps_qr = r.ps("ps_qr", [P, 2, CH])

        w_in, step = r.sem("w_in"), r.sem("step")
        turned, oT_ready, sum_ready, sum_read = r.sem("turned"), r.sem("oT_ready"), r.sem("sum_ready"), r.sem("sum_read")
        acc_ready, x1_ready = r.sem("acc_ready"), r.sem("x1_ready")
        var_ready, root_ready = r.sem("var_ready"), r.sem("root_ready")
        xturned, xnT_ready = r.sem("xturned"), r.sem("xnT_ready")
        v_ready, v_kept = r.sem("v_ready"), r.sem("v_kept")
        q_ready, rot_a, rot_b, full_ready = r.sem("q_ready"), r.sem("rot_a"), r.sem("rot_b"), r.sem("full_ready")
        high_ready, rest_ready, mid_ready, low_ready = (r.sem("high_ready"), r.sem("rest_ready"), r.sem("mid_ready"),
                                                        r.sem("low_ready"))
        saved = [r.sem(f"saved{i}") for i in range(NBUF)]
        NCQ = NT * P // CH
        XN0 = 2 + 5
        UB = 2 * NPAIR

        with nc.Block() as block:
            @block.sync
            def _(sp):
                for dst, src in ((wo[:, :], g.d_wo0), (bo[:, :], g.d_bo0), (b2[:, :], g.d_b2),
                                 (wv[:, :], g.d_wv1), (cos[:, :], g.d_cos), (sin[:, :], g.d_sin),
                                 (wqk[:, :, :], g.d_wqk1.rearrange("i (m o) -> i m o", o=P)),
                                 (wqk_rot[:, :, :], g.d_wqk1r.rearrange("i (m o) -> i m o", o=P))):
                    sp.dma_start(dst, src).then_inc(w_in, 16)
                sp.wait_ge(w_in, 16 * 8)
                with sp.Fori(0, B) as b:
                    for half in range(2):
                        for m in range(NPAIR):
                            u = half * NPAIR + m
                            sp.wait_ge(low_ready, b * UB + (u + 1))
                            sp.wait_ge(mid_ready, b * UB + (u + 1))
                            for part in range(3):
                                if m < H1 // 2:
                                    dst = g.d_q1[part, bass.ds(b, 1), m * P:(m + 1) * P, half * CH:(half + 1) * CH]
                                else:
                                    mk = m - H1 // 2
                                    dst = g.d_k1[part, bass.ds(b, 1), mk * P:(mk + 1) * P, half * CH:(half + 1) * CH]
                                sp.dma_start(dst, parts[:, u % NBUF, part, :]).then_inc(saved[u % NBUF], 16)
                for p in range(NBUF):
                    sp.wait_ge(saved[p], 16 * 3 * UB * B // NBUF)

            @block.tensor
            def _(pe):
                pe.wait_ge(w_in, 16 * 8)
                def turn(t):
                    if t >= 2:
                        pe.wait_ge(oT_ready, 2 * (t - 1))
                    pe.transpose(ps_a[:, t % 2, 0:P], g.o0[:, t // TB, t % TB, :], g.ident[:, :])
                    pe.transpose(ps_a[0:NE, t % 2, P:2 * P], g.comb[:, t, :], g.ident[:, :]).then_inc(turned, 1)

                turn(0)
                for t in range(NT):
                    if t + 1 < NT:
                        turn(t + 1)
                    pe.wait_ge(oT_ready, 2 * (t + 1))
                    if t >= 2:
                        pe.wait_ge(acc_ready, t - 1)
                    out = ps_b[:, t % 2, 0:P]
                    pe.matmul(out, oT[:, t % 2, :], wo[:, :], start=True, stop=False)
                    pe.matmul(out, g.ones[0:1, :], bo[0:1, :], start=False, stop=False)
                    pe.matmul(out, cT[:, t % 2, :], b2[:, :], start=False, stop=True).then_inc(sum_ready, 1)
                for t in range(NT):
                    pe.wait_ge(step, XN0 + t + 1)
                    if t % 4 == 0 and t >= 8:
                        pe.wait_ge(xnT_ready, t // 4 - 1)
                    m = pe.transpose(ps_a[:, (t // 4) % 2, (t % 4) * P:(t % 4 + 1) * P], xn[:, t, :], g.ident[:, :])
                    if t % 4 == 3:
                        m.then_inc(xturned, 1)
                for t in range(NT):
                    pe.wait_ge(xnT_ready, t // 4 + 1)
                    if t >= 2:
                        pe.wait_ge(v_kept, t - 1)
                    pe.matmul(ps_b[:, t % 2, 0:KV1 * DH1], g.xnT[:, t * P:(t + 1) * P], wv[:, :],
                              start=True, stop=True).then_inc(v_ready, 1)

                def batch(b, first):
                    for u in range(UB):
                        half, m = u // NPAIR, u % NPAIR
                        if not (first and u < 2):
                            pe.wait_ge(rot_a, b * UB + (u - 1))
                            pe.wait_ge(rot_b, b * UB + (u - 1))
                        xs = g.xnT[:, bass.ds(b * S + half * CH, CH)]
                        pe.matmul(ps_q[:, u % 2, :], wqk[:, m, :], xs, start=True, stop=True)
                        pe.matmul(ps_qr[:, u % 2, :], wqk_rot[:, m, :], xs, start=True, stop=True).then_inc(q_ready, 1)

                batch(0, True)
                with pe.Fori(1, B) as b:
                    batch(b, False)

            @block.vector
            def _(dve):
                dve.memset(g.v1[:, :, :, :], 1.0)
                chain = Chain(dve, step)
                for t in range(NT):
                    dve.tensor_tensor(g.x[:, t, :], g.x[:, t, :], g.acc[:, t, :], ALU.add).then_inc(x1_ready, 1)
                for t in range(NT):
                    dve.wait_ge(sum_ready, t + 1)
                    dve.wait_ge(x1_ready, t + 1)
                    dve.tensor_tensor(g.x[:, t, :], g.x[:, t, :], ps_b[:, t % 2, 0:P], ALU.add).then_inc(acc_ready, 1)
                dve.wait_ge(acc_ready, NT)
                norm_rows(dve, chain, g.x, xn, stats, mv, rs, t1, var_ready, root_ready)
                for t in range(NT):
                    b, j = t // TB, t % TB
                    dve.wait_ge(v_ready, t + 1)
                    dve.tensor_copy(g.v1[:, b * KV1:(b + 1) * KV1, j, 0:DH1],
                                    ps_b[:, t % 2, 0:KV1 * DH1].rearrange("p (h d) -> p h d", d=DH1)).then_inc(v_kept, 1)

                def rest_of(unit, u):
                    dve.wait_ge(high_ready, unit + 1)
                    dve.tensor_tensor(rest[:, u % 2, :], full[:, u % 2, :], parts[:, u % NBUF, 0, :],
                                      ALU.subtract).then_inc(rest_ready, 1)

                def low_of(unit, u):
                    dve.wait_ge(mid_ready, unit + 1)
                    dve.tensor_tensor(parts[:, u % NBUF, 2, :], rest[:, u % 2, :], parts[:, u % NBUF, 1, :],
                                      ALU.subtract).then_inc(low_ready, 1)

                def batch(b, first):
                    for u in range(UB):
                        half = u // NPAIR
                        base = b * UB + u
                        dve.wait_ge(q_ready, base + 1)
                        if not (first and u < 2):
                            dve.wait_ge(full_ready, base - 1)
                        dve.tensor_tensor(ra[:, u % 2, :], ps_q[:, u % 2, :], cos[:, half * CH:(half + 1) * CH],
                                          ALU.mult).then_inc(rot_a, 1)
                        dve.tensor_tensor(rb[:, u % 2, :], ps_qr[:, u % 2, :], sin[:, half * CH:(half + 1) * CH],
                                          ALU.mult).then_inc(rot_b, 1)
                        if not (first and u < 2):
                            low_of(base - 2, u + UB - 2)
                        if not (first and u < 1):
                            if not (first and u < 3):
                                dve.wait_ge(low_ready, base - 2)
                            rest_of(base - 1, u + UB - 1)

                batch(0, True)
                with dve.Fori(1, B) as b:
                    batch(b, False)
                low_of(B * UB - 2, UB - 2)
                rest_of(B * UB - 1, UB - 1)
                low_of(B * UB - 1, UB - 1)

            @block.gpsimd
            def _(pool):
                def batch(b, first):
                    for u in range(UB):
                        base = b * UB + u
                        pool.wait_ge(rot_a, base + 1)
                        pool.wait_ge(rot_b, base + 1)
                        if not (first and u < 2):
                            pool.wait_ge(rest_ready, base - 1)
                            pool.wait_ge(high_ready, base - 1)
                        pool.tensor_tensor(full[:, u % 2, :], ra[:, u % 2, :], rb[:, u % 2, :],
                                           ALU.add).then_inc(full_ready, 1)

                batch(0, True)
                with pool.Fori(1, B) as b:
                    batch(b, False)

            @block.scalar
            def _(act):
                for t in range(NT):
                    act.wait_ge(turned, t + 1)
                    if t >= 2:
                        act.wait_ge(sum_ready, t - 1)
                    act.activation(oT[:, t % 2, :], ps_a[:, t % 2, 0:P], ACT.Copy).then_inc(oT_ready, 1)
                    act.activation(cT[:, t % 2, :], ps_a[0:NE, t % 2, P:2 * P], ACT.Copy).then_inc(oT_ready, 1)
                act.wait_ge(var_ready, 1)
                act.activation(rs[:, 1, :], rs[:, 0, :], ACT.Sqrt).then_inc(root_ready, 1)
                for c in range(NCQ):
                    act.wait_ge(xturned, c + 1)
                    act.activation(g.xnT[:, c * CH:(c + 1) * CH], ps_a[:, c % 2, :], ACT.Copy).then_inc(xnT_ready, 1)

                def middle(unit, u):
                    act.wait_ge(rest_ready, unit + 1)
                    act.activation(parts[:, u % NBUF, 1, :], rest[:, u % 2, :], ACT.Copy).then_inc(mid_ready, 1)

                def batch(b, first):
                    for u in range(UB):
                        base = b * UB + u
                        act.wait_ge(full_ready, base + 1)
                        if not (first and u < NBUF):
                            act.wait_ge(saved[u % NBUF], b * (48 * UB // NBUF) + 48 * (u // NBUF))
                        act.activation(parts[:, u % NBUF, 0, :], full[:, u % 2, :], ACT.Copy).then_inc(high_ready, 1)
                        if not (first and u < 1):
                            middle(base - 1, u + UB - 1)

                batch(0, True)
                with act.Fori(1, B) as b:
                    batch(b, False)
                middle(B * UB - 1, UB - 1)


def attend_layer1(nc, g):
    with ExitStack() as ctx:
        r = Room(nc, ctx, "a1")
        NH = B * H1
        GRP = H1 // KV1
        ROUNDS = TOPK // 8
        COUNTS = 5
        NS = TB - 1
        NB = 16
        DOWN = 2.0 ** -24
        SCALE = DOWN / 8.0
        AIM = float(2 * TOPK - NB)
        POOL_CUTS = (3, 4, 5, 6)
        MARKS = {3: (0, 0), 4: (1, 0), 5: (0, 5 * P), 6: (1, 4 * P)}
        LEAD = float(np.log(2 * TOPK / AIM))
        LESS = 2 * TOPK - 0.25
        PW = sum((i + 1) * P for i in range(TB))
        OFF = [sum((a + 1) * P for a in range(i)) for i in range(TB)]
        TILE = [TB - 1 - j for j in range(TB)]
        CHUNKS = [(j, TILE[j], c, min(4, TILE[j] + 1 - c)) for j in range(TB) for c in range(0, TILE[j] + 1, 4)]
        TU = len(CHUNKS)
        EARLY = 2
        NTAL = COUNTS * NS
        OWN = 2
        NPOOL = NS - OWN
        assert TU % 2 == 0

        q = r.sb("q", [P, 2, 2, S], BF16)
        k = r.sb("k", [P, 2, 3, S], BF16)
        sc = r.sb("sc", [P, 2, PW])
        prob = r.sb("prob", [P, 2, PW])
        work = r.sb("work", [P, 2, S])
        work0 = r.sb("work0", [P, P])
        trash = r.sb("trash", [P, 2, S], BF16)
        kT = r.sb("kT", [P, 2, CH])
        iota = r.sb("iota", [P, NS, NB])
        wide = r.sb("wide", [P, NS])
        peak = r.sb("peak", [P, 2, TB])
        npeak = r.sb("npeak", [P, 2, TB])
        sample = r.sb("sample", [P, NS, 8])
        spread = r.sb("spread", [P, 2, NS])
        trial = r.sb("trial", [P, 2, COUNTS, NS])
        balance = r.sb("balance", [P, 2, COUNTS, NS])
        above2 = r.sb("above2", [P, 2, COUNTS, NS])
        diff = r.sb("diff", [P, NS])
        total = r.sb("total", [P, NS])
        move = r.sb("move", [P, NS])
        num = r.sb("num", [P, NS])
        den = r.sb("den", [P, NS])
        fac = r.sb("fac", [P, NS])
        stride = r.sb("stride", [P, NS])
        low2 = r.sb("low2", [P, COUNTS, NS])
        far = r.sb("far", [P, COUNTS, NS])
        found2 = r.sb("found2", [P, NS])
        found = r.sb("found", [P, NS])
        sorted_ = r.sb("sorted", [P, NS, NB])
        hit = r.sb("hit", [P, NS, NB])
        picked = r.sb("picked", [P, NS, NB])
        hits = r.sb("hits", [P, NS])
        bad = r.sb("bad", [P, 3, NS])
        verdict = r.sb("verdict", [P, NS + 1])
        flag = r.sb("flag", [1, NS + 1], mybir.dt.int32)
        best = r.sb("best", [P, ROUNDS, 8])
        again = r.sb("again", [P, ROUNDS, 8])
        thr = r.sb("thr", [P, NS])
        rec = r.sb("rec", [P, 2, 4])
        ps_s = r.ps("ps_s", [P, 2, S])
        ps_t = r.ps("ps_t", [P, 2, CH])
        ps_o = r.ps("ps_o", [P, 2, CH])
        outs = [ps_o[:, x, 0:4 * VW1].rearrange("p (i w) -> p i w", w=VW1) for x in range(2)]
        ps_flag = ps_o[0:1, 0, 4 * VW1:4 * VW1 + NS + 1]

        qk_in = [r.sem(f"qk_in{i}") for i in range(2)]
        table_in = r.sem("table_in")
        s_ready, s_kept, step = r.sem("s_ready"), r.sem("s_kept"), r.sem("step")
        start_ready, tallied, moved = r.sem("start_ready"), r.sem("tallied"), r.sem("moved")
        verdict_ready, flag_back, redo = r.sem("verdict_ready"), r.sem("flag_back"), r.sem("redo")
        p_ready, cut_ready = r.sem("p_ready"), r.sem("cut_ready")
        found_ready, marked, aside, sort_done = (r.sem("found_ready"), r.sem("marked"), r.sem("aside"),
                                                 r.sem("sort_done"))
        tick, thr_ready, cut_marked, cut_pool = r.sem("tick"), r.sem("thr_ready"), r.sem("cut_marked"), r.sem("cut_pool")
        t_ready, t_read, pv_done, o_kept = r.sem("t_ready"), r.sem("t_read"), r.sem("pv_done"), r.sem("o_kept")

        def parts_of(n):
            if not isinstance(n, int):
                return True, True, True, True
            return n + 1 < NH, 0 <= n < NH, 1 <= n <= NH, 2 <= n

        def sections(eng, section):
            for n in (-1, 0, 1):
                section(n, n // 2, n % 2)
            with eng.Fori(1, NH // 2 - 1) as i:
                section(i * 2, i, 0)
                section(i * 2 + 1, i, 1)
            for n in range(NH - 2, NH + 2):
                section(n, n // 2, n % 2)

        def wait_cut(eng, n, j):
            if j in POOL_CUTS:
                eng.wait_ge(cut_pool, n * len(POOL_CUTS) + POOL_CUTS.index(j) + 1)
            else:
                eng.wait_ge(cut_ready, n * (TB - len(POOL_CUTS)) + sum(a not in POOL_CUTS for a in range(j + 1)))

        def columns(buf, p, i):
            return buf[:, p, OFF[i]:OFF[i] + (i + 1) * P]

        with nc.Block() as block:
            @block.sync
            def _(sp):
                def load(n, p):
                    for st, (top, low) in enumerate(((0, 1), (0, 2))):
                        for half, part in enumerate((top, low)):
                            src = g.d_q1.rearrange("t b (h r) n -> t (b h) r n", r=DH1)[part, bass.ds(n, 1)]
                            sp.dma_start(q[half * DH1:(half + 1) * DH1, p, st, :], src).then_inc(qk_in[p], 16)
                    for st, (top, low) in enumerate(((0, 0), (1, 1), (2, 0))):
                        for half, part in enumerate((top, low)):
                            src = g.d_k1.rearrange("t b (h r) n -> t (b h) r n", r=DH1)[part, bass.ds(n // GRP, 1)]
                            sp.dma_start(k[half * DH1:(half + 1) * DH1, p, st, :], src).then_inc(qk_in[p], 16)

                load(0, 0)
                load(1, 1)
                sp.dma_start(iota.rearrange("p s j -> p (s j)"), g.d_rank).then_inc(table_in, 16)
                sp.dma_start(wide[:, :], g.d_wide).then_inc(table_in, 16)
                with sp.Fori(0, NH // 2 - 1) as i:
                    for p in range(2):
                        sp.wait_ge(s_ready, (i * 2 + p + 1) * TB)
                        load(i * 2 + 2 + p, p)

            @block.tensor
            def _(pe):
                v = g.v1.rearrange("p n j w -> p (n j w)")

                def scores(n, i2, p, j):
                    i = TILE[j]
                    if j == 0:
                        pe.wait_ge(qk_in[p], i2 * 160 + 160)
                    wait(pe, s_kept, n * TB + (j - 1))
                    width = (i + 1) * P
                    qa, qc = q[:, p, 0, i * P:width], q[:, p, 1, i * P:width]
                    for c in range(0, width, CH):
                        w = min(CH, width - c)
                        out = ps_s[:, j % 2, c:c + w]
                        pe.matmul(out, qa, k[:, p, 0, c:c + w], start=True, stop=False)
                        pe.matmul(out, qa, k[:, p, 1, c:c + w], start=False, stop=False)
                        m = pe.matmul(out, qc, k[:, p, 2, c:c + w], start=False, stop=True)
                    m = pe.matmul(ps_s[:, j % 2, width - P:width], g.identb[:, :], g.maskq[:, :],
                                  start=False, stop=True, skip_group_check=True)
                    m.then_inc(s_ready, 1)

                def turn(n, p, x):
                    j, i, c, cnt = CHUNKS[x]
                    wait_cut(pe, n, j)
                    wait(pe, t_read, n * TU + (x - 1))
                    for a in range(cnt):
                        m = pe.transpose(ps_t[:, x % 2, a * P:(a + 1) * P],
                                         columns(prob, p, i)[:, (c + a) * P:(c + a + 1) * P], g.ident[:, :])
                    m.then_inc(t_ready, 1)

                def weigh(n, x):
                    j, i, c, cnt = CHUNKS[x]
                    if x == 0:
                        wait(pe, o_kept, n * 2)
                    pe.wait_ge(t_read, n * TU + (x + 1))
                    for a in range(cnt):
                        m = pe.matmul(outs[i // 4][:, i % 4, :], kT[:, x % 2, a * P:(a + 1) * P],
                                      v[:, bass.ds((n // GRP) * (TB * VW1) + (c + a) * VW1, VW1)],
                                      start=(c + a == 0), stop=(c + a == i))
                    m.then_inc(pv_done, 1)

                def section(n, i2, p):
                    ahead, _, ends, last = parts_of(n)
                    if ahead:
                        scores(n + 1, i2 + p, 1 - p, 0)
                        scores(n + 1, i2 + p, 1 - p, 1)
                    if last:
                        turn(n - 2, p, EARLY)
                        for x in range(EARLY + 1, TU):
                            turn(n - 2, p, x)
                            weigh(n - 2, x - 1)
                        weigh(n - 2, TU - 1)
                    if ends:
                        pe.wait_ge(verdict_ready, n)
                        pe.matmul(ps_flag, g.ones[:, 0:1], verdict[:, :], start=True, stop=True).then_inc(flag_back, 1)
                    if ends:
                        for x in range(EARLY):
                            turn(n - 1, 1 - p, x)
                    for x in range(TB - 2):
                        if ahead:
                            scores(n + 1, i2 + p, 1 - p, 2 + x)
                        if ends and 1 <= x <= EARLY:
                            weigh(n - 1, x - 1)

                sections(pe, section)

            @block.gpsimd
            def _(pool):
                def mark(n, p, j):
                    i = TILE[j]
                    if j == OWN:
                        wait(pool, pv_done, (n - 1) * TU)
                        pool.wait_ge(found_ready, n + 1)
                        pool.sem_inc(tick, 1)
                        pool.wait_ge(tick, 1)
                    pool.tensor_scalar(columns(prob, p, i), columns(sc, p, i), found[:, i - 1:i], None,
                                       ALU.is_gt).then_inc(marked, 1)

                def put_aside(n, p, j):
                    i = TILE[j]
                    pool.wait_ge(marked, n * NPOOL + (j - OWN + 1))
                    pool.tensor_tensor(columns(prob, p, i), columns(sc, p, i), columns(prob, p, i),
                                       ALU.subtract).then_inc(aside, 1)

                def marks(j):
                    lane, c = MARKS[j]
                    return work[:, lane, c:c + (TILE[j] + 1) * P]

                def mark_kept(p, j):
                    i = TILE[j]
                    pool.tensor_scalar(marks(j), columns(sc, p, i), thr[:, i - 1:i], None,
                                       ALU.is_ge).then_inc(cut_marked, 1)

                def cut(n, p, j):
                    i = TILE[j]
                    pool.wait_ge(cut_marked, n * len(POOL_CUTS) + (POOL_CUTS.index(j) + 1))
                    pool.tensor_tensor(columns(prob, p, i), columns(prob, p, i), marks(j),
                                       ALU.mult).then_inc(cut_pool, 1)

                def section(n, i2, p):
                    if parts_of(n)[2]:
                        pool.sem_clear(tick)
                        mark(n - 1, 1 - p, OWN)
                        for j in range(OWN + 1, NS):
                            mark(n - 1, 1 - p, j)
                            put_aside(n - 1, 1 - p, j - 1)
                        put_aside(n - 1, 1 - p, NS - 1)
                        pool.wait_ge(thr_ready, n)
                        pool.wait_ge(p_ready, (n - 1) * TB + (POOL_CUTS[-1] + 1))
                        pool.sem_inc(tick, 1)
                        pool.wait_ge(tick, 2)
                        mark_kept(1 - p, POOL_CUTS[0])
                        for a in range(1, len(POOL_CUTS)):
                            mark_kept(1 - p, POOL_CUTS[a])
                            cut(n - 1, 1 - p, POOL_CUTS[a - 1])
                        cut(n - 1, 1 - p, POOL_CUTS[-1])

                sections(pool, section)

            @block.scalar
            def _(act):
                def counts(n, p, c, s):
                    i = TILE[s]
                    if s == 0 and c == 0:
                        act.wait_ge(start_ready, n * 2 + 2)
                    elif s == 0:
                        act.wait_ge(moved, n * (COUNTS - 1) + c)
                    u = c * NS + s
                    wait(act, tallied, n * NTAL + (u - 1))
                    act.activation(trash[:, (p * NTAL + u) % 2, 0:(i + 1) * P], columns(sc, p, i), ACT.Sign,
                                   scale=-1.0, bias=trial[:, p, c, i - 1:i],
                                   accum_out=balance[:, p, c, i - 1:i]).then_inc(tallied, 1)

                def weights(n, p, j):
                    if j == 0:
                        wait(act, pv_done, (n - 1) * TU)
                    i = TILE[j]
                    if OWN <= j < NS:
                        act.wait_ge(sort_done, n * NPOOL + (j - OWN + 1))
                    act.activation(columns(prob, p, i), columns(sc, p, i), ACT.Exp, scale=1.0 / DOWN,
                                   bias=npeak[:, p, i:i + 1]).then_inc(p_ready, 1)

                def turned(n, x):
                    act.wait_ge(t_ready, n * TU + (x + 1))
                    wait(act, pv_done, n * TU + (x - 1))
                    cnt = CHUNKS[x][3]
                    act.activation(kT[:, x % 2, 0:cnt * P], ps_t[:, x % 2, 0:cnt * P], ACT.Copy).then_inc(t_read, 1)

                def section(n, i2, p):
                    _, counting, ends, last = parts_of(n)
                    SOON = ((3, 3), (3, 6))
                    LATE = ((1, 1), (1, 3), (1, 5), (2, 0), (2, 2), (2, 4), (2, 6))
                    LATE_AFTER = (2, 1, 0, 0, 0)
                    EXPS_AFTER = (1, 1, 6, 0, 0)
                    late = iter(range(EARLY, TU))
                    soon = iter(range(EARLY))
                    exps = iter(range(TB))
                    for c in range(COUNTS):
                        for s in range(NS):
                            if counting:
                                counts(n, p, c, s)
                            if last and (c, s) in LATE:
                                turned(n - 2, next(late))
                            if ends and (c, s) in SOON:
                                turned(n - 1, next(soon))
                        for _ in range(LATE_AFTER[c]):
                            if last:
                                turned(n - 2, next(late))
                        for _ in range(EXPS_AFTER[c]):
                            if ends:
                                weights(n - 1, 1 - p, next(exps))

                sections(act, section)

            @block.vector
            def _(dve):
                def section(n, i2, p):
                    ahead, counting, ends, last = parts_of(n)
                    p1 = 1 - p
                    made = [0]

                    def did(ins):
                        ins.then_inc(step, 1)
                        made[0] += 1
                        return made[0]

                    def after(number):
                        dve.wait_ge(step, number)

                    dve.sem_clear(step)

                    zero = {"k": 0, "last": 0}

                    def first_tile():
                        kk = zero["k"]
                        if not ends or kk >= 2 * ROUNDS - 1:
                            return
                        src = columns(sc, p1, 0) if kk < 2 else work0[:, :]
                        if kk:
                            after(zero["last"])
                        if kk % 2 == 0:
                            zero["last"] = did(dve.max(best[:, kk // 2, :], src))
                        else:
                            zero["last"] = did(dve.match_replace(work0[:, :], best[:, kk // 2, :], src, -3.0e38))
                        zero["k"] += 1

                    def chained(ins):
                        number = did(ins)
                        first_tile()
                        after(number)

                    def move_trial(c):
                        dve.wait_ge(tallied, n * NTAL + (c + 1) * NS)
                        t, a2 = trial[:, p, c, :], above2[:, p, c, :]
                        chained(dve.tensor_tensor(a2, wide[:, :], balance[:, p, c, :], ALU.subtract))
                        if c == 0:
                            did(dve.tensor_scalar(den[:, :], a2, AIM, None, ALU.add))
                            chained(dve.tensor_scalar(num[:, :], a2, AIM, 2.0, ALU.subtract, ALU.mult))
                        else:
                            t1, a1 = trial[:, p, c - 1, :], above2[:, p, c - 1, :]
                            did(dve.scalar_tensor_tensor(diff[:, :], a1, 0.25, a2, ALU.add, ALU.subtract))
                            did(dve.tensor_tensor(total[:, :], a1, a2, ALU.add))
                            chained(dve.tensor_tensor(move[:, :], t, t1, ALU.subtract))
                            did(dve.scalar_tensor_tensor(den[:, :], a2, AIM, diff[:, :], ALU.add, ALU.mult))
                            chained(dve.scalar_tensor_tensor(num[:, :], a2, AIM, total[:, :], ALU.subtract, ALU.mult))
                        chained(dve.reciprocal(fac[:, :], den[:, :]))
                        chained(dve.tensor_tensor(fac[:, :], fac[:, :], num[:, :], ALU.mult))
                        if c == 0:
                            chained(dve.tensor_tensor(stride[:, :], fac[:, :], spread[:, p, :], ALU.mult))
                        else:
                            chained(dve.tensor_tensor(stride[:, :], fac[:, :], move[:, :], ALU.mult))
                            chained(dve.scalar_tensor_tensor(stride[:, :], spread[:, p, :], -1.0, stride[:, :],
                                                             ALU.mult, ALU.max))
                            chained(dve.tensor_tensor(stride[:, :], stride[:, :], spread[:, p, :], ALU.min))
                        dve.tensor_tensor(trial[:, p, c + 1, :], t, stride[:, :], ALU.add).then_inc(moved, 1)

                    def keep_trial():
                        dve.wait_ge(tallied, n * NTAL)
                        c = COUNTS - 1
                        after(did(dve.tensor_tensor(above2[:, p1, c, :], wide[:, :], balance[:, p1, c, :], ALU.subtract)))
                        a2 = above2[:, p1, :, :]
                        did(dve.tensor_scalar(far[:, :, :], a2, LESS, 3.0e38, ALU.is_ge, ALU.mult))
                        after(did(dve.scalar_tensor_tensor(low2[:, :, :], a2, LESS, a2, ALU.is_lt, ALU.mult)))
                        did(dve.tensor_reduce(found2[:, :], low2.rearrange("p c s -> p s c"), AX.X, ALU.max))
                        after(did(dve.tensor_tensor(far[:, :, :], far[:, :, :], trial[:, p1, :, :], ALU.add)))
                        dve.tensor_reduce(found[:, :], far.rearrange("p c s -> p s c"), AX.X,
                                          ALU.min).then_inc(found_ready, 1)
                        dve.wait_ge(found_ready, n)

                    LANES = [(j, j + 1) if j + 1 < NS else (j,) for j in range(0, NS, 2)]
                    lane_done = [0, 0]

                    def sort_stage(lane, stage):
                        for a, j in enumerate(LANES[lane]):
                            i = TILE[j]
                            w, s = (i + 1) * P, i - 1
                            buf = work[:, a, 0:w] if j < OWN else columns(prob, p1, i)
                            if j >= OWN and stage == 1:
                                if a == 0:
                                    dve.wait_ge(aside, (n - 1) * NPOOL + (LANES[lane][-1] - OWN + 1))
                                    dve.sem_inc(step, 1)
                                    made[0] += 1
                                    after(made[0])
                            elif stage:
                                after(lane_done[a])
                            if stage == 0:
                                if j >= OWN:
                                    continue
                                m = dve.scalar_tensor_tensor(buf, columns(sc, p1, i), found[:, s:s + 1],
                                                             columns(sc, p1, i), ALU.is_gt, ALU.subtract, reverse1=True)
                            elif stage == 1:
                                m = dve.max(sorted_[:, s, 0:8], buf)
                            elif stage == 2:
                                m = dve.match_replace(buf, sorted_[:, s, 0:8], buf, -3.0e38)
                            else:
                                m = dve.max(sorted_[:, s, 8:16], buf)
                                if j >= OWN:
                                    m.then_inc(sort_done, 1)
                                    continue
                            lane_done[a] = did(m)
                        if len(LANES[lane]) == 1:
                            first_tile()

                    def pick():
                        after(made[0])
                        dve.wait_ge(sort_done, n * NPOOL)
                        rank = found2[:, :].rearrange("p (s o) -> p s o", o=1).broadcast_to([P, NS, NB])
                        chained(dve.tensor_tensor(hit[:, :, :], iota[:, :, :], rank, ALU.is_equal))
                        did(dve.tensor_reduce(hits[:, :], hit[:, :, :], AX.X, ALU.add))
                        did(dve.tensor_tensor(bad[:, 0, :], sorted_[:, :, 0], found[:, :], ALU.is_ge))
                        chained(dve.tensor_tensor(picked[:, :, :], hit[:, :, :], sorted_[:, :, :], ALU.mult))
                        did(dve.scalar_tensor_tensor(bad[:, 1, :], peak[:, p1, 1:TB], 0.5, bad[:, 0, :],
                                                     ALU.is_ge, ALU.add))
                        chained(dve.tensor_reduce(thr[:, :], picked[:, :, :], AX.X, ALU.add))
                        chained(dve.scalar_tensor_tensor(bad[:, 2, :], thr[:, :], -0.5, bad[:, 1, :],
                                                         ALU.is_lt, ALU.add))
                        chained(dve.tensor_tensor(verdict[:, 0:NS], bad[:, 2, :], hits[:, :], ALU.subtract))
                        dve.tensor_reduce(verdict[:, NS:NS + 1], verdict[:, 0:NS], AX.X, ALU.add).then_inc(verdict_ready, 1)

                    def leave():
                        dve.wait_ge(pv_done, (n - 1) * TU)
                        b = (n - 2) // H1
                        dve.reciprocal(rec[:, 0, :], outs[0][:, :, DH1]).then_inc(step, 1)
                        dve.reciprocal(rec[:, 1, :], outs[1][:, :, DH1]).then_inc(step, 1)
                        made[0] += 2
                        after(made[0])
                        for x in range(2):
                            o = g.o1[:, bass.ds(b, 1), 4 * x:4 * x + 4, bass.ds(((n - 2) % H1) * DH1, DH1)]
                            dve.tensor_tensor(o, outs[x][:, :, 0:DH1],
                                              rec[:, x, :].rearrange("p (i o) -> p i o", o=1).broadcast_to([P, 4, DH1]),
                                              ALU.mult).then_inc(o_kept, 1)

                    def do_again(s):
                        w = (s + 2) * P
                        dve.sem_clear(redo)
                        chain = Chain(dve, redo)
                        src = columns(sc, p1, s + 1)
                        chain(dve.max(again[:, 0, :], src))
                        for rd in range(1, ROUNDS):
                            chain(dve.match_replace(work[:, 0, 0:w], again[:, rd - 1, :], src, -3.0e38))
                            src = work[:, 0, 0:w]
                            chain(dve.max(again[:, rd, :], src))
                        chain(dve.tensor_copy(thr[:, s:s + 1], again[:, ROUNDS - 1, 7:8]))

                    def judge():
                        dve.wait_ge(flag_back, n)
                        number = did(dve.tensor_scalar(flag[:, 0:NS], ps_flag[:, 0:NS], float(P), None, ALU.add))
                        number = did(dve.tensor_scalar(flag[:, NS:NS + 1], ps_flag[:, NS:NS + 1], float(NS * P), None, ALU.add))
                        if last:
                            leave()
                        after(number)
                        any_bad = dve.value_load(flag[0:1, NS:NS + 1], min_val=0, max_val=8 * NS * P)
                        with dve.If(any_bad > 0):
                            for s in range(NS):
                                is_bad = dve.value_load(flag[0:1, s:s + 1], min_val=0, max_val=8 * P)
                                with dve.If(is_bad > 0):
                                    do_again(s)

                    def cut(j):
                        i = TILE[j]
                        limit = thr[:, i - 1:i] if i else best[:, ROUNDS - 1, 7:8]
                        dve.wait_ge(p_ready, (n - 1) * TB + (j + 1))
                        dve.scalar_tensor_tensor(columns(prob, p1, i), columns(sc, p1, i), limit, columns(prob, p1, i),
                                                 ALU.is_ge, ALU.mult).then_inc(cut_ready, 1)

                    def keep_scores(j):
                        i = TILE[j]
                        if ends:
                            wait_cut(dve, n - 1, j)
                        wait(dve, s_kept, (n + 1) * TB + j)
                        dve.wait_ge(s_ready, (n + 1) * TB + (j + 1))
                        dve.tensor_scalar(columns(sc, p1, i), ps_s[:, j % 2, 0:(i + 1) * P], SCALE, None,
                                          ALU.mult, ALU.max, accum_out=peak[:, p1, i:i + 1]).then_inc(s_kept, 1)

                    def sample_scores(j):
                        i = TILE[j]
                        if i:
                            did(dve.max(sample[:, i - 1, :], columns(sc, p1, i)[:, 0:(i + 1) * P:8]))

                    def seed():
                        dve.wait_ge(s_kept, (n + 2) * TB)
                        dve.tensor_scalar(npeak[:, p1, :], peak[:, p1, :], -1.0 / DOWN, None, ALU.mult).then_inc(start_ready, 1)
                        after(made[0])
                        after(did(dve.tensor_reduce(spread[:, p1, :], sample[:, :, 0:7], AX.X, ALU.add)))
                        after(did(dve.scalar_tensor_tensor(spread[:, p1, :], spread[:, p1, :], 1.0 / 7.0, sample[:, :, 7],
                                                           ALU.mult, ALU.subtract)))
                        after(did(dve.tensor_scalar(spread[:, p1, :], spread[:, p1, :], 1.0e-6 * DOWN, None, ALU.max)))
                        dve.scalar_tensor_tensor(trial[:, p1, 0, :], spread[:, p1, :], LEAD, sample[:, :, 7],
                                                 ALU.mult, ALU.add).then_inc(start_ready, 1)

                    def move_if(c):
                        if counting:
                            move_trial(c)

                    if is_at(n, -1):
                        dve.wait_ge(table_in, 32)
                    if ends:
                        keep_trial()
                        wait(dve, cut_pool, (n - 1) * len(POOL_CUTS))
                    for lane in range(len(LANES)):
                        for stage in range(4):
                            if ends:
                                sort_stage(lane, stage)
                            if (lane, stage) in MOVE_AT:
                                move_if(MOVE_AT[(lane, stage)])
                    if ends:
                        pick()
                    move_if(2)
                    if ends:
                        judge()
                        while zero["k"] < 2 * ROUNDS - 1:
                            first_tile()
                        after(made[0])
                        dve.sem_inc(thr_ready, 1)
                    elif last:
                        leave()
                    for j in range(TB + 2):
                        if ends and j < TB and j not in POOL_CUTS:
                            cut(j)
                        if ahead and 1 <= j <= TB:
                            keep_scores(j - 1)
                        if ahead and j >= 2:
                            sample_scores(j - 2)
                        if j == LAST_MOVE:
                            move_if(3)
                    if ahead:
                        seed()
                    if made[0]:
                        after(made[0])

                MOVE_AT = {(0, 1): 0, (1, 2): 1}
                LAST_MOVE = 2
                sections(dve, section)
                dve.wait_ge(o_kept, 2 * NH)


def walk_trees(nc, g):
    with ExitStack() as ctx:
        r = Room(nc, ctx, "ff")
        win, wout, bin32 = g.win, g.wout, g.bin32
        rest = r.sb("rest", [1, WIDTH])
        binp = r.sb("binp", [1, 3, WIDTH], BF16)
        bins = r.sb("bins", [3, WIDTH], BF16)
        xt = r.sb("xt", [P, 2, P])
        dec = r.sb("dec", [P, PAR, NODES], BF16)
        path = r.sb("path", [P, PAR, NODES], BF16)
        act_v = r.sb("act_v", [P, 2, WIDTH])
        mT = r.sb("mT", [P, 2, CH])
        ps_l = r.ps("ps_l", [P, 4 * CH])
        ps_t = r.ps("ps_t", [P, 2, CH])
        ps_f = r.ps("ps_f", [P, CH])

        w_in, bias_ready, step = r.sem("w_in"), r.sem("bias_ready"), r.sem("step")
        x_ready, l_ready, dec_ready, silu_ready = r.sem("x_ready"), r.sem("l_ready"), r.sem("dec_ready"), r.sem("silu_ready")
        masked, t_ready, t_read, f_ready, f_read = (r.sem("masked"), r.sem("t_ready"), r.sem("t_read"), r.sem("f_ready"),
                                                    r.sem("f_read"))
        NCK = (NCH + 3) // 4
        STEPS = 2 * DEPTH - 1
        HALVES = [(0, 2 * CH), (2 * CH, WIDTH)]
        BOUNDS = [(c * CH, min(CH, WIDTH - c * CH)) for c in range(4)]

        with nc.Block() as block:
            @block.sync
            def _(sp):
                sp.wait_ge(bias_ready, 4)
                for part in range(3):
                    sp.dma_start(bins[part:part + 1, :], binp[0:1, part, :]).then_inc(w_in, 16)
                sp.wait_ge(w_in, 48)

            @block.gpsimd
            def _(pool):
                def tile(t, p, first):
                    if not first:
                        pool.wait_ge(l_ready, t * 2 - 2)
                    pool.tensor_copy(xt[:, p, :], g.xnT[:, bass.ds(t * P, P)]).then_inc(x_ready, 1)

                tile(0, 0, True)
                tile(1, 1, True)
                with pool.Fori(1, NT // 2) as i:
                    tile(i * 2, 0, False)
                    tile(i * 2 + 1, 1, False)

            @block.tensor
            def _(pe):
                pe.wait_ge(g.trees_in, 64)
                pe.wait_ge(w_in, 48)

                def logits(t, p, first):
                    pe.wait_ge(x_ready, t + 1)
                    for x in range(2):
                        if not (first and p == 0):
                            pe.wait_ge(silu_ready, t * 2 + (x - 1))
                        for c, w in BOUNDS[2 * x:2 * x + 2]:
                            pe.matmul(ps_l[:, c:c + w], g.onesb[0:3, :], bins[:, c:c + w], start=True, stop=False)
                            m = pe.matmul(ps_l[:, c:c + w], xt[:, p, :], win[:, c:c + w], start=False, stop=True)
                        m.then_inc(l_ready, 1)

                def outputs(t, p, first):
                    pe.wait_ge(masked, t + 1)
                    if not (first and p == 0):
                        pe.wait_ge(f_read, t)

                    def turn(x):
                        if not (first and p == 0 and x < 2):
                            pe.wait_ge(t_read, t * NCK + (x - 1))
                        for c in range(4 * x, min(4 * x + 4, NCH)):
                            w = P if c < NCH - 1 else LASTW
                            m = pe.transpose(ps_t[0:w, x % 2, (c % 4) * P:(c % 4 + 1) * P],
                                             act_v[:, p, c * P:c * P + w], g.ident[:, :])
                        m.then_inc(t_ready, 1)

                    turn(0)
                    for x in range(NCK):
                        if x + 1 < NCK:
                            turn(x + 1)
                        pe.wait_ge(t_read, t * NCK + (x + 1))
                        for c in range(4 * x, min(4 * x + 4, NCH)):
                            w = P if c < NCH - 1 else LASTW
                            m = pe.matmul(ps_f[:, 0:P], mT[0:w, x % 2, (c % 4) * P:(c % 4 + 1) * P],
                                          wout[0:w, c, :], start=(c == 0), stop=(c == NCH - 1))
                        if x == NCK - 1:
                            m.then_inc(f_ready, 1)

                logits(0, 0, True)
                logits(1, 1, True)
                outputs(0, 0, True)
                with pe.Fori(1, NT // 2) as i:
                    logits(i * 2, 0, False)
                    outputs(i * 2 - 1, 1, False)
                    logits(i * 2 + 1, 1, False)
                    outputs(i * 2, 0, False)
                outputs(NT - 1, 1, False)

            @block.scalar
            def _(act):
                def silu(t, p, first):
                    if not first:
                        act.wait_ge(t_ready, (t - 1) * NCK)
                    for x, (lo, hi) in enumerate(HALVES):
                        act.wait_ge(dec_ready, t * 2 + (x + 1))
                        act.activation(act_v[:, p, lo:hi], ps_l[:, lo:hi], ACT.Silu).then_inc(silu_ready, 1)

                def turned(t, p, first):
                    for x in range(NCK):
                        act.wait_ge(t_ready, t * NCK + (x + 1))
                        full = 4 * P if x < NCK - 1 else (NCH - 1 - 4 * x) * P
                        if x < NCK - 1:
                            act.activation(mT[:, x % 2, 0:full], ps_t[:, x % 2, 0:full], ACT.Copy).then_inc(t_read, 1)
                        else:
                            act.activation(mT[:, x % 2, 0:full], ps_t[:, x % 2, 0:full], ACT.Copy)
                            act.activation(mT[0:LASTW, x % 2, full:full + P], ps_t[0:LASTW, x % 2, full:full + P],
                                           ACT.Copy).then_inc(t_read, 1)

                silu(0, 0, True)
                silu(1, 1, True)
                turned(0, 0, True)
                with act.Fori(1, NT // 2) as i:
                    silu(i * 2, 0, False)
                    turned(i * 2 - 1, 1, False)
                    silu(i * 2 + 1, 1, False)
                    turned(i * 2, 0, False)
                turned(NT - 1, 1, False)

            @block.vector
            def _(dve):
                dve.wait_ge(g.trees_in, 64)
                b = Chain(dve, bias_ready)
                b(dve.tensor_copy(binp[0:1, 0, :], bin32[0:1, :]))
                b(dve.tensor_tensor(rest[0:1, :], bin32[0:1, :], binp[0:1, 0, :], ALU.subtract))
                b(dve.tensor_copy(binp[0:1, 1, :], rest[0:1, :]))
                b(dve.tensor_tensor(binp[0:1, 2, :], rest[0:1, :], binp[0:1, 1, :], ALU.subtract))
                b(dve.memset(path[:, :, 0:1], 1.0))

                def walk(t, p):
                    for x, (lo, hi) in enumerate(HALVES):
                        dve.wait_ge(l_ready, t * 2 + (x + 1))
                        dve.tensor_scalar(dec.rearrange("p a n -> p (a n)")[:, lo:hi], ps_l[:, lo:hi], 0.0, None,
                                          ALU.is_gt).then_inc(dec_ready, 1)
                    dve.wait_ge(dec_ready, t * 2 + 2)
                    chain = Chain(dve, step, t * STEPS)
                    for d in range(DEPTH):
                        lo, nx = 2 ** d - 1, 2 ** (d + 1) - 1
                        here = path[:, :, lo:lo + 2 ** d]
                        kids = path[:, :, nx:nx + 2 ** (d + 1)].rearrange("p a (n k) -> p a n k", k=2)
                        chain(dve.tensor_tensor(kids[:, :, :, 1], here, dec[:, :, lo:lo + 2 ** d], ALU.mult))
                        m = dve.tensor_tensor(kids[:, :, :, 0], here, kids[:, :, :, 1], ALU.subtract)
                        if d < DEPTH - 1:
                            chain(m)
                    m.then_inc(leaf_ready, 1)
                    dve.wait_ge(leaf_ready, t + 1)
                    dve.wait_ge(silu_ready, t * 2 + 2)
                    a = act_v[:, p, :]
                    dve.tensor_tensor(a, a, path.rearrange("p a n -> p (a n)"), ALU.mult).then_inc(masked, 1)

                def add(t):
                    dve.wait_ge(f_ready, t + 1)
                    xs = g.x.rearrange("p t d -> p (t d)")[:, bass.ds(t * P, P)]
                    dve.tensor_tensor(xs, xs, ps_f[:, 0:P], ALU.add).then_inc(f_read, 1)

                leaf_ready = r.sem("leaf_ready")
                walk(0, 0)
                walk(1, 1)
                add(0)
                with dve.Fori(1, NT // 2) as i:
                    walk(i * 2, 0)
                    add(i * 2 - 1)
                    walk(i * 2 + 1, 1)
                    add(i * 2)
                add(NT - 1)


def finish(nc, g):
    with ExitStack() as ctx:
        r = Room(nc, ctx, "fin")
        wo = r.sb("wo", [P, H1 // 2, D])
        oT = r.sb("oT", [P, 4, CH])
        ps_t = r.ps("ps_t", [P, 4, CH])
        ps_f = r.ps("ps_f", [P, 2, CH])
        w_in, turned, oT_ready = r.sem("w_in"), r.sem("turned"), r.sem("oT_ready")
        f_ready, f_read, out_done = r.sem("f_ready"), r.sem("f_read"), r.sem("out_done")

        with nc.Block() as block:
            @block.sync
            def _(sp):
                sp.dma_start(wo[:, :, :], g.d_wo1.rearrange("(c p) d -> p c d", p=P)).then_inc(w_in, 16)
                for t in range(NT):
                    sp.wait_ge(f_read, t + 1)
                    b, j = t // TB, t % TB
                    sp.dma_start(g.d_out[b, j * P:(j + 1) * P, :], g.x[:, t, :]).then_inc(out_done, 16)
                sp.wait_ge(out_done, 16 * NT)

            @block.tensor
            def _(pe):
                pe.wait_ge(w_in, 16)

                def turn(t):
                    b, i = t // TB, t % TB
                    for x in range(2):
                        u = 2 * t + x
                        if u >= 4:
                            pe.wait_ge(oT_ready, u - 3)
                        for c in range(4):
                            f = (4 * x + c) * P
                            m = pe.transpose(ps_t[:, u % 4, c * P:(c + 1) * P], g.o1[:, b, i, f:f + P], g.ident[:, :])
                        m.then_inc(turned, 1)

                turn(0)
                for t in range(NT):
                    if t + 1 < NT:
                        turn(t + 1)
                    pe.wait_ge(oT_ready, 2 * t + 2)
                    if t >= 2:
                        pe.wait_ge(f_read, t - 1)
                    for c in range(8):
                        u = 2 * t + c // 4
                        m = pe.matmul(ps_f[:, t % 2, 0:P], oT[:, u % 4, (c % 4) * P:(c % 4 + 1) * P], wo[:, c, :],
                                      start=(c == 0), stop=(c == 7))
                    m.then_inc(f_ready, 1)

            @block.scalar
            def _(act):
                for u in range(2 * NT):
                    act.wait_ge(turned, u + 1)
                    if u >= 4:
                        act.wait_ge(f_ready, (u - 4) // 2 + 1)
                    act.activation(oT[:, u % 4, :], ps_t[:, u % 4, :], ACT.Copy).then_inc(oT_ready, 1)

            @block.vector
            def _(dve):
                for t in range(NT):
                    dve.wait_ge(f_ready, t + 1)
                    dve.tensor_tensor(g.x[:, t, :], g.x[:, t, :], ps_f[:, t % 2, 0:P], ALU.add).then_inc(f_read, 1)


class Shared:
    pass


def build_program(nc, g):
    with ExitStack() as ctx:
        r = Room(nc, ctx, "g")
        g.d_stack0 = nc.dram_tensor("stack0", (2, B, H0, ROWS0, S), BF16, kind="Internal").ap()
        g.d_q1 = nc.dram_tensor("q1parts", (3, B, H1 * DH1, S), BF16, kind="Internal").ap()
        g.d_k1 = nc.dram_tensor("k1parts", (3, B, KV1 * DH1, S), BF16, kind="Internal").ap()
        g.ident = r.sb("ident", [P, P])
        g.identb = r.sb("identb", [P, P], BF16)
        g.maskq = r.sb("maskq", [P, P], BF16)
        g.maskk = r.sb("maskk", [P, P], BF16)
        g.ones = r.sb("ones", [P, P])
        g.onesb = r.sb("onesb", [P, P], BF16)
        g.x = r.sb("x", [P, NT, D])
        g.v1 = r.sb("v1", [P, B * KV1, TB, VW1])
        with ExitStack() as layer:
            r0 = Room(nc, layer, "l0")
            g.xnT = r0.sb("xnT", [P, NT * P])
            g.desc = r0.sb("desc", [P, NT * NE])
            g.logits = r0.sb("logits", [P, NT, NE])
            g.comb = r0.sb("comb", [P, NT, NE])
            g.v0 = r0.sb("v0", [P, B * H0, TB, VW0])
            g.o0 = r0.sb("o0", [P, B, TB, H0 * DH0])
            g.acc = r0.sb("acc", [P, NT, D])
            g.w1 = r0.sb("w1", [P, NE, HID])
            g.w2 = r0.sb("w2", [P, NE, HC, D])
            g.b1 = r0.sb("b1", [P, NE, HC])
            g.win = r0.sb("win", [P, WIDTH])
            g.wout = r0.sb("wout", [P, NCH, D])
            g.bin32 = r0.sb("bin32", [1, WIDTH])
            g.experts_in, g.trees_in = r0.sem("experts_in"), r0.sem("trees_in")
            project_layer0(nc, g)
            attend_layer0(nc, g)
            run_experts(nc, g)
            project_layer1(nc, g)
            walk_trees(nc, g)
        with ExitStack() as layer:
            r1 = Room(nc, layer, "l1")
            g.o1 = r1.sb("o1", [P, B, TB, H1 * DH1])
            attend_layer1(nc, g)
            finish(nc, g)


_OUTS = [((B, S, D), "float32")]


def kernel(L0_attn_x, L0_attn_Wq, L0_attn_bq, L0_attn_Wk, L0_attn_bk, L0_attn_Wv, L0_attn_bv, L0_attn_Wo,
           L0_attn_bo, L0_ffn_Wr, L0_ffn_W1, L0_ffn_b1, L0_ffn_W2, L0_ffn_b2, L1_attn_Wq, L1_attn_Wk, L1_attn_Wv,
           L1_attn_Wo, L1_ffn_W_in, L1_ffn_b_in, L1_ffn_W_out):
    import ml_dtypes
    import numpy as np
    import concourse.bacc as bacc
    from concourse.bass_utils import run_bass_kernel_spmd

    def lay(a):
        return np.ascontiguousarray(a)

    future = np.triu(np.ones((P, P), bool), 1)
    maskq = np.where(future, np.float32(NEG), np.float32(0)).astype(ml_dtypes.bfloat16)
    inv_freq = (1.0 / np.float32(10000.0) ** (np.arange(0, DH1, 2, dtype=np.float32) / np.float32(DH1)))
    angles = np.outer(np.arange(S, dtype=np.float32), inv_freq.astype(np.float32))
    emb = np.concatenate([angles, angles], axis=-1)
    cos, sin = np.cos(emb).T, np.sin(emb).T
    sign = np.where(np.arange(DH1) < DH1 // 2, -1.0, 1.0).astype(np.float32)[:, None]
    desc = np.tile(np.arange(NE, 0, -1, dtype=np.float32), (P, NT))

    rank = np.tile((2 * (TOPK - 1) - 2 * np.arange(16)).astype(np.float32), (P, TB - 1))
    wide = np.tile(((np.arange(1, TB) + 1) * P).astype(np.float32), (P, 1))

    wqk = np.concatenate([np.asarray(L1_attn_Wq), np.asarray(L1_attn_Wk)], axis=0)
    half = DH1 // 2
    turned = wqk.reshape(H1 + KV1, 2, half, D)[:, ::-1].reshape(wqk.shape)
    feeds = {
        "d_x": lay(L0_attn_x), "d_wq0": lay(np.asarray(L0_attn_Wq).T), "d_wk0": lay(np.asarray(L0_attn_Wk).T),
        "d_wv0": lay(np.asarray(L0_attn_Wv).T), "d_wo0": lay(np.asarray(L0_attn_Wo).T),
        "d_bq0": lay(np.asarray(L0_attn_bq).reshape(P, 1)), "d_bk0": lay(np.asarray(L0_attn_bk).reshape(P, 1)),
        "d_bv0": lay(np.asarray(L0_attn_bv).reshape(1, P)), "d_bo0": lay(np.asarray(L0_attn_bo).reshape(1, P)),
        "d_wr": lay(np.asarray(L0_ffn_Wr).T), "d_w1": lay(L0_ffn_W1), "d_b1": lay(L0_ffn_b1),
        "d_w2": lay(L0_ffn_W2), "d_b2": lay(L0_ffn_b2),
        "d_wqk1": lay(wqk.T), "d_wqk1r": lay(turned.T), "d_wv1": lay(np.asarray(L1_attn_Wv).T),
        "d_wo1": lay(np.asarray(L1_attn_Wo).T), "d_win": lay(np.asarray(L1_ffn_W_in).T),
        "d_bin": lay(np.asarray(L1_ffn_b_in).reshape(1, WIDTH)), "d_wout": lay(np.asarray(L1_ffn_W_out).T),
        "d_ident": np.eye(P, dtype=np.float32), "d_identb": np.eye(P, dtype=np.float32).astype(ml_dtypes.bfloat16),
        "d_maskq": lay(maskq), "d_maskk": lay(maskq.T), "d_desc": desc, "d_rank": rank, "d_wide": wide,
        "d_cos": lay(np.concatenate([cos, cos]).astype(np.float32)),
        "d_sin": lay(np.concatenate([sin * sign, sin * sign]).astype(np.float32)),
    }
    nc = bacc.Bacc("TRN2", target_bir_lowering=False, num_devices=1)
    g = Shared()
    arrays = {}
    for name, a in feeds.items():
        arrays[name] = a
        g.__dict__[name] = nc.dram_tensor(name, a.shape, mybir.dt.from_np(a.dtype), kind="ExternalInput").ap()
    shape, dtype = _OUTS[0]
    g.d_out = nc.dram_tensor("out", shape, mybir.dt.from_np(np.dtype(dtype)), kind="ExternalOutput").ap()
    build_program(nc, g)
    r = run_bass_kernel_spmd(nc, [arrays], core_ids=[0])
    return r.results[0]["out"]
```
